# Optimizing a Trainium2 kernel written in Bass

```python
import numpy as np
import jax
import jax.numpy as jnp

def _softmax(x, axis=-1):
    return jax.nn.softmax(x, axis=axis)

def _gelu(x):
    return jax.nn.gelu(x, approximate=True)

def _silu(x):
    return jax.nn.silu(x)

def _sigmoid(x):
    return jax.nn.sigmoid(x)

def _layernorm(x, axis=-1, eps=1e-05):
    m = jnp.mean(x, axis=axis, keepdims=True)
    v = jnp.var(x, axis=axis, keepdims=True)
    return (x - m) / jnp.sqrt(v + eps)

def _scatter_add(tgt, idx, src, axis=0):
    return tgt.at[idx].add(src)

def _segment_sum(src, seg, n):
    return jax.ops.segment_sum(src, seg, n)
kernel_name = 'mk_adaln_d1_jaxref_r4_671407'

def setup_inputs(seed: int=0):
    np.random.seed(seed)
    _w = jnp.asarray

    def _L0_attn_setup():
        import jax, jax.numpy as jnp
        import numpy as np
        EPS = 1.1920929e-07

        def _rms(x):
            return x * jax.lax.rsqrt(jnp.mean(x * x, axis=-1, keepdims=True) + EPS)
        key = jax.random.key(seed)
        k0, k1, k2, k3 = jax.random.split(key, 4)
        B, S, D, DFF = (4, 512, 512, 2048)
        x = jax.random.normal(k0, (B, S, D), dtype=jnp.float32)
        w_qkv = jax.random.normal(k1, (3 * D, D), dtype=jnp.float32) * 0.02
        w_swiglu = jax.random.normal(k2, (2 * DFF, D), dtype=jnp.float32) * 0.02
        w_out = jax.random.normal(k3, (D, DFF), dtype=jnp.float32) * 0.02
        return {'x': x, 'w_qkv': w_qkv, 'w_swiglu': w_swiglu, 'w_out': w_out}
    _L0_attn_in = _L0_attn_setup()

    def _L0_ffn_setup():
        import jax, jax.numpy as jnp
        import numpy as np
        _FP4_LUT = jnp.array([0.0, 0.5, 1.0, 1.5, 2.0, 3.0, 4.0, 6.0, -0.0, -0.5, -1.0, -1.5, -2.0, -3.0, -4.0, -6.0], dtype=jnp.float32)
        GROUP_SIZE = 128
        EPS = 1e-06

        def _dequant_fp4(packed_i32, scales_f16, group_size):
            out_f, in_p = packed_i32.shape
            w = packed_i32.astype(jnp.uint32)
            shifts = jnp.arange(8, dtype=jnp.uint32) * 4
            nib = w[:, :, None] >> shifts & jnp.uint32(15)
            vals = _FP4_LUT[nib.astype(jnp.int32)].reshape(out_f, in_p * 8)
            s = scales_f16.astype(jnp.float32).T
            s_full = jnp.repeat(s, group_size, axis=1)
            return vals * s_full
        key = jax.random.key(seed)
        k1, k2, k3, k4, k5 = jax.random.split(key, 5)
        B, S, H, I = (4, 512, 512, 1408)
        x = jax.random.normal(k1, (B, S, H), dtype=jnp.float32)
        gate_up_packed = jax.random.randint(k2, (2 * I, H // 8), 0, 2147483647, dtype=jnp.int32)
        gate_up_scales = jax.random.uniform(k3, (H // GROUP_SIZE, 2 * I), dtype=jnp.float32).astype(jnp.float16)
        down_packed = jax.random.randint(k4, (H, I // 8), 0, 2147483647, dtype=jnp.int32)
        down_scales = jax.random.uniform(k5, (I // GROUP_SIZE, H), dtype=jnp.float32).astype(jnp.float16)
        return {'x': x, 'gate_up_packed': gate_up_packed, 'gate_up_scales': gate_up_scales, 'down_packed': down_packed, 'down_scales': down_scales}
    _L0_ffn_in = _L0_ffn_setup()
    _L0_c = _w((lambda *s: np.random.randn(*s).astype(np.float32) * 0.05)(1, 512))
    _L0_wmod = _w((lambda *s: np.random.randn(*s).astype(np.float32) * 0.05)(512, 6 * 512) * 512 ** (-0.5))
    _d = {'L0_attn_x': _L0_attn_in['x'], 'L0_attn_w_qkv': _L0_attn_in['w_qkv'], 'L0_attn_w_swiglu': _L0_attn_in['w_swiglu'], 'L0_attn_w_out': _L0_attn_in['w_out'], 'L0_ffn_gate_up_packed': _L0_ffn_in['gate_up_packed'], 'L0_ffn_gate_up_scales': _L0_ffn_in['gate_up_scales'], 'L0_ffn_down_packed': _L0_ffn_in['down_packed'], 'L0_ffn_down_scales': _L0_ffn_in['down_scales'], 'L0_c': _L0_c, 'L0_wmod': _L0_wmod}
    _x0 = _d['L0_attn_x']
    _d['L0_attn_x'] = jax.random.normal(jax.random.fold_in(jax.random.key(seed), 1), (1, 4096, 512), dtype=_x0.dtype)
    del _x0
    return _d

def reference(L0_attn_x, L0_attn_w_qkv, L0_attn_w_swiglu, L0_attn_w_out, L0_ffn_gate_up_packed, L0_ffn_gate_up_scales, L0_ffn_down_packed, L0_ffn_down_scales, L0_c, L0_wmod):

    def _L0_attn_ref(x, w_qkv, w_swiglu, w_out):
        import jax, jax.numpy as jnp
        import numpy as np
        EPS = 1.1920929e-07

        def _rms(x):
            return x * jax.lax.rsqrt(jnp.mean(x * x, axis=-1, keepdims=True) + EPS)
        qkv = _rms(x) @ w_qkv.T
        q, k, v = jnp.split(qkv, 3, axis=-1)
        q = _rms(q)
        k = _rms(k)
        w = jnp.exp(k)
        kv_cum = jnp.cumsum(w * v, axis=1)
        w_cum = jnp.cumsum(w, axis=1)
        y = jax.nn.sigmoid(q) * (kv_cum / (w_cum + 1e-06))
        uv = y @ w_swiglu.T
        u, g = jnp.split(uv, 2, axis=-1)
        return x + u * jax.nn.silu(g) @ w_out.T

    def _L0_ffn_ref(x, gate_up_packed, gate_up_scales, down_packed, down_scales):
        import jax, jax.numpy as jnp
        import numpy as np
        _FP4_LUT = jnp.array([0.0, 0.5, 1.0, 1.5, 2.0, 3.0, 4.0, 6.0, -0.0, -0.5, -1.0, -1.5, -2.0, -3.0, -4.0, -6.0], dtype=jnp.float32)
        GROUP_SIZE = 128
        EPS = 1e-06

        def _dequant_fp4(packed_i32, scales_f16, group_size):
            out_f, in_p = packed_i32.shape
            w = packed_i32.astype(jnp.uint32)
            shifts = jnp.arange(8, dtype=jnp.uint32) * 4
            nib = w[:, :, None] >> shifts & jnp.uint32(15)
            vals = _FP4_LUT[nib.astype(jnp.int32)].reshape(out_f, in_p * 8)
            s = scales_f16.astype(jnp.float32).T
            s_full = jnp.repeat(s, group_size, axis=1)
            return vals * s_full
        I = gate_up_packed.shape[0] // 2
        w_gu = _dequant_fp4(gate_up_packed, gate_up_scales, GROUP_SIZE)
        w_down = _dequant_fp4(down_packed, down_scales, GROUP_SIZE)
        gate_up = jnp.einsum('bsh,oh->bso', x, w_gu)
        gate, up = (gate_up[..., :I], gate_up[..., I:])
        h = jax.nn.silu(gate) * up
        y = jnp.einsum('bsi,hi->bsh', h, w_down)
        rms = jnp.sqrt(jnp.mean(y * y, axis=-1, keepdims=True) + EPS)
        return y / rms
    x = L0_attn_x
    mod = (_silu(L0_c) @ L0_wmod).reshape(L0_c.shape[0], 6, 1, -1)
    sa, ca, ga, sb, cb, gb = (mod[:, 0], mod[:, 1], mod[:, 2], mod[:, 3], mod[:, 4], mod[:, 5])
    ga = (2 * (ga >= 0) - 1) * jnp.maximum(jnp.abs(ga), 0.25)
    gb = (2 * (gb >= 0) - 1) * jnp.maximum(jnp.abs(gb), 0.25)
    h = _layernorm(x, axis=-1) * (1 + ca) + sa
    x = x + ga * _L0_attn_ref(h, L0_attn_w_qkv, L0_attn_w_swiglu, L0_attn_w_out)
    h = _layernorm(x, axis=-1) * (1 + cb) + sb
    x = x + gb * _L0_ffn_ref(h, L0_ffn_gate_up_packed, L0_ffn_gate_up_scales, L0_ffn_down_packed, L0_ffn_down_scales)
    return x

_drawn_inputs = setup_inputs


def setup_inputs(seed=0):
    import zlib

    import numpy as np

    out = dict(_drawn_inputs(seed))
    spreads = {}
    factors = {'L0_attn_w_qkv': 8.0, 'L0_attn_w_swiglu': 8.0, 'L0_attn_w_out': 8.0}
    for name, (base, spread) in spreads.items():
        noise = np.random.default_rng([zlib.crc32(name.encode()), seed]).standard_normal(out[name].shape)
        drawn = base * np.exp(spread * noise) if base else spread * noise
        out[name] = jnp.asarray(drawn.astype(out[name].dtype))
    for name, factor in factors.items():
        out[name] = (out[name] * factor).astype(out[name].dtype)
    return out
```

```python
from contextlib import ExitStack

import concourse.bass as bass
from concourse import mybir

ALU = mybir.AluOpType
ACT = mybir.ActivationFunctionType
F32 = mybir.dt.float32
F16 = mybir.dt.float16
BF16 = mybir.dt.bfloat16
I32 = mybir.dt.int32

P = 128


def program(nc, xT, wqkvT, wswT, woutT, packed, gu_scales, down_scales, c_col, wmod, outT):
    D, S = xT.shape
    T = 512
    NB = S // T
    DT = D // P
    FT = woutT.shape[0] // P
    I_T = gu_scales.shape[1] // 2
    GU = DT * 2 * I_T * P
    QKV = 3 * DT
    LN_EPS, RMS_EPS, CUM_EPS, FFN_EPS = 1e-5, 1.1920929e-07, 1e-6, 1e-6

    xT_t = xT.rearrange("(c p) s -> p c s", p=P)
    outT_t = outT.rearrange("(c p) s -> p c s", p=P)
    h_dram = nc.dram_tensor("h_scratch", [D, S], F32, kind="Internal").ap()
    x1_dram = nc.dram_tensor("x1_scratch", [D, S], F32, kind="Internal").ap()
    h_t = h_dram.rearrange("(c p) s -> p c s", p=P)
    x1_t = x1_dram.rearrange("(c p) s -> p c s", p=P)

    whole = ExitStack()
    with whole:
        def sem(name):
            return whole.enter_context(nc.semaphore(name))

        def keep(name, shape, dt):
            return whole.enter_context(nc.sbuf_tensor(name, shape, dt))

        mod = keep("mod", [P, 24], F32)
        ones = keep("ones", [P, P], F32)
        eps = keep("eps", [P, 3], F32)
        bank = [whole.enter_context(nc.psum_tensor(f"bank{i}", [P, T], F32)) for i in range(8)]
        SA, CA, GA, SB, CB, GB = (slice(DT * i, DT * i + DT) for i in range(6))

        mixer(nc, locals())
        ffn(nc, locals())


def counts(eng, *values):
    return [n if isinstance(n, int) else eng.snap(n) for n in values]


def mixer(nc, v):
    P_, T, NB, DT, FT, QKV, S = P, v["T"], v["NB"], v["DT"], v["FT"], v["QKV"], v["S"]
    mod, ones, eps, bank = v["mod"], v["ones"], v["eps"], v["bank"]
    SA, CA, GA = v["SA"], v["CA"], v["GA"]
    GB = v["GB"]
    xT_t, h_t, x1_t = v["xT_t"], v["h_t"], v["x1_t"]
    with ExitStack() as ctx:
        def sb(name, shape, dt):
            return ctx.enter_context(nc.sbuf_tensor(name, shape, dt))

        def sem(name):
            return v["sem"]("a_" + name)

        wqkv = sb("wqkv", [P, 2, DT, QKV * P], F16)
        wsw = sb("wsw", [P, 2, DT, 2 * FT * P], F16)
        wout = sb("wout", [P, 2, FT, DT * P], F16)
        X = sb("X", [P, DT, T], F32)
        H = sb("H", [P, 2, DT, T], F16)
        K = sb("K", [P, DT, T], F32)
        V = sb("V", [P, DT, T], F32)
        Q = sb("Q", [P, DT, T], F32)
        Y = sb("Y", [P, 2, DT, T], F16)
        SQ = sb("SQ", [P, 2, T], F32)
        RS = sb("RS", [P, T], F32)
        RD = sb("RD", [P, 2, T], F32)
        G = sb("G", [P, T], F32)
        UG = sb("UG", [P, 2, 2, T], F16)
        XR = sb("XR", [P, T], F32)
        HR = sb("HR", [P, T], F32)
        run = sb("run", [P, T], BF16)
        carry = sb("carry", [P, 2, DT], F32)
        cc = sb("cc", [P, 2, DT], F32)
        gtmp = sb("gtmp", [P, 3, 2 * DT], F32)
        U_BANK, G_BANK, R_BANK, O_BANK = bank[0], bank[1], bank[2:4], bank[4:8]
        MEAN, VAR, HSQ, KSQ, QSQ = range(5)
        SLOT = [0, 1, 0, 1, 0]
        WAVE = {VAR: 0, HSQ: 1, KSQ: 2, QSQ: 3}

        stage = [V, Q]
        const_ready = sem("const_ready")
        c_loaded = sem("c_loaded")
        wmod_loaded = sem("wmod_loaded")
        c_silu = sem("c_silu")
        mod_summed = sem("mod_summed")
        mod_copied = sem("mod_copied")
        mod_step = sem("mod_step")
        mod_ready = sem("mod_ready")
        scale_loaded = sem("scale_loaded")
        w_loaded = [sem("w_loaded0"), sem("w_loaded1")]
        w_high = sem("w_high")
        w_low = sem("w_low")
        x_loaded = sem("x_loaded")
        tile_sum = sem("tile_sum")
        squared = sem("squared")
        sq_sum = sem("sq_sum")
        reduced = sem("reduced")
        centred = sem("centred")
        root = sem("root")
        recip = sem("recip")
        scaled = sem("scaled")
        h_ready = sem("h_ready")
        h_stored = sem("h_stored")
        hn_ready = sem("hn_ready")
        H_high = sem("H_high")
        H_low = sem("H_low")
        qkv_done = sem("qkv_done")
        qkv_out = sem("qkv_out")
        k_norm = sem("k_norm")
        q_norm = sem("q_norm")
        k_exp = sem("k_exp")
        wv_ready = sem("wv_ready")
        k_run = sem("k_run")
        v_run = sem("v_run")
        k_carry = sem("k_carry")
        v_carry = sem("v_carry")
        k_eps = sem("k_eps")
        k_inv = sem("k_inv")
        q_sig = sem("q_sig")
        kv_mean = sem("kv_mean")
        y_ready = sem("y_ready")
        Y_high = sem("Y_high")
        Y_low = sem("Y_low")
        u_done = sem("u_done")
        g_done = sem("g_done")
        g_silu = sem("g_silu")
        ug_ready = sem("ug_ready")
        UG_high = sem("UG_high")
        UG_low = sem("UG_low")
        out_used = sem("out_used")
        res_loaded = sem("res_loaded")
        res_sum = sem("res_sum")
        x1_ready = sem("x1_ready")
        x1_stored = sem("x1_stored")

        def tok(b):
            return bass.ds(b * T, T)

        wq_src = v["wqkvT"].rearrange("(c p) n -> p c n", p=P)
        ws_src = v["wswT"].rearrange("(c p) n -> p c n", p=P)
        wo_src = v["woutT"].rearrange("(c p) n -> p c n", p=P)
        pieces = [(wqkv[:, :, :, n * T:(n + 1) * T], wq_src[:, :, n * T:(n + 1) * T]) for n in range(QKV * P // T)]
        pieces += [(wsw[:, :, :, n * T:(n + 1) * T], ws_src[:, :, n * T:(n + 1) * T]) for n in range(2 * FT * P // T)]
        pieces += [(wout[:, :, n * DT:(n + 1) * DT, :], wo_src[:, n * DT:(n + 1) * DT, :]) for n in range(FT // DT)]
        wmod_t = v["wmod"].rearrange("(k p) n -> p k n", p=P)
        wmod_sb = wsw[:, 1, :, :].rearrange("p c n -> p (c n)").bitcast(F32)
        HALF = 3 * DT * P
        assert DT * HALF <= DT * FT * P

        block = ctx.enter_context(nc.Block())

        @block.sync
        def _(sp):
            def load_x(b):
                if not (isinstance(b, int) and b == 0):
                    sp.wait_ge(H_low, DT * b)
                sp.dma_start(X[:], xT_t[:, :, tok(b)]).then_inc(x_loaded, 16)

            def store_h(b):
                sp.wait_ge(h_ready, DT * (b + 1))
                sp.dma_start(h_t[:, :, tok(b)], X[:]).then_inc(h_stored, 16)

            def residual(b):
                stored, = counts(sp, 16 * (b + 1))
                sp.wait_ge(h_stored, stored)
                for c in range(DT):
                    free, ready = counts(sp, 16 * (DT * b + c), DT * b + c + 1)
                    sp.wait_ge(x1_stored, free)
                    sp.dma_start(XR[:], xT_t[:, c, tok(b)]).then_inc(res_loaded, 16)
                    sp.dma_start(HR[:], h_t[:, c, tok(b)]).then_inc(res_loaded, 16)
                    sp.wait_ge(x1_ready, ready)
                    sp.dma_start(x1_t[:, c, tok(b)], XR[:]).then_inc(x1_stored, 16)

            sp.dma_start(cc[:, 0, :], v["c_col"]).then_inc(c_loaded, 16)
            load_x(0)
            for half in range(2):
                if half:
                    sp.wait_ge(mod_summed, 1)
                for k in range(DT):
                    sp.dma_start(wmod_sb[:, k * HALF:(k + 1) * HALF],
                                 wmod_t[:, k, half * HALF:(half + 1) * HALF]).then_inc(wmod_loaded, 16)
            for n, (_, src) in enumerate(pieces):
                if n == QKV * P // T + 2:
                    store_h(0)
                if n >= 2:
                    sp.wait_ge(w_low, n - 1)
                sp.dma_start(stage[n % 2][:], src).then_inc(w_loaded[n % 2], 16)
            load_x(1)
            store_h(1)

            def iteration(b, s1):
                if s1:
                    load_x(b + 2)
                    store_h(b + 2)
                residual(b)

            iteration(0, True)
            with sp.Fori(1, NB - 2) as b:
                iteration(b, True)
            iteration(NB - 2, False)
            iteration(NB - 1, False)
            sp.wait_ge(h_stored, 16 * NB)
            sp.wait_ge(x1_stored, 16 * DT * NB)

        @block.tensor
        def _(pe):
            def reduce(kind, b):
                slot = SLOT[kind]
                if kind == MEAN:
                    pe.wait_ge(tile_sum, 3 * (b + 1))
                else:
                    pe.wait_ge(sq_sum, 3 * (4 * b + WAVE[kind] + 1))
                if kind in (HSQ,):
                    pe.wait_ge(centred, DT * (b + 1))
                elif kind == QSQ:
                    pe.wait_ge(root, 4 * b + 2)
                elif kind == KSQ:
                    pe.wait_ge(root, 4 * b + 1)
                elif not (isinstance(b, int) and b == 0):
                    pe.wait_ge(root, 4 * b)
                nc.tensor.matmul(R_BANK[slot][:], ones[:], RS[:], start=True, stop=True).then_inc(reduced, 1)

            def three_pass(out, w, x, kt, last_kt, first=0):
                for k in range(kt):
                    for pw, px in ((0, 0), (1, 0), (0, 1)):
                        mm = nc.tensor.matmul(out, w(pw, k), x(px, k), start=(k == 0 and pw == 0 and px == 0),
                                              stop=(k == kt - 1 and px == 1))
                return mm

            def qkv(b, order=((1, 0), (0, 1), (2, 2))):
                pe.wait_ge(H_high, DT * (b + 1))
                pe.wait_ge(H_low, DT * (b + 1))
                n = 0
                for part, _ in order:
                    for c in range(DT):
                        out = bank[n % 2]
                        col = (part * DT + c) * P
                        if n >= 2:
                            pe.wait_ge(qkv_out, QKV * b + n - 1)
                        elif not (isinstance(b, int) and b == 0):
                            pe.wait_ge((ug_ready, g_silu)[n], FT * (b - 1))
                            pe.wait_ge(qkv_out, QKV * b)
                        three_pass(out[:], lambda pw, k: wqkv[:, pw, k, col:col + P],
                                   lambda px, k: H[:, px, k, :], DT, 0).then_inc(qkv_done, 1)
                        n += 1
                    if part == 0:
                        reduce(KSQ, b)
                reduce(QSQ, b)

            def output(b, j):
                pe.wait_ge(UG_high, FT * b + j + 1)
                pe.wait_ge(UG_low, FT * b + j + 1)
                if j == 0:
                    pe.wait_ge(res_sum, DT * b)
                for c in range(DT):
                    for pw, px in ((0, 0), (1, 0), (0, 1)):
                        mm = nc.tensor.matmul(O_BANK[c][:], wout[:, pw, j, c * P:(c + 1) * P], UG[:, j % 2, px, :],
                                              start=(j == 0 and pw == 0 and px == 0), stop=(j == FT - 1 and px == 1))
                mm.then_inc(out_used, 1)

            def swiglu(b, s2, s1):
                pe.wait_ge(Y_high, DT * (b + 1))
                pe.wait_ge(Y_low, DT * (b + 1))
                for j in range(FT):
                    for which, out, done, read in ((0, U_BANK, u_done, ug_ready), (1, G_BANK, g_done, g_silu)):
                        if j == 0:
                            pe.wait_ge(read, FT * b)
                            pe.wait_ge(qkv_out, QKV * (b + 2 if s2 else b + 1))
                        else:
                            pe.wait_ge(read, FT * b + j)
                        col = (which * FT + j) * P
                        three_pass(out[:], lambda pw, k: wsw[:, pw, k, col:col + P],
                                   lambda px, k: Y[:, px, k, :], DT, 0).then_inc(done, 1)
                    if s1 and j in (7, 9, 12):
                        reduce({7: MEAN, 9: VAR, 12: HSQ}[j], b + 2)
                    if j:
                        output(b, j - 1)
                output(b, FT - 1)

            def iteration(b, s2, s1):
                if s2:
                    qkv(b + 1)
                swiglu(b, s2, s1)

            pe.wait_ge(const_ready, 1)
            pe.wait_ge(c_silu, 1)
            for half in range(2):
                pe.wait_ge(wmod_loaded, 16 * DT * (half + 1))
                for n in range(3 * DT):
                    for k in range(DT):
                        mm = nc.tensor.matmul(bank[4 + half][:, n:n + 1], wmod_sb[:, k * HALF + n * P:k * HALF + (n + 1) * P],
                                              cc[:, 1, k:k + 1], start=(k == 0), stop=(k == DT - 1))
                mm.then_inc(mod_summed, 1)
            for kind in (MEAN, VAR, HSQ):
                reduce(kind, 0)
            pe.wait_ge(w_low, QKV * P // T)
            pe.wait_ge(w_high, QKV * P // T)
            qkv(0)
            for kind in (MEAN, VAR, HSQ):
                reduce(kind, 1)
            pe.wait_ge(w_low, len(pieces))
            pe.wait_ge(w_high, len(pieces))
            iteration(0, True, True)
            with pe.Fori(1, NB - 2) as b:
                iteration(b, True, True)
            iteration(NB - 2, True, False)
            iteration(NB - 1, False, False)

        @block.scalar
        def _(act):
            def square(kind, b, src, ready, per, c0=0):
                use = 4 * b + WAVE[kind]
                for c in range(DT):
                    act.wait_ge(ready, per * b + c0 + c + 1)
                    if c >= 2:
                        act.wait_ge(sq_sum, 3 * use + 1)
                    elif not (isinstance(b, int) and b == 0 and kind == VAR):
                        act.wait_ge(sq_sum, 3 * use - 1 + c)
                    nc.scalar.activation(SQ[:, c % 2, :], src[:, c, :], ACT.Square).then_inc(squared, 1)

            def sqrt(kind, b):
                slot = SLOT[kind]
                use = 4 * b + WAVE[kind]
                act.wait_ge(reduced, 5 * b + kind + 1)
                if kind == VAR:
                    if not (isinstance(b, int) and b == 0):
                        act.wait_ge(k_norm, DT * b)
                elif kind == HSQ:
                    if not (isinstance(b, int) and b == 0):
                        act.wait_ge(q_norm, DT * b)
                elif kind == KSQ:
                    act.wait_ge(scaled, DT * (b + 1))
                else:
                    act.wait_ge(hn_ready, DT * (b + 1))
                nc.scalar.activation(RD[:, slot, :], R_BANK[slot][:], ACT.Sqrt,
                                     bias=eps[:, (0 if kind == VAR else 1):(1 if kind == VAR else 2)]).then_inc(root, 1)

            def s1_var(b):
                square(VAR, b, X, centred, DT)

            def s1_h(b):
                square(HSQ, b, X, h_ready, DT)

            def s1_split(b):
                for c in range(DT):
                    act.wait_ge(hn_ready, DT * b + c + 1)
                    if c == 0 and not (isinstance(b, int) and b == 0):
                        act.wait_ge(qkv_done, QKV * b)
                    nc.scalar.activation(H[:, 0, c, :], X[:, c, :], ACT.Copy).then_inc(H_high, 1)

            def copy_out(b, n, dst):
                act.wait_ge(qkv_done, QKV * b + n + 1)
                nc.scalar.activation(dst[:, n % DT, :], bank[n % 2][:], ACT.Copy).then_inc(qkv_out, 1)

            def s2_copies(b):
                if isinstance(b, int) and b == 0:
                    act.wait_ge(w_low, len(pieces))
                else:
                    act.wait_ge(Y_low, DT * b)
                    act.wait_ge(Y_high, DT * b)
                    act.wait_ge(k_carry, DT * b)
                    act.wait_ge(v_carry, DT * b)
                for c in range(DT):
                    copy_out(b, c, K)
                square(KSQ, b, K, qkv_out, QKV)
                for c in range(DT):
                    copy_out(b, DT + c, Q)
                copy_out(b, 2 * DT, V)
                square(QSQ, b, Q, qkv_out, QKV, c0=DT)
                for c in range(1, DT):
                    copy_out(b, 2 * DT + c, V)

            def s2_exp(b):
                for c in range(DT):
                    act.wait_ge(k_norm, DT * b + c + 1)
                    nc.scalar.activation(K[:, c, :], K[:, c, :], ACT.Exp).then_inc(k_exp, 1)

            def s2_sigmoid(b):
                for c in range(DT):
                    act.wait_ge(q_norm, DT * b + c + 1)
                    nc.scalar.activation(Q[:, c, :], Q[:, c, :], ACT.Sigmoid).then_inc(q_sig, 1)

            def s2_split(b):
                if not (isinstance(b, int) and b == 0):
                    act.wait_ge(g_done, FT * b)
                for c in range(DT):
                    act.wait_ge(y_ready, DT * b + c + 1)
                    nc.scalar.activation(Y[:, 0, c, :], V[:, c, :], ACT.Copy).then_inc(Y_high, 1)

            def hidden(b, j):
                act.wait_ge(g_done, FT * b + j + 1)
                act.wait_ge(UG_low, FT * b + j)
                nc.scalar.activation(G[:], G_BANK[:], ACT.Silu).then_inc(g_silu, 1)
                act.wait_ge(ug_ready, FT * b + j + 1)
                if j >= 2:
                    act.wait_ge(out_used, FT * b + j - 1)
                else:
                    act.wait_ge(out_used, FT * b)
                nc.scalar.activation(UG[:, j % 2, 0, :], G[:], ACT.Copy).then_inc(UG_high, 1)

            def iteration(b, s2, s1):
                if s2:
                    s2_copies(b + 1)
                for j in range(FT):
                    hidden(b, j)
                    if s2 and j == 1:
                        sqrt(KSQ, b + 1)
                        sqrt(QSQ, b + 1)
                    if s2 and j == 2:
                        s2_exp(b + 1)
                    if s2 and j == 3:
                        s2_sigmoid(b + 1)
                    if s1 and j == 8:
                        s1_var(b + 2)
                    if s1 and j == 9:
                        sqrt(VAR, b + 2)
                    if s1 and j == 11:
                        s1_h(b + 2)
                    if s1 and j == 12:
                        sqrt(HSQ, b + 2)
                    if s1 and j == 14:
                        s1_split(b + 2)
                if s2:
                    s2_split(b + 1)

            def split(n):
                act.wait_ge(w_loaded[n % 2], 16 * (n // 2 + 1))
                if n == QKV * P // T:
                    act.wait_ge(mod_summed, 2)
                nc.scalar.activation(pieces[n][0][:, 0], stage[n % 2][:], ACT.Copy).then_inc(w_high, 1)

            act.wait_ge(c_loaded, 16)
            nc.scalar.activation(cc[:, 1, :], cc[:, 0, :], ACT.Silu).then_inc(c_silu, 1)
            for n in range(QKV * P // T):
                split(n)
            act.wait_ge(const_ready, 1)
            s1_var(0)
            sqrt(VAR, 0)
            s1_h(0)
            sqrt(HSQ, 0)
            s1_split(0)
            for n in range(QKV * P // T, len(pieces)):
                split(n)
            s2_copies(0)
            sqrt(KSQ, 0)
            sqrt(QSQ, 0)
            s2_exp(0)
            s2_sigmoid(0)
            s2_split(0)
            s1_var(1)
            sqrt(VAR, 1)
            s1_h(1)
            sqrt(HSQ, 1)
            s1_split(1)
            iteration(0, True, True)
            with act.Fori(1, NB - 2) as b:
                iteration(b, True, True)
            iteration(NB - 2, True, False)
            iteration(NB - 1, False, False)

        @block.gpsimd
        def _(pool):
            def add_squares(kind, b):
                use = 4 * b + WAVE[kind]
                pool.wait_ge(reduced, 5 * b + kind)
                pool.wait_ge(squared, DT * use + 2)
                nc.gpsimd.tensor_tensor(RS[:], SQ[:, 0, :], SQ[:, 1, :], ALU.add).then_inc(sq_sum, 1)
                for c in range(2, DT):
                    pool.wait_ge(squared, DT * use + c + 1)
                    pool.wait_ge(sq_sum, 3 * use + c - 1)
                    nc.gpsimd.tensor_tensor(RS[:], RS[:], SQ[:, c % 2, :], ALU.add).then_inc(sq_sum, 1)

            def add_x(b):
                pool.wait_ge(x_loaded, 16 * (b + 1))
                if not (isinstance(b, int) and b == 0):
                    pool.wait_ge(reduced, 5 * b)
                nc.gpsimd.tensor_tensor(RS[:], X[:, 0, :], X[:, 1, :], ALU.add).then_inc(tile_sum, 1)
                for c in range(2, DT):
                    pool.wait_ge(tile_sum, 3 * b + c - 1)
                    nc.gpsimd.tensor_tensor(RS[:], RS[:], X[:, c, :], ALU.add).then_inc(tile_sum, 1)

            def weigh(b):
                for c in range(DT):
                    pool.wait_ge(k_exp, DT * b + c + 1)
                    pool.wait_ge(qkv_out, QKV * (b + 1))
                    nc.gpsimd.tensor_tensor(V[:, c, :], K[:, c, :], V[:, c, :], ALU.mult).then_inc(wv_ready, 1)

            def low(b, j):
                pool.wait_ge(UG_high, FT * b + j + 1)
                nc.gpsimd.tensor_tensor(UG[:, j % 2, 1, :], G[:], UG[:, j % 2, 0, :], ALU.subtract).then_inc(UG_low, 1)

            def iteration(b, s2, s1):
                if s2:
                    add_squares(KSQ, b + 1)
                    add_squares(QSQ, b + 1)
                for j in range(FT):
                    low(b, j)
                    if s2 and j == 2:
                        weigh(b + 1)
                    if s1 and j == 6:
                        add_x(b + 2)
                    if s1 and j == 8:
                        add_squares(VAR, b + 2)
                    if s1 and j == 11:
                        add_squares(HSQ, b + 2)

            add_x(0)
            add_squares(VAR, 0)
            add_squares(HSQ, 0)
            add_squares(KSQ, 0)
            add_squares(QSQ, 0)
            weigh(0)
            add_x(1)
            add_squares(VAR, 1)
            add_squares(HSQ, 1)
            iteration(0, True, True)
            with pool.Fori(1, NB - 2) as b:
                iteration(b, True, True)
            iteration(NB - 2, True, False)
            iteration(NB - 1, False, False)

        @block.vector
        def _(dve):
            def inverse(kind, b):
                n = 4 * b + WAVE[kind] + 1
                dve.wait_ge(root, n)
                nc.vector.reciprocal(RD[:, SLOT[kind], :], RD[:, SLOT[kind], :]).then_inc(recip, 1)
                dve.wait_ge(recip, n)

            def times(dst, a, b_, done):
                nc.vector.tensor_tensor(dst, a, b_, ALU.mult).then_inc(done, 1)

            def s1_centre(b):
                dve.wait_ge(reduced, 5 * b + MEAN + 1)
                for c in range(DT):
                    nc.vector.tensor_tensor(X[:, c, :], X[:, c, :], R_BANK[SLOT[MEAN]][:], ALU.subtract).then_inc(centred, 1)

            def s1_modulate(b):
                inverse(VAR, b)
                for c in range(DT):
                    dve.wait_ge(squared, DT * (4 * b + WAVE[VAR] + 1))
                    times(X[:, c, :], X[:, c, :], RD[:, SLOT[VAR], :], scaled)
                for c in range(DT):
                    dve.wait_ge(scaled, DT * b + c + 1)
                    nc.vector.tensor_scalar(X[:, c, :], X[:, c, :], mod[:, CA][:, c:c + 1], mod[:, SA][:, c:c + 1],
                                            ALU.mult, ALU.add).then_inc(h_ready, 1)

            def s1_norm(b):
                inverse(HSQ, b)
                dve.wait_ge(h_stored, 16 * (b + 1))
                dve.wait_ge(squared, DT * (4 * b + WAVE[HSQ] + 1))
                for c in range(DT):
                    times(X[:, c, :], X[:, c, :], RD[:, SLOT[HSQ], :], hn_ready)

            def s1_low(b):
                for c in range(DT):
                    dve.wait_ge(H_high, DT * b + c + 1)
                    nc.vector.tensor_tensor(H[:, 1, c, :], X[:, c, :], H[:, 0, c, :], ALU.subtract).then_inc(H_low, 1)

            def s2_norm(b):
                inverse(KSQ, b)
                for c in range(DT):
                    times(K[:, c, :], K[:, c, :], RD[:, SLOT[KSQ], :], k_norm)
                inverse(QSQ, b)
                for c in range(DT):
                    times(Q[:, c, :], Q[:, c, :], RD[:, SLOT[QSQ], :], q_norm)

            def scan(b, buf, which, ready, done, copied):
                for c in range(DT):
                    dve.wait_ge(ready, DT * b + c + 1)
                    dve.wait_ge(wv_ready, DT * b + c + 1)
                    if not (isinstance(b, int) and b == 0):
                        dve.wait_ge(copied, DT * b)
                    first = isinstance(b, int) and b == 0
                    nc.vector.tensor_tensor_scan(buf[:, c, :], run[:], buf[:, c, :],
                                                 0.0 if first else carry[:, which, c:c + 1],
                                                 ALU.mult, ALU.add).then_inc(done, 1)
                for c in range(DT):
                    dve.wait_ge(done, DT * b + c + 1)
                    nc.vector.tensor_copy(carry[:, which, c:c + 1], buf[:, c, T - 1:T]).then_inc(copied, 1)

            def s2_inverse(b):
                for c in range(DT):
                    dve.wait_ge(k_carry, DT * b + c + 1)
                    nc.vector.tensor_scalar(K[:, c, :], K[:, c, :], v["CUM_EPS"], None, ALU.add).then_inc(k_eps, 1)
                for c in range(DT):
                    dve.wait_ge(k_eps, DT * b + c + 1)
                    nc.vector.reciprocal(K[:, c, :], K[:, c, :]).then_inc(k_inv, 1)

            def s2_mean(b):
                for c in range(DT):
                    dve.wait_ge(k_inv, DT * b + c + 1)
                    dve.wait_ge(v_carry, DT * b + c + 1)
                    times(V[:, c, :], V[:, c, :], K[:, c, :], kv_mean)

            def s2_gate(b):
                for c in range(DT):
                    dve.wait_ge(kv_mean, DT * b + c + 1)
                    dve.wait_ge(q_sig, DT * b + c + 1)
                    times(V[:, c, :], V[:, c, :], Q[:, c, :], y_ready)

            def s2_low(b):
                for c in range(DT):
                    dve.wait_ge(Y_high, DT * b + c + 1)
                    nc.vector.tensor_tensor(Y[:, 1, c, :], V[:, c, :], Y[:, 0, c, :], ALU.subtract).then_inc(Y_low, 1)

            def hidden(b, j):
                dve.wait_ge(u_done, FT * b + j + 1)
                dve.wait_ge(g_silu, FT * b + j + 1)
                times(G[:], G[:], U_BANK[:], ug_ready)

            def residual(b):
                dve.wait_ge(out_used, FT * (b + 1))
                for c in range(DT):
                    n = DT * b + c
                    dve.wait_ge(res_loaded, 32 * (n + 1))
                    nc.vector.tensor_tensor(HR[:], HR[:], O_BANK[c][:], ALU.add).then_inc(res_sum, 1)
                    dve.wait_ge(res_sum, n + 1)
                    nc.vector.scalar_tensor_tensor(XR[:], HR[:], mod[:, GA][:, c:c + 1], XR[:],
                                                   ALU.mult, ALU.add).then_inc(x1_ready, 1)

            def iteration(b, s2, s1):
                for j in range(FT):
                    hidden(b, j)
                    if s2 and j == 1:
                        s2_norm(b + 1)
                    if s2 and j == 3:
                        scan(b + 1, K, 0, k_exp, k_run, k_carry)
                    if s2 and j == 4:
                        scan(b + 1, V, 1, wv_ready, v_run, v_carry)
                    if s2 and j == 5:
                        s2_inverse(b + 1)
                    if s2 and j == 6:
                        s2_mean(b + 1)
                        s2_gate(b + 1)
                    if s1 and j == 7:
                        s1_centre(b + 2)
                    if s1 and j == 10:
                        s1_modulate(b + 2)
                    if s1 and j == 13:
                        s1_norm(b + 2)
                    if s1 and j == 15:
                        s1_low(b + 2)
                if s2:
                    s2_low(b + 1)
                residual(b)

            def split(n):
                dve.wait_ge(w_high, n + 1)
                nc.vector.tensor_tensor(pieces[n][0][:, 1], stage[n % 2][:], pieces[n][0][:, 0],
                                        ALU.subtract).then_inc(w_low, 1)

            nc.vector.memset(ones[:], 1.0 / (DT * P)).then_inc(mod_step, 1)
            nc.vector.memset(eps[:, 0:1], v["LN_EPS"]).then_inc(mod_step, 1)
            nc.vector.memset(eps[:, 1:2], v["RMS_EPS"]).then_inc(mod_step, 1)
            nc.vector.memset(eps[:, 2:3], v["FFN_EPS"]).then_inc(mod_step, 1)
            nc.vector.memset(run[:], 1.0).then_inc(mod_step, 1)
            dve.wait_ge(mod_step, 5)
            nc.vector.memset(gtmp[:], 0.0).then_inc(const_ready, 1)
            for n in range(QKV * P // T):
                split(n)
            for half in range(2):
                dve.wait_ge(mod_summed, half + 1)
                nc.vector.tensor_copy(mod[:, half * 3 * DT:(half + 1) * 3 * DT], bank[4 + half][:, 0:3 * DT]).then_inc(mod_copied, 1)
                dve.wait_ge(mod_copied, half + 1)
                cols = mod[:, (3 * half + 1) * DT:(3 * half + 2) * DT]
                gate = mod[:, (3 * half + 2) * DT:(3 * half + 3) * DT]
                n = 5 + 5 * half
                sign, size = gtmp[:, 0, 0:DT], gtmp[:, 1, 0:DT]
                nc.vector.tensor_scalar(cols, cols, 1.0, None, ALU.add).then_inc(mod_step, 1)
                nc.vector.tensor_scalar(sign, gate, 0.0, 2.0, ALU.is_ge, ALU.mult).then_inc(mod_step, 1)
                nc.vector.scalar_tensor_tensor(size, gate, -1.0, gate, ALU.mult, ALU.max).then_inc(mod_step, 1)
                dve.wait_ge(mod_step, n + 3)
                nc.vector.tensor_scalar(size, size, 0.25, None, ALU.max).then_inc(mod_step, 1)
                dve.wait_ge(mod_step, n + 4)
                nc.vector.scalar_tensor_tensor(gate, sign, -1.0, size, ALU.add, ALU.mult).then_inc(mod_step, 1)
                dve.wait_ge(mod_step, n + 5)
            s1_centre(0)
            s1_modulate(0)
            s1_norm(0)
            s1_low(0)
            for n in range(QKV * P // T, len(pieces)):
                split(n)
            s2_norm(0)
            scan(0, K, 0, k_exp, k_run, k_carry)
            scan(0, V, 1, wv_ready, v_run, v_carry)
            s2_inverse(0)
            s2_mean(0)
            s2_gate(0)
            s2_low(0)
            s1_centre(1)
            s1_modulate(1)
            s1_norm(1)
            s1_low(1)
            iteration(0, True, True)
            with dve.Fori(1, NB - 2) as b:
                iteration(b, True, True)
            iteration(NB - 2, True, False)
            iteration(NB - 1, False, False)


def ffn(nc, v):
    T, NB, DT, I_T, GU, D = v["T"], v["NB"], v["DT"], v["I_T"], v["GU"], v["D"]
    mod, ones, eps, bank = v["mod"], v["ones"], v["eps"], v["bank"]
    SB, CB, GB = v["SB"], v["CB"], v["GB"]
    x1_t, outT_t = v["x1_t"], v["outT_t"]
    NSUM = DT - 1
    with ExitStack() as ctx:
        def sb(name, shape, dt):
            return ctx.enter_context(nc.sbuf_tensor("f_" + name, shape, dt))

        def sem(name):
            return v["sem"]("f_" + name)

        DOWN = I_T * D
        CH = DOWN // 4
        NC = (GU + DOWN) // CH
        assert CH * NC == GU + DOWN and GU % CH == 0 and DOWN % CH == 0
        word = sb("word", [P, 2, CH], I32)
        low3 = sb("low3", [P, CH], I32)
        bit3 = sb("bit3", [P, CH], I32)
        t1 = sb("t1", [P, CH], F32)
        t2 = sb("t2", [P, CH], F32)
        lane = sb("lane", [P, 1], I32)
        shift = sb("shift", [P, 1], I32)
        gu_16 = sb("gu_16", [P, 2 * I_T, DT], F16)
        gu_s = sb("gu_s", [P, 2 * I_T, DT], F32)
        down_row = sb("down_row", [P, DOWN], F16)
        down_hi = sb("down_hi", [P, DOWN], F16)
        down_lo = sb("down_lo", [P, DOWN], BF16)
        values = sb("values", [P, GU], BF16)
        N = sb("N", [P, DT, T], F32)
        H = sb("H", [P, 2, 2, DT, T], F16)
        SQ = sb("SQ", [P, 2, T], F32)
        SQY = sb("SQY", [P, 2, T], F32)
        RS = sb("RS", [P, T], F32)
        RSY = sb("RSY", [P, T], F32)
        RV = sb("RV", [P, T], F32)
        RY = sb("RY", [P, T], F32)
        A = sb("A", [P, 3, 4, T], F32)
        HH = sb("HH", [P, 3, 2, T], F16)
        Y = sb("Y", [P, DT, T], F32)
        X = sb("X", [P, DT, T], F32)
        EV = bank[0:3]
        R = bank[3]
        O = bank[4:8]

        def slot(j):
            return 2 if j == I_T - 1 else j % 2

        GROUPS = 2 * DT
        EV_BANK = [m % 3 for m in range(GROUPS)]

        def before(m):
            if m >= 3:
                return 0, m - 3
            return 1, max(k for k in range(GROUPS) if EV_BANK[k] == EV_BANK[m])

        lane_ready, shift_ready, words_loaded, decode = map(sem, ("lane_ready", "shift_ready", "words_loaded", "decode"))
        wordsem = [words_loaded, sem("words_loaded1")]
        words_used, decoded = sem("words_used"), sem("decoded")
        scales_loaded, scales_ready = sem("scales_loaded"), sem("scales_ready")
        n_loaded, x_sum, mean_red, centred = map(sem, ("n_loaded", "x_sum", "mean_red", "centred"))
        squared, sq_sum, var_red, var_root, var_recip = map(sem, ("squared", "sq_sum", "var_red", "var_root", "var_recip"))
        scaled, h_ready, H_high, H_low = map(sem, ("scaled", "h_ready", "H_high", "H_low"))
        group_done, by_act, by_dve = map(sem, ("group_done", "by_act", "by_dve"))
        halves, gate_silu, hid_ready = map(sem, ("halves", "gate_silu", "hid_ready"))
        HH_high, HH_low, down_used, y_copied = map(sem, ("HH_high", "HH_low", "down_used", "y_copied"))
        y_squared, y_sum, y_red, y_root, y_recip = map(sem, ("y_squared", "y_sum", "y_red", "y_root", "y_recip"))
        y_norm, res_loaded, out_ready, out_stored = map(sem, ("y_norm", "res_loaded", "out_ready", "out_stored"))

        block = ctx.enter_context(nc.Block())

        def tok(b):
            return bass.ds(b * T, T)

        def first(b):
            return isinstance(b, int) and b == 0

        def blocks(eng, iteration):
            iteration(0, 0, False, True)
            iteration(1, 1, True, True)
            iteration(2, 0, True, True)
            with eng.Fori(3, NB - 2, 2) as b:
                iteration(b, 1, True, True)
                iteration(b + 1, 0, True, True)
            iteration(NB - 1, 1, True, False)

        def slot_free(eng, done, b, j):
            if j < 2:
                if not first(b):
                    eng.wait_ge(done, I_T * b - 2 + j)
            elif j == I_T - 1:
                if not first(b):
                    eng.wait_ge(done, I_T * b)
            else:
                eng.wait_ge(done, I_T * b + j - 1)

        @block.sync
        def _(sp):
            sp.dma_start(gu_16[:], v["gu_scales"]).then_inc(scales_loaded, 16)
            sp.dma_start(down_row[:], v["down_scales"].to_broadcast([P, DOWN])).then_inc(scales_loaded, 16)
            sp.dma_start(N[:], x1_t[:, :, tok(0)]).then_inc(n_loaded, 16)
            for n in range(NC):
                if n >= 2:
                    sp.wait_ge(words_used, n - 1)
                for r in range(P // 8):
                    sp.dma_start(word[8 * r:8 * r + 8, n % 2, :],
                                 v["packed"][r:r + 1, n * CH:(n + 1) * CH].to_broadcast([8, CH])).then_inc(wordsem[n % 2], 16)

            def iteration(b, s, prev, nxt):
                if nxt:
                    sp.wait_ge(H_low, DT * (b + 1))
                    sp.dma_start(N[:], x1_t[:, :, tok(b + 1)]).then_inc(n_loaded, 16)
                if prev:
                    output(b - 1)

            def output(b):
                if not first(b):
                    sp.wait_ge(out_stored, 16 * b)
                sp.dma_start(X[:], x1_t[:, :, tok(b)]).then_inc(res_loaded, 16)
                sp.wait_ge(out_ready, DT * (b + 1))
                sp.dma_start(outT_t[:, :, tok(b)], X[:]).then_inc(out_stored, 16)

            blocks(sp, iteration)
            output(NB - 1)
            sp.wait_ge(out_stored, 16 * NB)

        @block.tensor
        def _(pe):
            def bank_free(means, variances, ys):
                for s, n in ((centred, means * DT), (var_root, variances), (y_root, ys)):
                    if not (isinstance(n, int) and n <= 0):
                        pe.wait_ge(s, n)

            def mean(b):
                pe.wait_ge(x_sum, NSUM * (b + 1))
                nc.tensor.matmul(R[:], ones[:], RS[:], start=True, stop=True).then_inc(mean_red, 1)

            def variance(b):
                pe.wait_ge(sq_sum, NSUM * (b + 1))
                nc.tensor.matmul(R[:], ones[:], RS[:], start=True, stop=True).then_inc(var_red, 1)

            def y_square(b):
                pe.wait_ge(y_sum, NSUM * (b + 1))
                nc.tensor.matmul(R[:], ones[:], RSY[:], start=True, stop=True).then_inc(y_red, 1)

            def down(b, j):
                pe.wait_ge(HH_high, I_T * b + j + 1)
                pe.wait_ge(HH_low, I_T * b + j + 1)
                if j == 0 and not first(b):
                    pe.wait_ge(y_copied, DT * b)
                for c in range(DT):
                    col = j * D + c * P
                    for w, part in ((down_hi, 0), (down_lo, 0), (down_hi, 1)):
                        mm = nc.tensor.matmul(O[c][:], w[:, col:col + P], HH[:, slot(j), part, :],
                                              start=(j == 0 and w is down_hi and part == 0),
                                              stop=(j == I_T - 1 and part == 1))
                mm.then_inc(down_used, 1)

            def iteration(b, s, prev, nxt):
                pe.wait_ge(H_high, DT * (b + 1))
                pe.wait_ge(H_low, DT * (b + 1))
                for j in range(I_T):
                    if nxt and j == 5:
                        bank_free(b + 2, b + 1, b)
                        variance(b + 1)
                    for m in range(GROUPS):
                        back, k = before(m)
                        if not (j == 0 and back and first(b)):
                            pe.wait_ge((by_act, by_dve)[k % 2], DT * (I_T * b + j - back) + k // 2 + 1)
                        which, g = m // DT, m % DT
                        col = (g * 2 * I_T + which * I_T + j) * P
                        for part in range(2):
                            mm = nc.tensor.matmul(EV[EV_BANK[m]][:], values[:, col:col + P], H[:, s, part, g, :],
                                                  start=part == 0, stop=part == 1)
                        mm.then_inc(group_done, 1)
                    if j >= 2:
                        down(b, j - 2)
                    elif prev:
                        down(b - 1, I_T - 2 + j)
                    if nxt and j == 1:
                        bank_free(b + 1, b + 1, b - 1)
                        mean(b + 1)
                    if prev and j == 3:
                        bank_free(b + 2 if nxt else b + 1, b + 1, b - 1)
                        y_square(b - 1)

            mean(0)
            bank_free(1, 0, 0)
            variance(0)
            pe.wait_ge(decoded, NC)
            blocks(pe, iteration)
            down(NB - 1, I_T - 2)
            down(NB - 1, I_T - 1)
            bank_free(NB, NB, NB - 1)
            y_square(NB - 1)

        @block.scalar
        def _(act):
            def squares(b, ring, src, ready, done, sums):
                for c in range(DT):
                    act.wait_ge(ready, DT * b + c + 1)
                    if c >= 2:
                        act.wait_ge(sums, NSUM * b + 1)
                    elif not first(b):
                        act.wait_ge(sums, NSUM * b)
                    nc.scalar.activation(ring[:, c % 2, :], src[:, c, :], ACT.Square).then_inc(done, 1)

            def var_sqrt(b):
                act.wait_ge(var_red, b + 1)
                if not first(b):
                    act.wait_ge(scaled, DT * b)
                nc.scalar.activation(RV[:], R[:], ACT.Sqrt, bias=eps[:, 0:1]).then_inc(var_root, 1)

            def y_sqrt(b):
                act.wait_ge(y_red, b + 1)
                if not first(b):
                    act.wait_ge(y_norm, DT * b)
                nc.scalar.activation(RY[:], R[:], ACT.Sqrt, bias=eps[:, 2:3]).then_inc(y_root, 1)

            def split(b, s):
                if not first(b) and not (isinstance(b, int) and b == 1):
                    act.wait_ge(group_done, GROUPS * I_T * (b - 1))
                for c in range(DT):
                    act.wait_ge(h_ready, DT * b + c + 1)
                    nc.scalar.activation(H[:, s, 0, c, :], N[:, c, :], ACT.Copy).then_inc(H_high, 1)

            def take(b, j, m):
                which, g = m // DT, m % DT
                act.wait_ge(group_done, GROUPS * (I_T * b + j) + m + 1)
                if m == 0:
                    slot_free(act, HH_low, b, j)
                t = which * I_T + j
                nc.scalar.activation(A[:, slot(j), 2 * which + g // 2, :], EV[EV_BANK[m]][:], ACT.Copy,
                                     scale=gu_s[:, t, g:g + 1]).then_inc(by_act, 1)

            def high(b, j):
                act.wait_ge(hid_ready, I_T * b + j + 1)
                slot_free(act, down_used, b, j)
                nc.scalar.activation(HH[:, slot(j), 0, :], A[:, slot(j), 0, :], ACT.Copy).then_inc(HH_high, 1)

            def silu(b, j):
                act.wait_ge(halves, 2 * (I_T * b + j) + 1)
                nc.scalar.activation(A[:, slot(j), 0, :], A[:, slot(j), 0, :], ACT.Silu).then_inc(gate_silu, 1)

            def iteration(b, s, prev, nxt):
                for j in range(I_T):
                    take(b, j, 0)
                    take(b, j, 2)
                    take(b, j, 4)
                    if j:
                        high(b, j - 1)
                    elif prev:
                        high(b - 1, I_T - 1)
                    take(b, j, 6)
                    silu(b, j)
                    if prev and j == 2:
                        squares(b - 1, SQY, Y, y_copied, y_squared, y_sum)
                    if nxt and j == 3:
                        squares(b + 1, SQ, N, centred, squared, sq_sum)
                    if j == 4:
                        if prev:
                            y_sqrt(b - 1)
                        if nxt:
                            var_sqrt(b + 1)
                    if nxt and j == 9:
                        split(b + 1, 1 - s)

            act.wait_ge(scales_loaded, 32)
            nc.scalar.activation(gu_s[:], gu_16[:], ACT.Copy).then_inc(scales_ready, 1)
            act.wait_ge(scales_ready, 1)
            squares(0, SQ, N, centred, squared, sq_sum)
            var_sqrt(0)
            split(0, 0)
            blocks(act, iteration)
            high(NB - 1, I_T - 1)
            squares(NB - 1, SQY, Y, y_copied, y_squared, y_sum)
            y_sqrt(NB - 1)

        @block.gpsimd
        def _(pool):
            def add_up(b, ring, rs, done, sums, reduced, reductions):
                for c in range(1, DT):
                    pool.wait_ge(done, DT * b + c + 1)
                    if c == 1:
                        if not (isinstance(reductions, int) and reductions == 0):
                            pool.wait_ge(reduced, reductions)
                        a = ring[:, 0, :]
                    else:
                        pool.wait_ge(sums, NSUM * b + c - 1)
                        a = rs[:]
                    nc.gpsimd.tensor_tensor(rs[:], a, ring[:, c % 2, :], ALU.add).then_inc(sums, 1)

            def add_x(b):
                pool.wait_ge(n_loaded, 16 * (b + 1))
                if not first(b):
                    pool.wait_ge(var_red, b)
                nc.gpsimd.tensor_tensor(RS[:], N[:, 0, :], N[:, 1, :], ALU.add).then_inc(x_sum, 1)
                for c in range(2, DT):
                    pool.wait_ge(x_sum, NSUM * b + c - 1)
                    nc.gpsimd.tensor_tensor(RS[:], RS[:], N[:, c, :], ALU.add).then_inc(x_sum, 1)

            def half(b, j, which):
                pool.wait_ge(by_dve, DT * (I_T * b + j) + 2 * which + 2)
                a = A[:, slot(j), 2 * which, :]
                nc.gpsimd.tensor_tensor(a, a, A[:, slot(j), 2 * which + 1, :], ALU.add).then_inc(halves, 1)

            def low(b, j):
                pool.wait_ge(HH_high, I_T * b + j + 1)
                nc.gpsimd.tensor_tensor(HH[:, slot(j), 1, :], A[:, slot(j), 0, :], HH[:, slot(j), 0, :],
                                        ALU.subtract).then_inc(HH_low, 1)

            def scale(b):
                pool.wait_ge(var_recip, b + 1)
                pool.wait_ge(squared, DT * (b + 1))
                for c in range(DT):
                    nc.gpsimd.tensor_tensor(N[:, c, :], N[:, c, :], RV[:], ALU.mult).then_inc(scaled, 1)

            def iteration(b, s, prev, nxt):
                for j in range(I_T):
                    half(b, j, 0)
                    if j:
                        low(b, j - 1)
                    elif prev:
                        low(b - 1, I_T - 1)
                    half(b, j, 1)
                    if nxt and j == 0:
                        add_x(b + 1)
                    if prev and j == 2:
                        add_up(b - 1, SQY, RSY, y_squared, y_sum, y_red, b - 1)
                    if nxt and j == 3:
                        add_up(b + 1, SQ, RS, squared, sq_sum, mean_red, b + 2)
                    if nxt and j == 6:
                        scale(b + 1)

            nc.gpsimd.iota(lane[:], pattern=[[0, 1]], base=0, channel_multiplier=1).then_inc(lane_ready, 1)
            add_x(0)
            add_up(0, SQ, RS, squared, sq_sum, mean_red, 1)
            scale(0)
            blocks(pool, iteration)
            low(NB - 1, I_T - 1)
            add_up(NB - 1, SQY, RSY, y_squared, y_sum, y_red, NB - 1)

        @block.vector
        def _(dve):
            def centre(b):
                dve.wait_ge(mean_red, b + 1)
                for c in range(DT):
                    nc.vector.tensor_tensor(N[:, c, :], N[:, c, :], R[:], ALU.subtract).then_inc(centred, 1)

            def inverse(b, buf, root, recip):
                dve.wait_ge(root, b + 1)
                nc.vector.reciprocal(buf[:], buf[:]).then_inc(recip, 1)

            def modulate(b):
                for c in range(DT):
                    dve.wait_ge(scaled, DT * b + c + 1)
                    nc.vector.tensor_scalar(N[:, c, :], N[:, c, :], mod[:, CB][:, c:c + 1], mod[:, SB][:, c:c + 1],
                                            ALU.mult, ALU.add).then_inc(h_ready, 1)

            def split_low(b, s):
                for c in range(DT):
                    dve.wait_ge(H_high, DT * b + c + 1)
                    nc.vector.tensor_tensor(H[:, s, 1, c, :], N[:, c, :], H[:, s, 0, c, :], ALU.subtract).then_inc(H_low, 1)

            def take(b, j, m):
                which, g = m // DT, m % DT
                dve.wait_ge(group_done, GROUPS * (I_T * b + j) + m + 1)
                dve.wait_ge(by_act, DT * (I_T * b + j) + m // 2 + 1)
                a = A[:, slot(j), 2 * which + g // 2, :]
                nc.vector.scalar_tensor_tensor(a, EV[EV_BANK[m]][:], gu_s[:, which * I_T + j, g:g + 1], a,
                                               ALU.mult, ALU.add).then_inc(by_dve, 1)

            def hidden(b, j):
                dve.wait_ge(gate_silu, I_T * b + j + 1)
                dve.wait_ge(halves, 2 * (I_T * b + j) + 2)
                a = A[:, slot(j), 0, :]
                nc.vector.tensor_tensor(a, a, A[:, slot(j), 2, :], ALU.mult).then_inc(hid_ready, 1)

            def copy_y(b):
                dve.wait_ge(down_used, I_T * (b + 1))
                if not first(b):
                    dve.wait_ge(out_ready, DT * b)
                for c in range(DT):
                    nc.vector.tensor_copy(Y[:, c, :], O[c][:]).then_inc(y_copied, 1)

            def norm_y(b):
                dve.wait_ge(y_recip, b + 1)
                dve.wait_ge(y_squared, DT * (b + 1))
                for c in range(DT):
                    nc.vector.tensor_tensor(Y[:, c, :], Y[:, c, :], RY[:], ALU.mult).then_inc(y_norm, 1)

            def result(b):
                dve.wait_ge(res_loaded, 16 * (b + 1))
                for c in range(DT):
                    dve.wait_ge(y_norm, DT * b + c + 1)
                    nc.vector.scalar_tensor_tensor(X[:, c, :], Y[:, c, :], mod[:, GB][:, c:c + 1], X[:, c, :],
                                                   ALU.mult, ALU.add).then_inc(out_ready, 1)

            def iteration(b, s, prev, nxt):
                for j in range(I_T):
                    if prev and j == 2:
                        copy_y(b - 1)
                    if nxt and j == 2:
                        centre(b + 1)
                    take(b, j, 1)
                    if j:
                        hidden(b, j - 1)
                    elif prev:
                        hidden(b - 1, I_T - 1)
                    take(b, j, 3)
                    take(b, j, 5)
                    take(b, j, 7)
                    if j == 6:
                        if nxt:
                            inverse(b + 1, RV, var_root, var_recip)
                        if prev:
                            inverse(b - 1, RY, y_root, y_recip)
                    if prev and j == 7:
                        norm_y(b - 1)
                    if nxt and j == 8:
                        modulate(b + 1)
                    if prev and j == 9:
                        result(b - 1)
                    if nxt and j == 10:
                        split_low(b + 1, 1 - s)

            dve.wait_ge(lane_ready, 1)
            nc.vector.tensor_scalar(lane[:], lane[:], 7, 2, ALU.bitwise_and, ALU.logical_shift_left).then_inc(shift_ready, 1)
            dve.wait_ge(shift_ready, 1)
            nc.vector.tensor_copy(shift[:], lane[:]).then_inc(shift_ready, 1)
            dve.wait_ge(shift_ready, 2)
            centre(0)
            steps = [0]

            def step(ins, hold=True):
                ins.then_inc(decode, 1)
                steps[0] += 1
                if hold:
                    dve.wait_ge(decode, steps[0])

            for n in range(NC):
                dve.wait_ge(wordsem[n % 2], 16 * (P // 8) * (n // 2 + 1))
                w = word[:, n % 2, :]
                step(nc.vector.tensor_scalar(low3[:], w, shift[:, 0:1], 7, ALU.logical_shift_right, ALU.bitwise_and), False)
                nc.vector.tensor_scalar(bit3[:], w, shift[:, 0:1], 8, ALU.logical_shift_right, ALU.bitwise_and).then_inc(words_used, 1)
                dve.wait_ge(decode, steps[0])
                step(nc.vector.scalar_tensor_tensor(t1[:], low3[:], 4.0, low3[:], ALU.max, ALU.add), False)
                step(nc.vector.tensor_scalar(t2[:], low3[:], 6.0, 2.0, ALU.max, ALU.mult))
                step(nc.vector.scalar_tensor_tensor(t1[:], t1[:], -16.0, t2[:], ALU.add, ALU.add))
                dve.wait_ge(words_used, n + 1)
                step(nc.vector.tensor_scalar(t2[:], bit3[:], -0.125, 0.5, ALU.mult, ALU.add))
                if n * CH < GU:
                    nc.vector.tensor_tensor(values[:, n * CH:(n + 1) * CH], t1[:], t2[:], ALU.mult).then_inc(decoded, 1)
                else:
                    at = slice(n * CH - GU, (n + 1) * CH - GU)
                    dve.wait_ge(scales_loaded, 32)
                    step(nc.vector.tensor_tensor(t1[:], t1[:], t2[:], ALU.mult))
                    step(nc.vector.tensor_tensor(t1[:], t1[:], down_row[:, at], ALU.mult))
                    step(nc.vector.tensor_copy(down_hi[:, at], t1[:]))
                    nc.vector.tensor_tensor(down_lo[:, at], t1[:], down_hi[:, at], ALU.subtract).then_inc(decoded, 1)
                dve.wait_ge(decoded, n + 1)
            inverse(0, RV, var_root, var_recip)
            modulate(0)
            split_low(0, 0)
            blocks(dve, iteration)
            hidden(NB - 1, I_T - 1)
            copy_y(NB - 1)
            inverse(NB - 1, RY, y_root, y_recip)
            norm_y(NB - 1)
            result(NB - 1)


def kernel(L0_attn_x, L0_attn_w_qkv, L0_attn_w_swiglu, L0_attn_w_out, L0_ffn_gate_up_packed,
           L0_ffn_gate_up_scales, L0_ffn_down_packed, L0_ffn_down_scales, L0_c, L0_wmod):
    import numpy as np
    import concourse.bacc as bacc
    from concourse.bass_utils import run_bass_kernel_spmd

    def groups(words):
        out, n = words.shape
        return words.T.reshape(n // 16, 16, out).transpose(1, 0, 2).reshape(16, -1)

    gus, dns = np.asarray(L0_ffn_gate_up_scales), np.asarray(L0_ffn_down_scales)
    arrays = {
        "xT": np.asarray(L0_attn_x)[0].T,
        "wqkvT": np.asarray(L0_attn_w_qkv).T,
        "wswT": np.asarray(L0_attn_w_swiglu).T,
        "woutT": np.asarray(L0_attn_w_out).T,
        "packed": np.concatenate([groups(np.asarray(L0_ffn_gate_up_packed)), groups(np.asarray(L0_ffn_down_packed))], axis=1),
        "gu_scales": gus.reshape(gus.shape[0], -1, P).transpose(2, 1, 0),
        "down_scales": dns.reshape(1, -1),
        "c_col": np.asarray(L0_c).reshape(-1, P).T,
        "wmod": np.asarray(L0_wmod),
    }
    arrays = {name: np.ascontiguousarray(a) for name, a in arrays.items()}
    nc = bacc.Bacc("TRN2", target_bir_lowering=False, num_devices=1)
    args = [nc.dram_tensor(name, a.shape, mybir.dt.from_np(a.dtype), kind="ExternalInput").ap() for name, a in arrays.items()]
    D, S = arrays["xT"].shape
    outT = nc.dram_tensor("outT", (D, S), F32, kind="ExternalOutput").ap()
    program(nc, *args, outT)
    r = run_bass_kernel_spmd(nc, [arrays], core_ids=[0])
    return np.ascontiguousarray(r.results[0]["outT"].T)[None]
```

```python
from contextlib import ExitStack

import concourse.bass as bass
from concourse import mybir

ALU = mybir.AluOpType
ACT = mybir.ActivationFunctionType
F32 = mybir.dt.float32
F16 = mybir.dt.float16
BF16 = mybir.dt.bfloat16
I32 = mybir.dt.int32

P = 128


def program(nc, xT, wqkvT, wswT, woutT, packed, gu_scales, down_scales, c_col, wmod, outT):
    D, S = xT.shape
    T = 512
    NB = S // T
    DT = D // P
    FT = woutT.shape[0] // P
    I_T = gu_scales.shape[1] // 2
    GU = DT * 2 * I_T * P
    QKV = 3 * DT
    DOWN = I_T * D
    LN_EPS, RMS_EPS, CUM_EPS, FFN_EPS = 1e-5, 1.1920929e-07, 1e-6, 1e-6

    xT_t = xT.rearrange("(c p) s -> p c s", p=P)
    outT_t = outT.rearrange("(c p) s -> p c s", p=P)
    h_dram = nc.dram_tensor("h_scratch", [D, S], F32, kind="Internal").ap()
    x1_dram = nc.dram_tensor("x1_scratch", [D, S], F32, kind="Internal").ap()
    h_t = h_dram.rearrange("(c p) s -> p c s", p=P)
    x1_t = x1_dram.rearrange("(c p) s -> p c s", p=P)
    gu_dram = nc.dram_tensor("gu_scratch", [P, GU], BF16, kind="Internal").ap()
    down_hi_dram = nc.dram_tensor("down_hi_scratch", [P, DOWN], F16, kind="Internal").ap()
    down_lo_dram = nc.dram_tensor("down_lo_scratch", [P, DOWN], BF16, kind="Internal").ap()

    whole = ExitStack()
    with whole:
        def sem(name):
            return whole.enter_context(nc.semaphore(name))

        def keep(name, shape, dt):
            return whole.enter_context(nc.sbuf_tensor(name, shape, dt))

        mod = keep("mod", [P, 24], F32)
        ones = keep("ones", [P, P], F32)
        eps = keep("eps", [P, 3], F32)
        bank = [whole.enter_context(nc.psum_tensor(f"bank{i}", [P, T], F32)) for i in range(8)]
        SA, CA, GA, SB, CB, GB = (slice(DT * i, DT * i + DT) for i in range(6))

        mixer(nc, locals())
        ffn(nc, locals())


def counts(eng, *values):
    for n in values:
        if not isinstance(n, int):
            eng.compute_val(n)
    return values


def mixer(nc, v):
    P_, T, NB, DT, FT, QKV, S = P, v["T"], v["NB"], v["DT"], v["FT"], v["QKV"], v["S"]
    mod, ones, eps, bank = v["mod"], v["ones"], v["eps"], v["bank"]
    SA, CA, GA = v["SA"], v["CA"], v["GA"]
    GB = v["GB"]
    xT_t, h_t, x1_t = v["xT_t"], v["h_t"], v["x1_t"]
    GU, DOWN = v["GU"], v["DOWN"]
    CUM_EPS = v["CUM_EPS"]
    GU_CHUNKS, DOWN_CHUNKS = 4, 2
    CHUNKS = GU_CHUNKS + DOWN_CHUNKS
    CH = GU // (NB * GU_CHUNKS)
    assert CH * NB * GU_CHUNKS == GU and CH * NB * DOWN_CHUNKS == DOWN
    with ExitStack() as ctx:
        def sb(name, shape, dt):
            return ctx.enter_context(nc.sbuf_tensor(name, shape, dt))

        def sem(name):
            return v["sem"]("a_" + name)

        wqkv = sb("wqkv", [P, 2, DT, QKV * P], F16)
        wsw = sb("wsw", [P, 2, DT, 2 * FT * P], F16)
        wout = sb("wout", [P, 2, FT, DT * P], F16)
        X = sb("X", [P, DT, T], F32)
        H = sb("H", [P, 2, DT, T], F16)
        K = sb("K", [P, DT, T], F32)
        V = sb("V", [P, DT, T], F32)
        Q = sb("Q", [P, DT, T], F32)
        Y = sb("Y", [P, 2, DT, T], F16)
        SQ = sb("SQ", [P, 2, T], F32)
        RS = sb("RS", [P, T], F32)
        RD = sb("RD", [P, 2, T], F32)
        late = sb("late", [P, 4 * T], F32)
        UG = late[:, 0:2 * T].bitcast(F16).rearrange("p (b h t) -> p b h t", b=2, h=2)
        G = late[:, 2 * T:3 * T]
        XR = late[:, 3 * T:4 * T]
        HR = sb("HR", [P, T], F32)
        run = sb("run", [P, T], BF16)
        carry = sb("carry", [P, 2, DT], F32)
        cc = sb("cc", [P, 2, DT], F32)
        gtmp = sb("gtmp", [P, 3, 2 * DT], F32)
        U_BANK, G_BANK, R_BANK, O_BANK = bank[0], bank[1], bank[2:4], bank[4:8]
        MEAN, VAR, HSQ, KSQ, QSQ = range(5)
        SLOT = [0, 1, 0, 1, 0]
        WAVE = {VAR: 0, HSQ: 1, KSQ: 2, QSQ: 3}

        word = sb("word", [P, 2, CH], I32)
        row = sb("row", [P, 2, CH], F16)
        low3 = sb("low3", [P, CH], I32)
        bit3 = sb("bit3", [P, CH], I32)
        t1 = sb("t1", [P, CH], F32)
        t2 = sb("t2", [P, CH], F32)
        val = sb("val", [P, CH], BF16)
        val_hi = sb("val_hi", [P, CH], F16)
        lane = sb("lane", [P, 1], I32)
        shift = sb("shift", [P, 1], I32)
        const_ready = sem("const_ready")
        c_loaded = sem("c_loaded")
        wmod_loaded = sem("wmod_loaded")
        c_silu = sem("c_silu")
        mod_summed = sem("mod_summed")
        mod_copied = sem("mod_copied")
        mod_step = sem("mod_step")
        mod_ready = sem("mod_ready")
        scale_loaded = sem("scale_loaded")
        w_loaded = [sem(f"w_loaded{i}") for i in range(5)]
        w_high = sem("w_high")
        w_high_pool = sem("w_high_pool")
        w_low = sem("w_low")
        x_loaded = sem("x_loaded")
        tile_sum = sem("tile_sum")
        squared = sem("squared")
        sq_sum = sem("sq_sum")
        reduced = sem("reduced")
        centred = sem("centred")
        root = sem("root")
        recip = sem("recip")
        scaled = sem("scaled")
        h_ready = sem("h_ready")
        h_stored = sem("h_stored")
        hn_ready = sem("hn_ready")
        H_high = sem("H_high")
        H_low = sem("H_low")
        qkv_done = sem("qkv_done")
        qkv_out = sem("qkv_out")
        k_norm = sem("k_norm")
        q_norm = sem("q_norm")
        k_exp = sem("k_exp")
        wv_ready = sem("wv_ready")
        k_run = sem("k_run")
        v_run = sem("v_run")
        k_carry = sem("k_carry")
        v_carry = sem("v_carry")
        k_eps = sem("k_eps")
        q_exp = sem("q_exp")
        denominator = sem("denominator")
        inverted = sem("inverted")
        lane_ready, shift_ready = sem("lane_ready"), sem("shift_ready")
        words_loaded = [sem("words_loaded0"), sem("words_loaded1")]
        rows_loaded = sem("rows_loaded")
        words_used = sem("words_used")
        low_bits = sem("low_bits")
        decode = [sem(f"decode{i}") for i in range(6)]
        decoded = sem("decoded")
        part_stored = sem("part_stored")
        y_ready = sem("y_ready")
        Y_high = sem("Y_high")
        Y_low = sem("Y_low")
        u_done = sem("u_done")
        g_done = sem("g_done")
        g_silu = sem("g_silu")
        ug_ready = sem("ug_ready")
        UG_high = sem("UG_high")
        UG_low = sem("UG_low")
        out_used = sem("out_used")
        res_loaded = sem("res_loaded")
        res_sum = sem("res_sum")
        x1_ready = sem("x1_ready")
        x1_stored = sem("x1_stored")

        def tok(b):
            return bass.ds(b * T, T)

        wq_src = v["wqkvT"].rearrange("(c p) n -> p c n", p=P)
        ws_src = v["wswT"].rearrange("(c p) n -> p c n", p=P)
        wo_src = v["woutT"].rearrange("(c p) n -> p c n", p=P)
        pieces = [(wqkv[:, :, :, n * T:(n + 1) * T], wq_src[:, :, n * T:(n + 1) * T]) for n in range(QKV * P // T)]
        pieces += [(wsw[:, :, :, n * T:(n + 1) * T], ws_src[:, :, n * T:(n + 1) * T]) for n in range(2 * FT * P // T)]
        pieces += [(wout[:, :, n * DT:(n + 1) * DT, :], wo_src[:, n * DT:(n + 1) * DT, :]) for n in range(FT // DT)]
        NQ = QKV * P // T
        STAGES = [K[:], V[:], Q[:], Y[:].rearrange("p a c t -> p (a c t)").bitcast(F32).rearrange("p (c t) -> p c t", t=T),
                  late[:].rearrange("p (c t) -> p c t", t=T)]

        def stage_of(n):
            return n if n < NQ else NQ + (n - NQ) % 2

        def stage_uses(n):
            return sum(1 for m in range(n + 1) if stage_of(m) == stage_of(n))

        wmod_t = v["wmod"].rearrange("(k p) n -> p k n", p=P)
        wmod_sb = [wsw[:, 1, :, :].rearrange("p c n -> p (c n)").bitcast(F32),
                   wout[:].rearrange("p h c n -> p (h c n)").bitcast(F32)]
        HALF = 3 * DT * P
        assert DT * HALF <= DT * FT * P
        n_wout = len(pieces) - FT // DT

        block = ctx.enter_context(nc.Block())

        @block.sync
        def _(sp):
            def load_x(b):
                if not (isinstance(b, int) and b == 0):
                    sp.wait_ge(H_low, DT * b)
                sp.dma_start(X[:], xT_t[:, :, tok(b)]).then_inc(x_loaded, 16)

            def store_h(b):
                sp.wait_ge(h_ready, DT * (b + 1))
                sp.dma_start(h_t[:, :, tok(b)], X[:]).then_inc(h_stored, 16)

            def residual(b):
                stored, free, ready = counts(sp, 16 * (b + 1), 16 * DT * b, DT * b + 1)
                sp.wait_ge(h_stored, stored)
                for c in range(DT):
                    if c:
                        free, ready = counts(sp, 16 * (DT * b + c), DT * b + c + 1)
                    sp.wait_ge(x1_stored, free)
                    sp.dma_start(XR, xT_t[:, c, tok(b)]).then_inc(res_loaded, 16)
                    sp.dma_start(HR[:], h_t[:, c, tok(b)]).then_inc(res_loaded, 16)
                    sp.wait_ge(x1_ready, ready)
                    sp.dma_start(x1_t[:, c, tok(b)], XR).then_inc(x1_stored, 16)

            def load_words(b, k):
                at = (GU_CHUNKS * b + k) * CH if k < GU_CHUNKS else GU + (DOWN_CHUNKS * b + k - GU_CHUNKS) * CH
                if k >= GU_CHUNKS:
                    counts(sp, (DOWN_CHUNKS * b + k - GU_CHUNKS) * CH * 2)
                if k >= 2:
                    sp.wait_ge(words_used, CHUNKS * b + k - 1)
                elif not (isinstance(b, int) and b == 0):
                    sp.wait_ge(words_used, CHUNKS * b)
                sp.dma_start(word[:, k % 2, :], v["packed"][:, bass.ds(at, CH)]).then_inc(words_loaded[k % 2], 16)
                if k >= GU_CHUNKS:
                    if not (isinstance(b, int) and b == 0):
                        sp.wait_ge(decoded, CHUNKS * b)
                    sp.dma_start(row[:, k - GU_CHUNKS, :],
                                 v["down_scales"][:, bass.ds((DOWN_CHUNKS * b + k - GU_CHUNKS) * CH, CH)].to_broadcast([P, CH])
                                 ).then_inc(rows_loaded, 16)

            def store_values(b, k):
                at = (GU_CHUNKS * b + k) * CH if k < GU_CHUNKS else (DOWN_CHUNKS * b + k - GU_CHUNKS) * CH
                counts(sp, at * 2)
                sp.wait_ge(decoded, CHUNKS * b + k + 1)
                at = bass.ds(at, CH)
                if k < GU_CHUNKS:
                    sp.dma_start(v["gu_dram"][:, at], val[:]).then_inc(part_stored, 16)
                else:
                    sp.dma_start(v["down_hi_dram"][:, at], val_hi[:]).then_inc(part_stored, 16)
                    sp.dma_start(v["down_lo_dram"][:, at], val[:]).then_inc(part_stored, 16)

            def load_piece(n):
                if n >= NQ + 2:
                    sp.wait_ge(w_low, n - 1)
                if n == n_wout:
                    sp.wait_ge(mod_summed, 2)
                sp.dma_start(STAGES[stage_of(n)], pieces[n][1]).then_inc(w_loaded[stage_of(n)], 16)

            def load_wmod(half):
                for k in range(DT):
                    sp.dma_start(wmod_sb[half][:, k * HALF:(k + 1) * HALF],
                                 wmod_t[:, k, half * HALF:(half + 1) * HALF]).then_inc(wmod_loaded, 16)

            sp.dma_start(cc[:, 0, :], v["c_col"]).then_inc(c_loaded, 16)
            load_x(0)
            load_wmod(0)
            for n in range(NQ + 2):
                load_piece(n)
            store_h(0)
            load_x(1)
            load_wmod(1)
            for n in range(NQ + 2, n_wout):
                load_piece(n)
            load_piece(n_wout)
            store_h(1)
            for n in range(n_wout + 1, len(pieces)):
                load_piece(n)

            def iteration(b, s1):
                load_words(b, 0)
                load_words(b, 1)
                if s1:
                    load_x(b + 2)
                store_values(b, 0)
                load_words(b, 2)
                store_values(b, 1)
                load_words(b, 3)
                if s1:
                    store_h(b + 2)
                for k in range(2, CHUNKS):
                    store_values(b, k)
                    if k + 2 < CHUNKS:
                        load_words(b, k + 2)
                residual(b)

            iteration(0, True)
            with sp.Fori(1, NB - 2) as b:
                iteration(b, True)
            iteration(NB - 2, False)
            iteration(NB - 1, False)
            sp.wait_ge(h_stored, 16 * NB)
            sp.wait_ge(x1_stored, 16 * DT * NB)
            sp.wait_ge(part_stored, 16 * (CHUNKS + DOWN_CHUNKS) * NB)

        @block.tensor
        def _(pe):
            def reduce(kind, b):
                slot = SLOT[kind]
                if kind == MEAN:
                    pe.wait_ge(tile_sum, 3 * (b + 1))
                else:
                    pe.wait_ge(sq_sum, 3 * (4 * b + WAVE[kind] + 1))
                if kind in (HSQ,):
                    pe.wait_ge(centred, DT * (b + 1))
                elif kind == QSQ:
                    pe.wait_ge(root, 4 * b + 2)
                elif kind == KSQ:
                    pe.wait_ge(root, 4 * b + 1)
                elif not (isinstance(b, int) and b == 0):
                    pe.wait_ge(root, 4 * b)
                nc.tensor.matmul(R_BANK[slot][:], ones[:], RS[:], start=True, stop=True).then_inc(reduced, 1)

            def three_pass(out, w, x, kt, last_kt, first=0):
                for k in range(kt):
                    for pw, px in ((0, 0), (1, 0), (0, 1)):
                        mm = nc.tensor.matmul(out, w(pw, k), x(px, k), start=(k == 0 and pw == 0 and px == 0),
                                              stop=(k == kt - 1 and px == 1))
                return mm

            def qkv(b):
                pe.wait_ge(H_high, DT * (b + 1))
                pe.wait_ge(H_low, DT * (b + 1))
                n = 0
                for part in (1, 0, 2):
                    for c in range(DT):
                        out = bank[n % 2]
                        col = (part * DT + c) * P
                        if n >= 2:
                            pe.wait_ge(qkv_out, QKV * b + n - 1)
                        elif not (isinstance(b, int) and b == 0):
                            if not (isinstance(b, int) and b == 1):
                                pe.wait_ge((ug_ready, g_silu)[n], FT * (b - 1))
                            pe.wait_ge(qkv_out, QKV * b)
                        three_pass(out[:], lambda pw, k: wqkv[:, pw, k, col:col + P],
                                   lambda px, k: H[:, px, k, :], DT, 0).then_inc(qkv_done, 1)
                        n += 1
                    if part == 0:
                        reduce(KSQ, b)
                reduce(QSQ, b)

            def output(b, j):
                pe.wait_ge(UG_high, FT * b + j + 1)
                pe.wait_ge(UG_low, FT * b + j + 1)
                if j == 0 and not (isinstance(b, int) and b == 0):
                    pe.wait_ge(res_sum, DT * b)
                for c in range(DT):
                    for pw, px in ((0, 0), (1, 0), (0, 1)):
                        mm = nc.tensor.matmul(O_BANK[c][:], wout[:, pw, j, c * P:(c + 1) * P], UG[:, j % 2, px, :],
                                              start=(j == 0 and pw == 0 and px == 0), stop=(j == FT - 1 and px == 1))
                mm.then_inc(out_used, 1)

            def swiglu(b, s2, s1):
                pe.wait_ge(Y_high, DT * (b + 1))
                pe.wait_ge(Y_low, DT * (b + 1))
                for j in range(FT):
                    for which, out, done, read in ((1, G_BANK, g_done, g_silu), (0, U_BANK, u_done, ug_ready)):
                        if j == 0:
                            if not (isinstance(b, int) and b == 0):
                                pe.wait_ge(read, FT * b)
                            pe.wait_ge(qkv_out, QKV * (b + 2 if s2 else b + 1))
                        else:
                            pe.wait_ge(read, FT * b + j)
                        col = (which * FT + j) * P
                        three_pass(out[:], lambda pw, k: wsw[:, pw, k, col:col + P],
                                   lambda px, k: Y[:, px, k, :], DT, 0).then_inc(done, 1)
                    if s1 and j in (1, 5, 10):
                        reduce({1: MEAN, 5: VAR, 10: HSQ}[j], b + 2)
                    if j:
                        output(b, j - 1)
                output(b, FT - 1)

            def iteration(b, s2, s1):
                if s2:
                    qkv(b + 1)
                swiglu(b, s2, s1)

            pe.wait_ge(const_ready, 1)
            pe.wait_ge(c_silu, 1)

            def modulation(half):
                pe.wait_ge(wmod_loaded, 16 * DT * (half + 1))
                for n in range(3 * DT):
                    for k in range(DT):
                        mm = nc.tensor.matmul(bank[4 + half][:, n:n + 1],
                                              wmod_sb[half][:, k * HALF + n * P:k * HALF + (n + 1) * P],
                                              cc[:, 1, k:k + 1], start=(k == 0), stop=(k == DT - 1))
                mm.then_inc(mod_summed, 1)

            reduce(MEAN, 0)
            modulation(0)
            reduce(VAR, 0)
            reduce(HSQ, 0)
            pe.wait_ge(w_low, NQ)
            pe.wait_ge(w_high, NQ)
            qkv(0)
            modulation(1)
            for kind in (MEAN, VAR, HSQ):
                reduce(kind, 1)
            pe.wait_ge(w_low, len(pieces))
            pe.wait_ge(w_high_pool, len(pieces) - NQ)
            iteration(0, True, True)
            with pe.Fori(1, NB - 2) as b:
                iteration(b, True, True)
            iteration(NB - 2, True, False)
            iteration(NB - 1, False, False)

        @block.scalar
        def _(act):
            def square(kind, b, src, ready, per, c0=0):
                use = 4 * b + WAVE[kind]
                for c in range(DT):
                    act.wait_ge(ready, per * b + c0 + c + 1)
                    if c >= 2:
                        act.wait_ge(sq_sum, 3 * use + 1)
                    elif not (isinstance(b, int) and b == 0 and kind == VAR):
                        act.wait_ge(sq_sum, 3 * use - 1 + c)
                    nc.scalar.activation(SQ[:, c % 2, :], src[:, c, :], ACT.Square).then_inc(squared, 1)

            def sqrt(kind, b):
                slot = SLOT[kind]
                use = 4 * b + WAVE[kind]
                act.wait_ge(reduced, 5 * b + kind + 1)
                if kind == VAR:
                    if not (isinstance(b, int) and b == 0):
                        act.wait_ge(k_norm, DT * b)
                elif kind == HSQ:
                    if not (isinstance(b, int) and b == 0):
                        act.wait_ge(q_norm, DT * b)
                elif kind == KSQ:
                    act.wait_ge(scaled, DT * (b + 1))
                else:
                    act.wait_ge(hn_ready, DT * (b + 1))
                nc.scalar.activation(RD[:, slot, :], R_BANK[slot][:], ACT.Sqrt,
                                     bias=eps[:, (0 if kind == VAR else 1):(1 if kind == VAR else 2)]).then_inc(root, 1)

            def s1_var(b):
                square(VAR, b, X, centred, DT)

            def s1_h(b):
                square(HSQ, b, X, h_ready, DT)

            def s1_split(b):
                for c in range(DT):
                    act.wait_ge(hn_ready, DT * b + c + 1)
                    if c == 0 and not (isinstance(b, int) and b == 0):
                        act.wait_ge(qkv_done, QKV * b)
                    nc.scalar.activation(H[:, 0, c, :], X[:, c, :], ACT.Copy).then_inc(H_high, 1)

            def copy_out(b, n, dst):
                act.wait_ge(qkv_done, QKV * b + n + 1)
                nc.scalar.activation(dst[:, n % DT, :], bank[n % 2][:], ACT.Copy).then_inc(qkv_out, 1)

            def s2_copies(b):
                if isinstance(b, int) and b == 0:
                    act.wait_ge(w_low, NQ)
                else:
                    act.wait_ge(Y_low, DT * b)
                    act.wait_ge(Y_high, DT * b)
                    act.wait_ge(k_carry, DT * b)
                    act.wait_ge(v_carry, DT * b)
                for c in range(DT):
                    copy_out(b, c, K)
                square(KSQ, b, K, qkv_out, QKV)
                for c in range(DT):
                    copy_out(b, DT + c, Q)
                copy_out(b, 2 * DT, V)
                square(QSQ, b, Q, qkv_out, QKV, c0=DT)
                for c in range(1, DT):
                    copy_out(b, 2 * DT + c, V)

            def s2_exp(b):
                for c in range(DT):
                    act.wait_ge(k_norm, DT * b + c + 1)
                    nc.scalar.activation(K[:, c, :], K[:, c, :], ACT.Exp).then_inc(k_exp, 1)

            def s2_exp_q(b):
                for c in range(DT):
                    act.wait_ge(q_norm, DT * b + c + 1)
                    nc.scalar.activation(Q[:, c, :], Q[:, c, :], ACT.Exp, scale=-1.0).then_inc(q_exp, 1)

            def s2_split(b):
                if not (isinstance(b, int) and b == 0):
                    act.wait_ge(u_done, FT * b)
                else:
                    act.wait_ge(w_low, len(pieces))
                for c in range(DT):
                    act.wait_ge(y_ready, DT * b + c + 1)
                    nc.scalar.activation(Y[:, 0, c, :], V[:, c, :], ACT.Copy).then_inc(Y_high, 1)

            def silu(b, j):
                act.wait_ge(g_done, FT * b + j + 1)
                if not (isinstance(b, int) and b == 0 and j == 0):
                    act.wait_ge(UG_low, FT * b + j)
                nc.scalar.activation(G, G_BANK[:], ACT.Silu).then_inc(g_silu, 1)

            def high(b, j):
                act.wait_ge(ug_ready, FT * b + j + 1)
                if j >= 2:
                    act.wait_ge(out_used, FT * b + j - 1)
                elif not (isinstance(b, int) and b == 0):
                    act.wait_ge(out_used, FT * b)
                nc.scalar.activation(UG[:, j % 2, 0, :], G, ACT.Copy).then_inc(UG_high, 1)

            def iteration(b, s2, s1):
                if s2:
                    s2_copies(b + 1)
                    sqrt(KSQ, b + 1)
                    sqrt(QSQ, b + 1)
                for j in range(FT):
                    silu(b, j)
                    if s2 and j == 1:
                        s2_exp(b + 1)
                    if s2 and j == 3:
                        s2_exp_q(b + 1)
                    if s1 and j == 4:
                        s1_var(b + 2)
                    if s1 and j == 6:
                        sqrt(VAR, b + 2)
                    if s1 and j == 9:
                        s1_h(b + 2)
                    if s1 and j == 11:
                        sqrt(HSQ, b + 2)
                    high(b, j)
                    if s1 and j == 14:
                        s1_split(b + 2)
                if s2:
                    s2_split(b + 1)

            def split(n):
                act.wait_ge(w_loaded[n], 16)
                nc.scalar.activation(pieces[n][0][:, 0], STAGES[n], ACT.Copy).then_inc(w_high, 1)

            act.wait_ge(c_loaded, 16)
            nc.scalar.activation(cc[:, 1, :], cc[:, 0, :], ACT.Silu).then_inc(c_silu, 1)
            act.wait_ge(const_ready, 1)
            s1_var(0)
            split(0)
            sqrt(VAR, 0)
            split(1)
            s1_h(0)
            split(2)
            sqrt(HSQ, 0)
            s1_split(0)
            s2_copies(0)
            sqrt(KSQ, 0)
            sqrt(QSQ, 0)
            s2_exp(0)
            s1_var(1)
            s2_exp_q(0)
            sqrt(VAR, 1)
            s1_h(1)
            sqrt(HSQ, 1)
            s1_split(1)
            s2_split(0)
            iteration(0, True, True)
            with act.Fori(1, NB - 2) as b:
                iteration(b, True, True)
            iteration(NB - 2, True, False)
            iteration(NB - 1, False, False)

        @block.gpsimd
        def _(pool):
            def add_squares(kind, b):
                use = 4 * b + WAVE[kind]
                pool.wait_ge(reduced, 5 * b + kind)
                pool.wait_ge(squared, DT * use + 2)
                nc.gpsimd.tensor_tensor(RS[:], SQ[:, 0, :], SQ[:, 1, :], ALU.add).then_inc(sq_sum, 1)
                for c in range(2, DT):
                    pool.wait_ge(squared, DT * use + c + 1)
                    pool.wait_ge(sq_sum, 3 * use + c - 1)
                    nc.gpsimd.tensor_tensor(RS[:], RS[:], SQ[:, c % 2, :], ALU.add).then_inc(sq_sum, 1)

            def add_x(b):
                pool.wait_ge(x_loaded, 16 * (b + 1))
                if not (isinstance(b, int) and b == 0):
                    pool.wait_ge(reduced, 5 * b)
                nc.gpsimd.tensor_tensor(RS[:], X[:, 0, :], X[:, 1, :], ALU.add).then_inc(tile_sum, 1)
                for c in range(2, DT):
                    pool.wait_ge(tile_sum, 3 * b + c - 1)
                    nc.gpsimd.tensor_tensor(RS[:], RS[:], X[:, c, :], ALU.add).then_inc(tile_sum, 1)

            def weigh(b):
                for c in range(DT):
                    pool.wait_ge(k_exp, DT * b + c + 1)
                    pool.wait_ge(qkv_out, QKV * (b + 1))
                    nc.gpsimd.tensor_tensor(V[:, c, :], K[:, c, :], V[:, c, :], ALU.mult).then_inc(wv_ready, 1)

            def low(b, j):
                pool.wait_ge(UG_high, FT * b + j + 1)
                nc.gpsimd.tensor_tensor(UG[:, j % 2, 1, :], G, UG[:, j % 2, 0, :], ALU.subtract).then_inc(UG_low, 1)

            def iteration(b, s2, s1):
                if s2:
                    add_squares(KSQ, b + 1)
                    add_squares(QSQ, b + 1)
                for j in range(FT):
                    if s1 and j == 4:
                        add_squares(VAR, b + 2)
                    if s1 and j == 9:
                        add_squares(HSQ, b + 2)
                    low(b, j)
                    if s1 and j == 0:
                        add_x(b + 2)
                    if s2 and j == 2:
                        weigh(b + 1)

            def split(n):
                pool.wait_ge(w_loaded[stage_of(n)], 16 * stage_uses(n))
                if n == NQ:
                    pool.wait_ge(mod_summed, 1)
                nc.gpsimd.tensor_copy(pieces[n][0][:, 0], STAGES[stage_of(n)]).then_inc(w_high_pool, 1)

            nc.gpsimd.iota(lane[:], pattern=[[0, 1]], base=0, channel_multiplier=1).then_inc(lane_ready, 1)
            add_x(0)
            add_squares(VAR, 0)
            add_squares(HSQ, 0)
            for n in range(NQ, NQ + 3):
                split(n)
            add_squares(KSQ, 0)
            split(NQ + 3)
            split(NQ + 4)
            add_squares(QSQ, 0)
            split(NQ + 5)
            add_x(1)
            split(NQ + 6)
            weigh(0)
            split(NQ + 7)
            add_squares(VAR, 1)
            split(NQ + 8)
            add_squares(HSQ, 1)
            for n in range(NQ + 9, len(pieces)):
                split(n)
            iteration(0, True, True)
            with pool.Fori(1, NB - 2) as b:
                iteration(b, True, True)
            iteration(NB - 2, True, False)
            iteration(NB - 1, False, False)

        @block.vector
        def _(dve):
            def inverse(kind, b):
                n = 4 * b + WAVE[kind] + 1
                dve.wait_ge(root, n)
                nc.vector.reciprocal(RD[:, SLOT[kind], :], RD[:, SLOT[kind], :]).then_inc(recip, 1)
                dve.wait_ge(recip, n)

            def times(dst, a, b_, done):
                nc.vector.tensor_tensor(dst, a, b_, ALU.mult).then_inc(done, 1)

            def s1_centre(b):
                dve.wait_ge(reduced, 5 * b + MEAN + 1)
                for c in range(DT):
                    nc.vector.tensor_tensor(X[:, c, :], X[:, c, :], R_BANK[SLOT[MEAN]][:], ALU.subtract).then_inc(centred, 1)

            def s1_modulate(b):
                dve.wait_ge(squared, DT * (4 * b + WAVE[VAR] + 1))
                for c in range(DT):
                    times(X[:, c, :], X[:, c, :], RD[:, SLOT[VAR], :], scaled)
                for c in range(DT):
                    dve.wait_ge(scaled, DT * b + c + 1)
                    nc.vector.tensor_scalar(X[:, c, :], X[:, c, :], mod[:, CA][:, c:c + 1], mod[:, SA][:, c:c + 1],
                                            ALU.mult, ALU.add).then_inc(h_ready, 1)

            def s1_norm(b):
                dve.wait_ge(h_stored, 16 * (b + 1))
                dve.wait_ge(squared, DT * (4 * b + WAVE[HSQ] + 1))
                for c in range(DT):
                    times(X[:, c, :], X[:, c, :], RD[:, SLOT[HSQ], :], hn_ready)

            def s1_low(b):
                for c in range(DT):
                    dve.wait_ge(H_high, DT * b + c + 1)
                    nc.vector.tensor_tensor(H[:, 1, c, :], X[:, c, :], H[:, 0, c, :], ALU.subtract).then_inc(H_low, 1)

            def s2_norm_k(b):
                for c in range(DT):
                    times(K[:, c, :], K[:, c, :], RD[:, SLOT[KSQ], :], k_norm)

            def s2_norm_q(b):
                for c in range(DT):
                    times(Q[:, c, :], Q[:, c, :], RD[:, SLOT[QSQ], :], q_norm)

            def scan(b, buf, which, ready, done, copied):
                for c in range(DT):
                    dve.wait_ge(ready, DT * b + c + 1)
                    dve.wait_ge(wv_ready, DT * b + c + 1)
                    if not (isinstance(b, int) and b == 0):
                        dve.wait_ge(copied, DT * b)
                    first = isinstance(b, int) and b == 0
                    nc.vector.tensor_tensor_scan(buf[:, c, :], run[:], buf[:, c, :],
                                                 0.0 if first else carry[:, which, c:c + 1],
                                                 ALU.mult, ALU.add).then_inc(done, 1)

            def keep_last(b, buf, which, done, copied):
                for c in range(DT):
                    dve.wait_ge(done, DT * b + c + 1)
                    nc.vector.tensor_copy(carry[:, which, c:c + 1], buf[:, c, T - 1:T]).then_inc(copied, 1)

            def s2_denominator(b):
                for c in range(DT):
                    dve.wait_ge(k_carry, DT * b + c + 1)
                    nc.vector.tensor_scalar(K[:, c, :], K[:, c, :], CUM_EPS, None, ALU.add).then_inc(k_eps, 1)
                for c in range(DT):
                    dve.wait_ge(k_eps, DT * b + c + 1)
                    dve.wait_ge(q_exp, DT * b + c + 1)
                    nc.vector.scalar_tensor_tensor(K[:, c, :], Q[:, c, :], 1.0, K[:, c, :],
                                                   ALU.add, ALU.mult).then_inc(denominator, 1)

            def s2_invert(b, c):
                dve.wait_ge(denominator, DT * b + c + 1)
                nc.vector.reciprocal(K[:, c, :], K[:, c, :]).then_inc(inverted, 1)

            def s2_y(b):
                for c in range(DT):
                    dve.wait_ge(inverted, DT * b + c + 1)
                    dve.wait_ge(v_carry, DT * b + c + 1)
                    times(V[:, c, :], V[:, c, :], K[:, c, :], y_ready)

            def s2_low(b):
                for c in range(DT):
                    dve.wait_ge(Y_high, DT * b + c + 1)
                    nc.vector.tensor_tensor(Y[:, 1, c, :], V[:, c, :], Y[:, 0, c, :], ALU.subtract).then_inc(Y_low, 1)

            def hidden(b, j):
                dve.wait_ge(u_done, FT * b + j + 1)
                dve.wait_ge(g_silu, FT * b + j + 1)
                times(G, G, U_BANK[:], ug_ready)

            def residual(b):
                dve.wait_ge(out_used, FT * (b + 1))
                for c in range(DT):
                    n = DT * b + c
                    dve.wait_ge(res_loaded, 32 * (n + 1))
                    nc.vector.tensor_tensor(HR[:], HR[:], O_BANK[c][:], ALU.add).then_inc(res_sum, 1)
                    dve.wait_ge(res_sum, n + 1)
                    nc.vector.scalar_tensor_tensor(XR, HR[:], mod[:, GA][:, c:c + 1], XR,
                                                   ALU.mult, ALU.add).then_inc(x1_ready, 1)

            def decode_chunk(b, k):
                n = CHUNKS * b + k + 1
                dve.wait_ge(words_loaded[k % 2], 16 * (CHUNKS // 2 * b + k // 2 + 1))
                w = word[:, k % 2, :]
                nc.vector.tensor_scalar(low3[:], w, shift[:, 0:1], 7, ALU.logical_shift_right, ALU.bitwise_and).then_inc(low_bits, 1)
                nc.vector.tensor_scalar(bit3[:], w, shift[:, 0:1], 8, ALU.logical_shift_right, ALU.bitwise_and).then_inc(words_used, 1)
                dve.wait_ge(low_bits, n)
                nc.vector.scalar_tensor_tensor(t1[:], low3[:], 4.0, low3[:], ALU.max, ALU.add).then_inc(decode[0], 1)
                nc.vector.tensor_scalar(t2[:], low3[:], 6.0, 2.0, ALU.max, ALU.mult).then_inc(decode[1], 1)
                dve.wait_ge(decode[0], n)
                dve.wait_ge(decode[1], n)
                nc.vector.scalar_tensor_tensor(t1[:], t1[:], -16.0, t2[:], ALU.add, ALU.add).then_inc(decode[2], 1)
                dve.wait_ge(decode[2], n)
                dve.wait_ge(words_used, n)
                nc.vector.tensor_scalar(t2[:], bit3[:], -0.125, 0.5, ALU.mult, ALU.add).then_inc(decode[3], 1)
                dve.wait_ge(decode[3], n)
                stored = (CHUNKS + DOWN_CHUNKS) * b + k + max(k - GU_CHUNKS, 0)
                if not (isinstance(stored, int) and stored == 0):
                    dve.wait_ge(part_stored, 16 * stored)
                if k < GU_CHUNKS:
                    nc.vector.tensor_tensor(val[:], t1[:], t2[:], ALU.mult).then_inc(decoded, 1)
                else:
                    m = DOWN_CHUNKS * b + k - GU_CHUNKS + 1
                    nc.vector.tensor_tensor(t1[:], t1[:], t2[:], ALU.mult).then_inc(decode[4], 1)
                    dve.wait_ge(decode[4], 2 * m - 1)
                    dve.wait_ge(rows_loaded, 16 * m)
                    nc.vector.tensor_tensor(t1[:], t1[:], row[:, k - GU_CHUNKS, :], ALU.mult).then_inc(decode[4], 1)
                    dve.wait_ge(decode[4], 2 * m)
                    nc.vector.tensor_copy(val_hi[:], t1[:]).then_inc(decode[5], 1)
                    dve.wait_ge(decode[5], m)
                    nc.vector.tensor_tensor(val[:], t1[:], val_hi[:], ALU.subtract).then_inc(decoded, 1)
                dve.wait_ge(decoded, n)

            def iteration(b, s2, s1):
                if s2:
                    inverse(KSQ, b + 1)
                for j in range(FT):
                    hidden(b, j)
                    if s2:
                        n = b + 1
                        if j == 0:
                            s2_norm_k(n)
                        if j == 1:
                            inverse(QSQ, n)
                        if j == 2:
                            s2_norm_q(n)
                        if j == 3:
                            scan(n, K, 0, k_exp, k_run, k_carry)
                        if j == 4:
                            scan(n, V, 1, wv_ready, v_run, v_carry)
                        if j == 5:
                            keep_last(n, K, 0, k_run, k_carry)
                            keep_last(n, V, 1, v_run, v_carry)
                            s2_denominator(n)
                        if j in (6, 9, 10, 11):
                            s2_invert(n, (6, 9, 10, 11).index(j))
                        if j == 13:
                            s2_y(n)
                    if s1:
                        n = b + 2
                        if j == 2:
                            s1_centre(n)
                        if j == 7:
                            inverse(VAR, n)
                        if j == 8:
                            s1_modulate(n)
                        if j == 12:
                            inverse(HSQ, n)
                        if j == 13:
                            s1_norm(n)
                        if j == 15:
                            s1_low(n)
                    if j in (0, 6, 10, 11, 12, 14):
                        decode_chunk(b, (0, 6, 10, 11, 12, 14).index(j))
                if s2:
                    s2_low(b + 1)
                residual(b)

            def split(n):
                if n < NQ:
                    dve.wait_ge(w_high, n + 1)
                else:
                    dve.wait_ge(w_high_pool, n - NQ + 1)
                nc.vector.tensor_tensor(pieces[n][0][:, 1], STAGES[stage_of(n)], pieces[n][0][:, 0],
                                        ALU.subtract).then_inc(w_low, 1)

            dve.wait_ge(lane_ready, 1)
            nc.vector.tensor_scalar(lane[:], lane[:], 7, 2, ALU.bitwise_and, ALU.logical_shift_left).then_inc(shift_ready, 1)
            dve.wait_ge(shift_ready, 1)
            nc.vector.tensor_copy(shift[:], lane[:]).then_inc(shift_ready, 1)
            dve.wait_ge(shift_ready, 2)
            nc.vector.memset(ones[:], 1.0 / (DT * P)).then_inc(mod_step, 1)
            nc.vector.memset(eps[:, 0:1], v["LN_EPS"]).then_inc(mod_step, 1)
            nc.vector.memset(eps[:, 1:2], v["RMS_EPS"]).then_inc(mod_step, 1)
            nc.vector.memset(eps[:, 2:3], v["FFN_EPS"]).then_inc(mod_step, 1)
            nc.vector.memset(run[:], 1.0).then_inc(mod_step, 1)
            dve.wait_ge(mod_step, 5)
            nc.vector.memset(gtmp[:], 0.0).then_inc(const_ready, 1)

            def modulation(half):
                dve.wait_ge(mod_summed, half + 1)
                nc.vector.tensor_copy(mod[:, half * 3 * DT:(half + 1) * 3 * DT], bank[4 + half][:, 0:3 * DT]).then_inc(mod_copied, 1)
                dve.wait_ge(mod_copied, half + 1)
                cols = mod[:, (3 * half + 1) * DT:(3 * half + 2) * DT]
                gate = mod[:, (3 * half + 2) * DT:(3 * half + 3) * DT]
                n = 5 + 5 * half
                sign, size = gtmp[:, 0, 0:DT], gtmp[:, 1, 0:DT]
                nc.vector.tensor_scalar(cols, cols, 1.0, None, ALU.add).then_inc(mod_step, 1)
                nc.vector.tensor_scalar(sign, gate, 0.0, 2.0, ALU.is_ge, ALU.mult).then_inc(mod_step, 1)
                nc.vector.scalar_tensor_tensor(size, gate, -1.0, gate, ALU.mult, ALU.max).then_inc(mod_step, 1)
                dve.wait_ge(mod_step, n + 3)
                nc.vector.tensor_scalar(size, size, 0.25, None, ALU.max).then_inc(mod_step, 1)
                dve.wait_ge(mod_step, n + 4)
                nc.vector.scalar_tensor_tensor(gate, sign, -1.0, size, ALU.add, ALU.mult).then_inc(mod_step, 1)
                dve.wait_ge(mod_step, n + 5)
            s1_centre(0)
            modulation(0)
            split(0)
            inverse(VAR, 0)
            s1_modulate(0)
            split(1)
            split(2)
            inverse(HSQ, 0)
            s1_norm(0)
            s1_low(0)
            for n in range(NQ, NQ + 5):
                split(n)
            inverse(KSQ, 0)
            s2_norm_k(0)
            modulation(1)
            inverse(QSQ, 0)
            s2_norm_q(0)
            split(NQ + 5)
            s1_centre(1)
            scan(0, K, 0, k_exp, k_run, k_carry)
            split(NQ + 6)
            scan(0, V, 1, wv_ready, v_run, v_carry)
            keep_last(0, K, 0, k_run, k_carry)
            keep_last(0, V, 1, v_run, v_carry)
            split(NQ + 7)
            inverse(VAR, 1)
            s1_modulate(1)
            s2_denominator(0)
            split(NQ + 8)
            s2_invert(0, 0)
            s2_invert(0, 1)
            inverse(HSQ, 1)
            s1_norm(1)
            for n in range(NQ + 9, len(pieces)):
                split(n)
            s1_low(1)
            s2_invert(0, 2)
            s2_invert(0, 3)
            s2_y(0)
            s2_low(0)
            iteration(0, True, True)
            with dve.Fori(1, NB - 2) as b:
                iteration(b, True, True)
            iteration(NB - 2, True, False)
            iteration(NB - 1, False, False)


def ffn(nc, v):
    T, NB, DT, I_T, GU, D = v["T"], v["NB"], v["DT"], v["I_T"], v["GU"], v["D"]
    mod, ones, eps, bank = v["mod"], v["ones"], v["eps"], v["bank"]
    SB, CB, GB = v["SB"], v["CB"], v["GB"]
    x1_t, outT_t = v["x1_t"], v["outT_t"]
    NSUM = DT - 1
    with ExitStack() as ctx:
        def sb(name, shape, dt):
            return ctx.enter_context(nc.sbuf_tensor("f_" + name, shape, dt))

        def sem(name):
            return v["sem"]("f_" + name)

        DOWN = v["DOWN"]
        gu_16 = sb("gu_16", [P, 2 * I_T, DT], F16)
        gu_s = sb("gu_s", [P, 2 * I_T, DT], F32)
        down_hi = sb("down_hi", [P, DOWN], F16)
        down_lo = sb("down_lo", [P, DOWN], BF16)
        values = sb("values", [P, GU], BF16)
        N = sb("N", [P, DT, T], F32)
        H = sb("H", [P, 2, 2, DT, T], F16)
        SQ = sb("SQ", [P, 2, T], F32)
        SQY = sb("SQY", [P, 2, T], F32)
        RS = sb("RS", [P, T], F32)
        RSY = sb("RSY", [P, T], F32)
        RV = sb("RV", [P, T], F32)
        RY = sb("RY", [P, T], F32)
        A = sb("A", [P, 3, 4, T], F32)
        HH = sb("HH", [P, 3, 2, T], F16)
        Y = sb("Y", [P, DT, T], F32)
        X = sb("X", [P, DT, T], F32)
        EV = bank[0:3]
        R = bank[3]
        O = bank[4:8]

        def slot(j):
            return 2 if j == I_T - 1 else j % 2

        GROUPS = 2 * DT
        EV_BANK = [m % 3 for m in range(GROUPS)]

        def before(m):
            if m >= 3:
                return 0, m - 3
            return 1, max(k for k in range(GROUPS) if EV_BANK[k] == EV_BANK[m])

        gu_loaded, down_loaded = sem("gu_loaded"), sem("down_loaded")
        scales_loaded, scales_ready = sem("scales_loaded"), sem("scales_ready")
        n_loaded, x_sum, mean_red, centred = map(sem, ("n_loaded", "x_sum", "mean_red", "centred"))
        squared, sq_sum, var_red, var_root, var_recip = map(sem, ("squared", "sq_sum", "var_red", "var_root", "var_recip"))
        scaled, h_ready, H_high, H_low = map(sem, ("scaled", "h_ready", "H_high", "H_low"))
        group_done, by_act, by_dve = map(sem, ("group_done", "by_act", "by_dve"))
        halves, gate_silu, hid_ready = map(sem, ("halves", "gate_silu", "hid_ready"))
        HH_high, HH_low, down_used, y_copied = map(sem, ("HH_high", "HH_low", "down_used", "y_copied"))
        y_squared, y_sum, y_red, y_root, y_recip = map(sem, ("y_squared", "y_sum", "y_red", "y_root", "y_recip"))
        y_norm, res_loaded, out_ready, out_stored = map(sem, ("y_norm", "res_loaded", "out_ready", "out_stored"))

        block = ctx.enter_context(nc.Block())

        def tok(b):
            return bass.ds(b * T, T)

        def first(b):
            return isinstance(b, int) and b == 0

        def blocks(eng, iteration):
            iteration(0, 0, False, True)
            iteration(1, 1, True, True)
            iteration(2, 0, True, True)
            with eng.Fori(3, NB - 2, 2) as b:
                iteration(b, 1, True, True)
                iteration(b + 1, 0, True, True)
            iteration(NB - 1, 1, True, False)

        def slot_free(eng, done, b, j):
            if j < 2:
                if not first(b):
                    eng.wait_ge(done, I_T * b - 2 + j)
            elif j == I_T - 1:
                if not first(b):
                    eng.wait_ge(done, I_T * b)
            else:
                eng.wait_ge(done, I_T * b + j - 1)

        @block.sync
        def _(sp):
            sp.dma_start(gu_16[:], v["gu_scales"]).then_inc(scales_loaded, 16)
            sp.dma_start(N[:], x1_t[:, :, tok(0)]).then_inc(n_loaded, 16)
            sp.dma_start(values[:], v["gu_dram"]).then_inc(gu_loaded, 16)
            sp.dma_start(down_hi[:], v["down_hi_dram"]).then_inc(down_loaded, 16)
            sp.dma_start(down_lo[:], v["down_lo_dram"]).then_inc(down_loaded, 16)

            def iteration(b, s, prev, nxt):
                if nxt:
                    sp.wait_ge(H_low, DT * (b + 1))
                    sp.dma_start(N[:], x1_t[:, :, tok(b + 1)]).then_inc(n_loaded, 16)
                if prev:
                    output(b - 1)

            def output(b):
                if not first(b):
                    sp.wait_ge(out_stored, 16 * b)
                sp.dma_start(X[:], x1_t[:, :, tok(b)]).then_inc(res_loaded, 16)
                sp.wait_ge(out_ready, DT * (b + 1))
                sp.dma_start(outT_t[:, :, tok(b)], X[:]).then_inc(out_stored, 16)

            blocks(sp, iteration)
            output(NB - 1)
            sp.wait_ge(out_stored, 16 * NB)

        @block.tensor
        def _(pe):
            def bank_free(means, variances, ys):
                for s, n in ((centred, means * DT), (var_root, variances), (y_root, ys)):
                    if not (isinstance(n, int) and n <= 0):
                        pe.wait_ge(s, n)

            def mean(b):
                pe.wait_ge(x_sum, NSUM * (b + 1))
                nc.tensor.matmul(R[:], ones[:], RS[:], start=True, stop=True).then_inc(mean_red, 1)

            def variance(b):
                pe.wait_ge(sq_sum, NSUM * (b + 1))
                nc.tensor.matmul(R[:], ones[:], RS[:], start=True, stop=True).then_inc(var_red, 1)

            def y_square(b):
                pe.wait_ge(y_sum, NSUM * (b + 1))
                nc.tensor.matmul(R[:], ones[:], RSY[:], start=True, stop=True).then_inc(y_red, 1)

            def down(b, j, c):
                if c == 0:
                    pe.wait_ge(HH_high, I_T * b + j + 1)
                    pe.wait_ge(HH_low, I_T * b + j + 1)
                    if j == 0 and not first(b):
                        pe.wait_ge(y_copied, DT * b)
                col = j * D + c * P
                for w, part in ((down_hi, 0), (down_lo, 0), (down_hi, 1)):
                    mm = nc.tensor.matmul(O[c][:], w[:, col:col + P], HH[:, slot(j), part, :],
                                          start=(j == 0 and w is down_hi and part == 0),
                                          stop=(j == I_T - 1 and part == 1))
                if c == DT - 1:
                    mm.then_inc(down_used, 1)

            def iteration(b, s, prev, nxt):
                pe.wait_ge(H_high, DT * (b + 1))
                pe.wait_ge(H_low, DT * (b + 1))
                for j in range(I_T):
                    if nxt and j == 5:
                        bank_free(b + 2, b + 1, b)
                        variance(b + 1)
                    for m in range(GROUPS):
                        back, k = before(m)
                        if not (j == 0 and back and first(b)):
                            pe.wait_ge((by_act, by_dve)[k % 2], DT * (I_T * b + j - back) + k // 2 + 1)
                        which, g = m // DT, m % DT
                        col = (g * 2 * I_T + which * I_T + j) * P
                        for part in range(2):
                            mm = nc.tensor.matmul(EV[EV_BANK[m]][:], values[:, col:col + P], H[:, s, part, g, :],
                                                  start=part == 0, stop=part == 1)
                        mm.then_inc(group_done, 1)
                        if m % 2:
                            if j >= 2:
                                down(b, j - 2, m // 2)
                            elif prev:
                                down(b - 1, I_T - 2 + j, m // 2)
                    if nxt and j == 1:
                        bank_free(b + 1, b + 1, b - 1)
                        mean(b + 1)
                    if prev and j == 3:
                        bank_free(b + 2 if nxt else b + 1, b + 1, b - 1)
                        y_square(b - 1)

            mean(0)
            bank_free(1, 0, 0)
            variance(0)
            pe.wait_ge(gu_loaded, 16)
            pe.wait_ge(down_loaded, 32)
            blocks(pe, iteration)
            for j in (I_T - 2, I_T - 1):
                for c in range(DT):
                    down(NB - 1, j, c)
            bank_free(NB, NB, NB - 1)
            y_square(NB - 1)

        @block.scalar
        def _(act):
            def squares(b, ring, src, ready, done, sums):
                for c in range(DT):
                    act.wait_ge(ready, DT * b + c + 1)
                    if c >= 2:
                        act.wait_ge(sums, NSUM * b + 1)
                    elif not first(b):
                        act.wait_ge(sums, NSUM * b)
                    nc.scalar.activation(ring[:, c % 2, :], src[:, c, :], ACT.Square).then_inc(done, 1)

            def var_sqrt(b):
                act.wait_ge(var_red, b + 1)
                if not first(b):
                    act.wait_ge(scaled, DT * b)
                nc.scalar.activation(RV[:], R[:], ACT.Sqrt, bias=eps[:, 0:1]).then_inc(var_root, 1)

            def y_sqrt(b):
                act.wait_ge(y_red, b + 1)
                if not first(b):
                    act.wait_ge(y_norm, DT * b)
                nc.scalar.activation(RY[:], R[:], ACT.Sqrt, bias=eps[:, 2:3]).then_inc(y_root, 1)

            def split(b, s):
                if not first(b) and not (isinstance(b, int) and b == 1):
                    act.wait_ge(group_done, GROUPS * I_T * (b - 1))
                for c in range(DT):
                    act.wait_ge(h_ready, DT * b + c + 1)
                    nc.scalar.activation(H[:, s, 0, c, :], N[:, c, :], ACT.Copy).then_inc(H_high, 1)

            def take(b, j, m):
                which, g = m // DT, m % DT
                act.wait_ge(group_done, GROUPS * (I_T * b + j) + m + 1)
                if m == 0:
                    slot_free(act, HH_low, b, j)
                t = which * I_T + j
                nc.scalar.activation(A[:, slot(j), 2 * which + g // 2, :], EV[EV_BANK[m]][:], ACT.Copy,
                                     scale=gu_s[:, t, g:g + 1]).then_inc(by_act, 1)

            def high(b, j):
                act.wait_ge(hid_ready, I_T * b + j + 1)
                slot_free(act, down_used, b, j)
                nc.scalar.activation(HH[:, slot(j), 0, :], A[:, slot(j), 0, :], ACT.Copy).then_inc(HH_high, 1)

            def silu(b, j):
                act.wait_ge(halves, 2 * (I_T * b + j) + 1)
                nc.scalar.activation(A[:, slot(j), 0, :], A[:, slot(j), 0, :], ACT.Silu).then_inc(gate_silu, 1)

            def iteration(b, s, prev, nxt):
                for j in range(I_T):
                    take(b, j, 0)
                    take(b, j, 2)
                    take(b, j, 4)
                    if j:
                        high(b, j - 1)
                    elif prev:
                        high(b - 1, I_T - 1)
                    take(b, j, 6)
                    silu(b, j)
                    if prev and j == 2:
                        squares(b - 1, SQY, Y, y_copied, y_squared, y_sum)
                    if nxt and j == 3:
                        squares(b + 1, SQ, N, centred, squared, sq_sum)
                    if j == 4:
                        if prev:
                            y_sqrt(b - 1)
                        if nxt:
                            var_sqrt(b + 1)
                    if nxt and j == 9:
                        split(b + 1, 1 - s)

            act.wait_ge(scales_loaded, 16)
            nc.scalar.activation(gu_s[:], gu_16[:], ACT.Copy).then_inc(scales_ready, 1)
            act.wait_ge(scales_ready, 1)
            squares(0, SQ, N, centred, squared, sq_sum)
            var_sqrt(0)
            split(0, 0)
            blocks(act, iteration)
            high(NB - 1, I_T - 1)
            squares(NB - 1, SQY, Y, y_copied, y_squared, y_sum)
            y_sqrt(NB - 1)

        @block.gpsimd
        def _(pool):
            def add_up(b, ring, rs, done, sums, reduced, reductions):
                for c in range(1, DT):
                    pool.wait_ge(done, DT * b + c + 1)
                    if c == 1:
                        if not (isinstance(reductions, int) and reductions == 0):
                            pool.wait_ge(reduced, reductions)
                        a = ring[:, 0, :]
                    else:
                        pool.wait_ge(sums, NSUM * b + c - 1)
                        a = rs[:]
                    nc.gpsimd.tensor_tensor(rs[:], a, ring[:, c % 2, :], ALU.add).then_inc(sums, 1)

            def add_x(b):
                pool.wait_ge(n_loaded, 16 * (b + 1))
                if not first(b):
                    pool.wait_ge(var_red, b)
                nc.gpsimd.tensor_tensor(RS[:], N[:, 0, :], N[:, 1, :], ALU.add).then_inc(x_sum, 1)
                for c in range(2, DT):
                    pool.wait_ge(x_sum, NSUM * b + c - 1)
                    nc.gpsimd.tensor_tensor(RS[:], RS[:], N[:, c, :], ALU.add).then_inc(x_sum, 1)

            def half(b, j, which):
                pool.wait_ge(by_dve, DT * (I_T * b + j) + 2 * which + 2)
                a = A[:, slot(j), 2 * which, :]
                nc.gpsimd.tensor_tensor(a, a, A[:, slot(j), 2 * which + 1, :], ALU.add).then_inc(halves, 1)

            def low(b, j):
                pool.wait_ge(HH_high, I_T * b + j + 1)
                nc.gpsimd.tensor_tensor(HH[:, slot(j), 1, :], A[:, slot(j), 0, :], HH[:, slot(j), 0, :],
                                        ALU.subtract).then_inc(HH_low, 1)

            def scale(b):
                pool.wait_ge(var_recip, b + 1)
                pool.wait_ge(squared, DT * (b + 1))
                for c in range(DT):
                    nc.gpsimd.tensor_tensor(N[:, c, :], N[:, c, :], RV[:], ALU.mult).then_inc(scaled, 1)

            def iteration(b, s, prev, nxt):
                for j in range(I_T):
                    half(b, j, 0)
                    if j:
                        low(b, j - 1)
                    elif prev:
                        low(b - 1, I_T - 1)
                    half(b, j, 1)
                    if nxt and j == 0:
                        add_x(b + 1)
                    if prev and j == 2:
                        add_up(b - 1, SQY, RSY, y_squared, y_sum, y_red, b - 1)
                    if nxt and j == 3:
                        add_up(b + 1, SQ, RS, squared, sq_sum, mean_red, b + 2)
                    if nxt and j == 6:
                        scale(b + 1)

            add_x(0)
            add_up(0, SQ, RS, squared, sq_sum, mean_red, 1)
            scale(0)
            blocks(pool, iteration)
            low(NB - 1, I_T - 1)
            add_up(NB - 1, SQY, RSY, y_squared, y_sum, y_red, NB - 1)

        @block.vector
        def _(dve):
            def centre(b):
                dve.wait_ge(mean_red, b + 1)
                for c in range(DT):
                    nc.vector.tensor_tensor(N[:, c, :], N[:, c, :], R[:], ALU.subtract).then_inc(centred, 1)

            def inverse(b, buf, root, recip):
                dve.wait_ge(root, b + 1)
                nc.vector.reciprocal(buf[:], buf[:]).then_inc(recip, 1)

            def modulate(b):
                for c in range(DT):
                    dve.wait_ge(scaled, DT * b + c + 1)
                    nc.vector.tensor_scalar(N[:, c, :], N[:, c, :], mod[:, CB][:, c:c + 1], mod[:, SB][:, c:c + 1],
                                            ALU.mult, ALU.add).then_inc(h_ready, 1)

            def split_low(b, s):
                for c in range(DT):
                    dve.wait_ge(H_high, DT * b + c + 1)
                    nc.vector.tensor_tensor(H[:, s, 1, c, :], N[:, c, :], H[:, s, 0, c, :], ALU.subtract).then_inc(H_low, 1)

            def take(b, j, m):
                which, g = m // DT, m % DT
                dve.wait_ge(group_done, GROUPS * (I_T * b + j) + m + 1)
                dve.wait_ge(by_act, DT * (I_T * b + j) + m // 2 + 1)
                a = A[:, slot(j), 2 * which + g // 2, :]
                nc.vector.scalar_tensor_tensor(a, EV[EV_BANK[m]][:], gu_s[:, which * I_T + j, g:g + 1], a,
                                               ALU.mult, ALU.add).then_inc(by_dve, 1)

            def hidden(b, j):
                dve.wait_ge(gate_silu, I_T * b + j + 1)
                dve.wait_ge(halves, 2 * (I_T * b + j) + 2)
                a = A[:, slot(j), 0, :]
                nc.vector.tensor_tensor(a, a, A[:, slot(j), 2, :], ALU.mult).then_inc(hid_ready, 1)

            def copy_y(b):
                dve.wait_ge(down_used, I_T * (b + 1))
                if not first(b):
                    dve.wait_ge(out_ready, DT * b)
                for c in range(DT):
                    nc.vector.tensor_copy(Y[:, c, :], O[c][:]).then_inc(y_copied, 1)

            def norm_y(b):
                dve.wait_ge(y_recip, b + 1)
                dve.wait_ge(y_squared, DT * (b + 1))
                for c in range(DT):
                    nc.vector.tensor_tensor(Y[:, c, :], Y[:, c, :], RY[:], ALU.mult).then_inc(y_norm, 1)

            def result(b):
                dve.wait_ge(res_loaded, 16 * (b + 1))
                for c in range(DT):
                    dve.wait_ge(y_norm, DT * b + c + 1)
                    nc.vector.scalar_tensor_tensor(X[:, c, :], Y[:, c, :], mod[:, GB][:, c:c + 1], X[:, c, :],
                                                   ALU.mult, ALU.add).then_inc(out_ready, 1)

            def iteration(b, s, prev, nxt):
                for j in range(I_T):
                    if prev and j == 2:
                        copy_y(b - 1)
                    if nxt and j == 2:
                        centre(b + 1)
                    take(b, j, 1)
                    if j:
                        hidden(b, j - 1)
                    elif prev:
                        hidden(b - 1, I_T - 1)
                    take(b, j, 3)
                    take(b, j, 5)
                    take(b, j, 7)
                    if j == 6:
                        if nxt:
                            inverse(b + 1, RV, var_root, var_recip)
                        if prev:
                            inverse(b - 1, RY, y_root, y_recip)
                    if prev and j == 7:
                        norm_y(b - 1)
                    if nxt and j == 8:
                        modulate(b + 1)
                    if prev and j == 9:
                        result(b - 1)
                    if nxt and j == 10:
                        split_low(b + 1, 1 - s)

            centre(0)
            inverse(0, RV, var_root, var_recip)
            modulate(0)
            split_low(0, 0)
            blocks(dve, iteration)
            hidden(NB - 1, I_T - 1)
            copy_y(NB - 1)
            inverse(NB - 1, RY, y_root, y_recip)
            norm_y(NB - 1)
            result(NB - 1)


def kernel(L0_attn_x, L0_attn_w_qkv, L0_attn_w_swiglu, L0_attn_w_out, L0_ffn_gate_up_packed,
           L0_ffn_gate_up_scales, L0_ffn_down_packed, L0_ffn_down_scales, L0_c, L0_wmod):
    import numpy as np
    import concourse.bacc as bacc
    from concourse.bass_utils import run_bass_kernel_spmd

    def groups(words):
        out, n = words.shape
        return np.repeat(words.T.reshape(n // 16, 16, out).transpose(1, 0, 2).reshape(16, -1), 8, axis=0)

    gus, dns = np.asarray(L0_ffn_gate_up_scales), np.asarray(L0_ffn_down_scales)
    arrays = {
        "xT": np.asarray(L0_attn_x)[0].T,
        "wqkvT": np.asarray(L0_attn_w_qkv).T,
        "wswT": np.asarray(L0_attn_w_swiglu).T,
        "woutT": np.asarray(L0_attn_w_out).T,
        "packed": np.concatenate([groups(np.asarray(L0_ffn_gate_up_packed)), groups(np.asarray(L0_ffn_down_packed))], axis=1),
        "gu_scales": gus.reshape(gus.shape[0], -1, P).transpose(2, 1, 0),
        "down_scales": dns.reshape(1, -1),
        "c_col": np.asarray(L0_c).reshape(-1, P).T,
        "wmod": np.asarray(L0_wmod),
    }
    arrays = {name: np.ascontiguousarray(a) for name, a in arrays.items()}
    nc = bacc.Bacc("TRN2", target_bir_lowering=False, num_devices=1)
    args = [nc.dram_tensor(name, a.shape, mybir.dt.from_np(a.dtype), kind="ExternalInput").ap() for name, a in arrays.items()]
    D, S = arrays["xT"].shape
    outT = nc.dram_tensor("outT", (D, S), F32, kind="ExternalOutput").ap()
    program(nc, *args, outT)
    r = run_bass_kernel_spmd(nc, [arrays], core_ids=[0])
    return np.ascontiguousarray(r.results[0]["outT"].T)[None]
```

```python
from contextlib import ExitStack

import concourse.bass as bass
from concourse import mybir

ALU = mybir.AluOpType
ACT = mybir.ActivationFunctionType
F32 = mybir.dt.float32
F16 = mybir.dt.float16
BF16 = mybir.dt.bfloat16
I32 = mybir.dt.int32

P = 128


def program(nc, xT, wqkvT, wswT, woutT, packed, gu_scales, down_scales, c_row, wmodT, outT):
    D, S = xT.shape
    T = 512
    NB = S // T
    DT = D // P
    FT = woutT.shape[0] // P
    I_T = gu_scales.shape[1] // 2
    GU = DT * 2 * I_T * P
    QKV = 3 * DT
    DOWN = I_T * D
    LN_EPS, RMS_EPS, CUM_EPS, FFN_EPS = 1e-5, 1.1920929e-07, 1e-6, 1e-6
    HIDDEN_UNIT = 2.0 ** -6

    xT_t = xT.rearrange("(c p) s -> p c s", p=P)
    outT_t = outT.rearrange("(c p) s -> p c s", p=P)
    h_dram = nc.dram_tensor("h_scratch", [D, S], F32, kind="Internal").ap()
    x1_dram = nc.dram_tensor("x1_scratch", [D, S], F32, kind="Internal").ap()
    h_t = h_dram.rearrange("(c p) s -> p c s", p=P)
    x1_t = x1_dram.rearrange("(c p) s -> p c s", p=P)
    gu_dram = nc.dram_tensor("gu_scratch", [P, GU], BF16, kind="Internal").ap()
    down_hi_dram = nc.dram_tensor("down_hi_scratch", [P, DOWN], F16, kind="Internal").ap()
    down_lo_dram = nc.dram_tensor("down_lo_scratch", [P, DOWN], BF16, kind="Internal").ap()

    whole = ExitStack()
    with whole:
        def sem(name):
            return whole.enter_context(nc.semaphore(name))

        def keep(name, shape, dt):
            return whole.enter_context(nc.sbuf_tensor(name, shape, dt))

        mod = keep("mod", [P, 24], F32)
        ones = keep("ones", [P, P], F32)
        eps = keep("eps", [P, 3], F32)
        wqkv = keep("wqkv", [P, 2, DT, QKV * P], F16)
        values = wqkv[:].rearrange("p a c n -> p (a c n)")[:, 0:GU].bitcast(BF16)
        H = keep("H", [P, 2, DT, T], F16)
        K = keep("K", [P, DT, T], F32)
        Q = keep("Q", [P, DT, T], F32)
        gu_16 = keep("gu_16", [P, 2 * I_T, DT], F16)
        gu_s = keep("gu_s", [P, 2 * I_T, DT], F32)
        bank = [whole.enter_context(nc.psum_tensor(f"bank{i}", [P, T], F32)) for i in range(8)]
        SA, CA, GA, SB, CB, GB = (slice(DT * i, DT * i + DT) for i in range(6))

        mixer(nc, locals())
        ffn(nc, locals())


def counts(eng, *values):
    for n in values:
        if not isinstance(n, int):
            eng.compute_val(n)
    return values


def mixer(nc, v):
    T, NB, DT, FT, QKV = v["T"], v["NB"], v["DT"], v["FT"], v["QKV"]
    mod, ones, eps, bank = v["mod"], v["ones"], v["eps"], v["bank"]
    SA, CA, GA, GB = v["SA"], v["CA"], v["GA"], v["GB"]
    xT_t, h_t, x1_t = v["xT_t"], v["h_t"], v["x1_t"]
    GU, DOWN = v["GU"], v["DOWN"]
    SB, CB = v["SB"], v["CB"]
    gu_16, gu_s = v["gu_16"], v["gu_s"]
    CUM_EPS = v["CUM_EPS"]
    GU_CHUNKS, DOWN_CHUNKS = 4, 2
    CHUNKS = GU_CHUNKS + DOWN_CHUNKS
    CH = GU // (NB * GU_CHUNKS)
    assert CH * NB * GU_CHUNKS == GU and CH * NB * DOWN_CHUNKS == DOWN
    with ExitStack() as ctx:
        def sb(name, shape, dt):
            return ctx.enter_context(nc.sbuf_tensor(name, shape, dt))

        def sem(name):
            return v["sem"]("a_" + name)

        wqkv = v["wqkv"]
        wsw = sb("wsw", [P, 2, DT, 2 * FT * P], F16)
        wout = sb("wout", [P, 2, FT, DT * P], F16)
        X = sb("X", [P, DT, T], F32)
        H = v["H"]
        K = v["K"]
        V = sb("V", [P, DT, T], F32)
        Q = v["Q"]
        Y = sb("Y", [P, 2, DT, T], F16)
        SQ = [sb("SQx", [P, 2, T], F32), sb("SQqk", [P, 2, T], F32)]
        RS = [sb("RSx", [P, T], F32), sb("RSqk", [P, T], F32)]
        RD = sb("RD", [P, 2, T], F32)
        late = sb("late", [P, 4 * T], F32)
        UG = late[:, 0:2 * T].bitcast(F16).rearrange("p (b h t) -> p b h t", b=2, h=2)
        G = late[:, 2 * T:3 * T]
        XR = late[:, 3 * T:4 * T]
        HR = sb("HR", [P, T], F32)
        run = sb("run", [P, T], BF16)
        carry = sb("carry", [P, 2, DT], F32)
        clamped = sb("clamped", [P, 2, DT], F32)
        U_BANK, G_BANK, O_BANK = bank[0], bank[1], bank[4:8]
        MEAN, VAR, HSQ, KSQ, QSQ = range(5)
        FAMILY = {MEAN: 0, VAR: 0, HSQ: 0, KSQ: 1, QSQ: 1}
        NTH = {MEAN: 0, VAR: 1, HSQ: 2, QSQ: 0, KSQ: 1}
        SQUARES = {VAR: 0, HSQ: 1, QSQ: 0, KSQ: 1}
        R_BANK = {MEAN: bank[2], VAR: bank[2], HSQ: bank[2], QSQ: bank[3], KSQ: bank[0]}
        DEV = {VAR: RD[:, 0, :], HSQ: RD[:, 0, :], KSQ: RD[:, 1, :], QSQ: HR[:]}

        def sum_bank(kind, b):
            return O_BANK[0] if kind == KSQ and isinstance(b, int) and b == 0 else R_BANK[kind]

        def reductions(kind, b):
            return (3, 2)[FAMILY[kind]] * b + NTH[kind]

        def nth_squares(kind, b):
            return 2 * b + SQUARES[kind]

        room = sb("room", [P, 8 * CH], F32)
        word = room[:, 0:2 * CH].bitcast(I32).rearrange("p (b n) -> p b n", b=2)
        low3 = room[:, 2 * CH:3 * CH].bitcast(I32)
        bit3 = room[:, 3 * CH:4 * CH].bitcast(I32)
        t1 = room[:, 4 * CH:5 * CH]
        t2 = room[:, 5 * CH:6 * CH]
        row = room[:, 6 * CH:7 * CH].bitcast(F16).rearrange("p (b n) -> p b n", b=2)
        val_both = room[:, 7 * CH:8 * CH].bitcast(F16).rearrange("p (b n) -> p b n", b=2)
        val, val_hi = val_both[:, 0, :].bitcast(BF16), val_both[:, 1, :]
        lane = sb("lane", [P, 1], I32)
        shift = sb("shift", [P, 1], I32)
        const_ready = sem("const_ready")
        c_loaded = sem("c_loaded")
        wmod_loaded = sem("wmod_loaded")
        c_silu = sem("c_silu")
        mod_summed = sem("mod_summed")
        mod_step = sem("mod_step")
        mod_ready = sem("mod_ready")
        scale_loaded = sem("scale_loaded")
        w_loaded = [sem(f"w_loaded{i}") for i in range(6)]
        w_high = sem("w_high")
        w_low = sem("w_low")
        w_low_pool = sem("w_low_pool")
        x_loaded = sem("x_loaded")
        tile_sum = sem("tile_sum")
        squared = [sem("x_squared"), sem("qk_squared")]
        sq_sum = [sem("x_sq_sum"), sem("qk_sq_sum")]
        reduced = [sem("x_reduced"), sem("qk_reduced")]
        centred = sem("centred")
        root = [sem("x_root"), sem("qk_root")]
        recip = {VAR: sem("var_recip"), HSQ: sem("h_recip"), KSQ: sem("k_recip"), QSQ: sem("q_recip")}
        scaled = sem("scaled")
        h_ready = sem("h_ready")
        h_stored = sem("h_stored")
        hn_ready = sem("hn_ready")
        H_high = sem("H_high")
        H_low = sem("H_low")
        qkv_done = sem("qkv_done")
        qkv_out = sem("qkv_out")
        k_norm = sem("k_norm")
        q_norm = sem("q_norm")
        k_exp = sem("k_exp")
        wv_ready = sem("wv_ready")
        k_run = sem("k_run")
        v_run = sem("v_run")
        k_carry = sem("k_carry")
        v_carry = sem("v_carry")
        k_eps = sem("k_eps")
        q_exp = sem("q_exp")
        denominator = sem("denominator")
        inverted = sem("inverted")
        lane_ready, shift_ready = sem("lane_ready"), sem("shift_ready")
        words_loaded = [sem("words_loaded0"), sem("words_loaded1")]
        rows_loaded = sem("rows_loaded")
        words_used = sem("words_used")
        low_bits = sem("low_bits")
        decode = [sem(f"decode{i}") for i in range(6)]
        decoded = sem("decoded")
        part_stored = sem("part_stored")
        y_ready = sem("y_ready")
        Y_high = sem("Y_high")
        Y_low = sem("Y_low")
        u_done = sem("u_done")
        g_done = sem("g_done")
        g_silu = sem("g_silu")
        ug_ready = sem("ug_ready")
        UG_high = sem("UG_high")
        UG_low = sem("UG_low")
        out_used = sem("out_used")
        res_loaded = sem("res_loaded")
        res_sum = sem("res_sum")
        x1_ready = sem("x1_ready")
        x1_stored = sem("x1_stored")
        wide_loaded = sem("wide_loaded")
        wide_stored = sem("wide_stored")
        values_loaded = sem("values_loaded")
        gu_scales_loaded, gu_scales_ready = sem("gu_scales_loaded"), sem("gu_scales_ready")

        def tok(b):
            return bass.ds(b * T, T)

        wq_src = v["wqkvT"].rearrange("(c p) n -> p c n", p=P)
        ws_src = v["wswT"].rearrange("(c p) n -> p c n", p=P)
        wo_src = v["woutT"].rearrange("(c p) n -> p c n", p=P)
        pieces = [(wqkv[:, :, :, n * T:(n + 1) * T], wq_src[:, :, n * T:(n + 1) * T]) for n in range(QKV * P // T)]
        pieces += [(wsw[:, :, :, n * T:(n + 1) * T], ws_src[:, :, n * T:(n + 1) * T]) for n in range(2 * FT * P // T)]
        pieces += [(wout[:, :, n * DT:(n + 1) * DT, :], wo_src[:, n * DT:(n + 1) * DT, :]) for n in range(FT // DT)]
        NQ = QKV * P // T
        STAGES = [K[:], V[:], Q[:], Y[:].rearrange("p a c t -> p (a c t)").bitcast(F32).rearrange("p (c t) -> p c t", t=T),
                  late[:].rearrange("p (c t) -> p c t", t=T),
                  room[:, 0:DT * T].rearrange("p (c t) -> p c t", t=T)]
        assert DT * T <= 8 * CH
        STAGE = [0, 1, 2, 3, 4, 5, 3, 4, 5, 4, 5, 4, 5, 4, 5]
        assert len(STAGE) == len(pieces)
        LAST = len(pieces) - 1
        BY_POOL = (4, 5, 7, 8, 9, 10, 12)

        def by_pool(n):
            return n in BY_POOL

        def uses(n):
            return sum(1 for m in range(n + 1) if STAGE[m] == STAGE[n])

        def lows(n):
            return sum(1 for m in range(n + 1) if by_pool(m) == by_pool(n))

        def before_in_stage(n):
            return max((m for m in range(n) if STAGE[m] == STAGE[n]), default=None)

        def wait_split(eng, n):
            eng.wait_ge(w_low, sum(1 for m in range(n + 1) if not by_pool(m)))
            pool = sum(1 for m in range(n + 1) if by_pool(m))
            if pool:
                eng.wait_ge(w_low_pool, pool)

        first_cols = 2 * DT
        wmod_sb = [wsw[:, 1, :, :].rearrange("p c n -> p (c n)").bitcast(F32)[:, 0:first_cols * DT * P],
                   wout[:].rearrange("p h c n -> p (h c n)").bitcast(F32)]
        wmod_cols = [range(0, first_cols), range(first_cols, 6 * DT)]
        assert len(wmod_cols[1]) * DT * P <= DT * FT * P and DT * P <= T
        c_silu_row = HR[:, 0:DT * P]
        n_wout = len(pieces) - FT // DT

        block = ctx.enter_context(nc.Block())

        @block.sync
        def _(sp):
            def load_x(b):
                if not (isinstance(b, int) and b == 0):
                    sp.wait_ge(H_low, DT * b)
                sp.dma_start(X[:], xT_t[:, :, tok(b)]).then_inc(x_loaded, 16)

            def store_h(b):
                sp.wait_ge(h_ready, DT * (b + 1))
                sp.dma_start(h_t[:, :, tok(b)], X[:]).then_inc(h_stored, 16)

            def residual(b):
                stored, free, ready = counts(sp, 16 * (b + 1), 16 * DT * b, DT * b + 1)
                sp.wait_ge(h_stored, stored)
                for c in range(DT):
                    if c:
                        free, ready = counts(sp, 16 * (DT * b + c), DT * b + c + 1)
                    sp.wait_ge(x1_stored, free)
                    sp.dma_start(XR, xT_t[:, c, tok(b)]).then_inc(res_loaded, 16)
                    sp.dma_start(HR[:], h_t[:, c, tok(b)]).then_inc(res_loaded, 16)
                    sp.wait_ge(x1_ready, ready)
                    sp.dma_start(x1_t[:, c, tok(b)], XR).then_inc(x1_stored, 16)

            def wide_load(b):
                if b == NB - 2:
                    sp.wait_ge(y_ready, DT * NB)
                else:
                    sp.wait_ge(wide_stored, 16)
                sp.dma_start(K[:], xT_t[:, :, tok(b)]).then_inc(wide_loaded, 16)
                sp.wait_ge(h_stored, 16 * (b + 1))
                sp.dma_start(Q[:], h_t[:, :, tok(b)]).then_inc(wide_loaded, 16)

            def wide_store(b):
                sp.wait_ge(x1_ready, DT * (b + 1))
                sp.dma_start(x1_t[:, :, tok(b)], K[:]).then_inc(wide_stored, 16)

            def load_words(b, k):
                at = (GU_CHUNKS * b + k) * CH if k < GU_CHUNKS else GU + (DOWN_CHUNKS * b + k - GU_CHUNKS) * CH
                if k >= GU_CHUNKS:
                    counts(sp, (DOWN_CHUNKS * b + k - GU_CHUNKS) * CH * 2)
                if k >= 2:
                    sp.wait_ge(words_used, CHUNKS * b + k - 1)
                elif not (isinstance(b, int) and b == 0):
                    sp.wait_ge(words_used, CHUNKS * b)
                sp.dma_start(word[:, k % 2, :], v["packed"][:, bass.ds(at, CH)]).then_inc(words_loaded[k % 2], 16)
                if k >= GU_CHUNKS:
                    if not (isinstance(b, int) and b == 0):
                        sp.wait_ge(decoded, CHUNKS * b)
                    sp.dma_start(row[:, k - GU_CHUNKS, :],
                                 v["down_scales"][:, bass.ds((DOWN_CHUNKS * b + k - GU_CHUNKS) * CH, CH)].to_broadcast([P, CH])
                                 ).then_inc(rows_loaded, 16)

            def store_values(b, k):
                at = (GU_CHUNKS * b + k) * CH if k < GU_CHUNKS else (DOWN_CHUNKS * b + k - GU_CHUNKS) * CH
                counts(sp, at * 2)
                sp.wait_ge(decoded, CHUNKS * b + k + 1)
                at = bass.ds(at, CH)
                if k < GU_CHUNKS:
                    sp.dma_start(v["gu_dram"][:, at], val).then_inc(part_stored, 16)
                else:
                    sp.dma_start(v["down_hi_dram"][:, at], val_hi).then_inc(part_stored, 16)
                    sp.dma_start(v["down_lo_dram"][:, at], val).then_inc(part_stored, 16)

            def load_piece(n):
                m = before_in_stage(n)
                if m is not None:
                    sp.wait_ge(w_low_pool if by_pool(m) else w_low, lows(m))
                sp.dma_start(STAGES[STAGE[n]], pieces[n][1]).then_inc(w_loaded[STAGE[n]], 16)

            def load_wmod(part):
                cols = wmod_cols[part]
                sp.dma_start(wmod_sb[part], v["wmodT"][:, cols.start:cols.stop, :].rearrange("p n k -> p (n k)")
                             ).then_inc(wmod_loaded, 16)

            load_x(0)
            sp.dma_start(c_silu_row, v["c_row"].to_broadcast([P, DT * P])).then_inc(c_loaded, 16)
            load_wmod(0)
            for n in range(NQ + 3):
                load_piece(n)
            sp.dma_start(gu_16[:], v["gu_scales"]).then_inc(gu_scales_loaded, 16)
            store_h(0)
            load_wmod(1)
            load_x(1)
            for n in range(NQ + 3, NQ + 6):
                load_piece(n)
            store_h(1)
            for n in range(NQ + 6, LAST + 1):
                load_piece(n)
            wait_split(sp, LAST)

            def iteration(b, s1):
                load_words(b, 0)
                load_words(b, 1)
                if s1:
                    load_x(b + 2)
                elif b == NB - 1:
                    wide_load(b)
                    sp.wait_ge(H_low, DT * NB)
                    sp.wait_ge(x1_stored, 16 * DT)
                    sp.dma_start(X[:], x1_t[:, :, tok(0)]).then_inc(x_loaded, 16)
                store_values(b, 0)
                load_words(b, 2)
                store_values(b, 1)
                load_words(b, 3)
                if s1:
                    store_h(b + 2)
                for k in range(2, CHUNKS):
                    store_values(b, k)
                    if k + 2 < CHUNKS:
                        load_words(b, k + 2)
                    if not s1 and b == NB - 1 and k == GU_CHUNKS - 1:
                        sp.wait_ge(qkv_done, QKV * NB)
                        sp.wait_ge(part_stored, 16 * ((CHUNKS + DOWN_CHUNKS) * b + GU_CHUNKS))
                        sp.dma_start(v["values"], v["gu_dram"]).then_inc(values_loaded, 16)
                if s1:
                    residual(b)
                else:
                    if b == NB - 2:
                        wide_load(b)
                        wide_store(b)

            iteration(0, True)
            with sp.Fori(1, NB - 2) as b:
                iteration(b, True)
            iteration(NB - 2, False)
            iteration(NB - 1, False)
            sp.wait_ge(h_stored, 16 * NB)
            sp.wait_ge(x1_stored, 16 * DT * (NB - 2))
            sp.wait_ge(wide_stored, 16)
            sp.wait_ge(wide_loaded, 64)
            sp.wait_ge(values_loaded, 16)
            sp.wait_ge(part_stored, 16 * (CHUNKS + DOWN_CHUNKS) * NB)

        @block.tensor
        def _(pe):
            def reduce(kind, b):
                f = FAMILY[kind]
                if kind == MEAN:
                    pe.wait_ge(tile_sum, 3 * (b + 1))
                else:
                    pe.wait_ge(sq_sum[f], 3 * (nth_squares(kind, b) + 1))
                bank_read(kind, b)
                nc.tensor.matmul(sum_bank(kind, b)[:], ones[:], RS[f][:], start=True, stop=True).then_inc(reduced[f], 1)

            def bank_read(kind, b):
                if kind == VAR:
                    pe.wait_ge(centred, DT * (b + 1))
                elif kind == HSQ:
                    pe.wait_ge(root[0], 2 * b + 1)
                elif isinstance(b, int) and b == 0:
                    pass
                elif kind == KSQ:
                    pe.wait_ge(qkv_out, QKV * b + QKV - 1)
                else:
                    pe.wait_ge(root[FAMILY[kind]], 2 * b)

            def reduce_tiles(kind, b):
                f = FAMILY[kind]
                for c in range(DT):
                    if kind == MEAN:
                        tile, sums = X[:, c, :], tile_sum
                        pe.wait_ge(x_loaded, 16 * (b + 1))
                    else:
                        tile, sums = SQ[f][:, c % 2, :], sq_sum[f]
                        pe.wait_ge(squared[f], DT * nth_squares(kind, b) + c + 1)
                    if c == 0:
                        bank_read(kind, b)
                    mm = nc.tensor.matmul(R_BANK[kind][:], ones[:], tile, start=c == 0, stop=c == DT - 1)
                    if c in (1, 2):
                        mm.then_inc(sums, c)
                mm.then_inc(reduced[f], 1)

            def qkv(b):
                n = 0
                for part in range(3):
                    if isinstance(b, int) and b == 0:
                        pe.wait_ge(w_low, part + 1)
                    for c in range(DT):
                        out = bank[n % 2]
                        col = (part * DT + c) * P
                        if n >= 2:
                            pe.wait_ge(qkv_out, QKV * b + n - 1)
                        elif not (isinstance(b, int) and b == 0):
                            if not (isinstance(b, int) and b == 1):
                                pe.wait_ge((ug_ready, g_silu)[n], FT * (b - 1))
                            pe.wait_ge(qkv_out, QKV * b)
                            pe.wait_ge(root[1], 2 * b)
                        for k in range(DT):
                            if n == 0:
                                pe.wait_ge(H_high, DT * b + k + 1)
                                pe.wait_ge(H_low, DT * b + k + 1)
                            for pw, px in ((0, 0), (1, 0), (0, 1)):
                                mm = nc.tensor.matmul(out[:], wqkv[:, pw, k, col:col + P], H[:, px, k, :],
                                                      start=(k == 0 and pw == 0 and px == 0), stop=(k == DT - 1 and px == 1))
                        mm.then_inc(qkv_done, 1)
                        n += 1
                        if isinstance(b, int) and b == 0 and n in (5, 6, 8, 10):
                            reduce(*{5: (MEAN, 1), 6: (QSQ, 0), 8: (VAR, 1), 10: (KSQ, 0)}[n])
                    if part == 1 and not (isinstance(b, int) and b == 0):
                        reduce(QSQ, b)
                if isinstance(b, int) and b == 0:
                    reduce(HSQ, 1)
                else:
                    reduce(KSQ, b)

            def output(b, j):
                if j == 0 and isinstance(b, int) and b == 0:
                    wait_split(pe, LAST)
                pe.wait_ge(UG_high, FT * b + j + 1)
                pe.wait_ge(UG_low, FT * b + j + 1)
                if j == 0 and not (isinstance(b, int) and b == 0):
                    pe.wait_ge(res_sum, DT * b)
                for c in range(DT):
                    for pw, px in ((0, 0), (1, 0), (0, 1)):
                        mm = nc.tensor.matmul(O_BANK[c][:], wout[:, pw, j, c * P:(c + 1) * P], UG[:, j % 2, px, :],
                                              start=(j == 0 and pw == 0 and px == 0), stop=(j == FT - 1 and px == 1))
                mm.then_inc(out_used, 1)

            def swiglu(b, s2, s1):
                if isinstance(b, int) and b == 0:
                    wait_split(pe, n_wout - 1)
                pe.wait_ge(Y_high, DT * (b + 1))
                pe.wait_ge(Y_low, DT * (b + 1))
                for j in range(FT):
                    for which, out, done, read in ((1, G_BANK, g_done, g_silu), (0, U_BANK, u_done, ug_ready)):
                        if j == 0:
                            if not (isinstance(b, int) and b == 0):
                                pe.wait_ge(read, FT * b)
                            pe.wait_ge(qkv_out, QKV * (b + 2 if s2 else b + 1))
                            if which == 0:
                                pe.wait_ge(root[1], 2 * (b + 2 if s2 else b + 1))
                        else:
                            pe.wait_ge(read, FT * b + j)
                        col = (which * FT + j) * P
                        for k in range(DT):
                            for pw, px in ((0, 0), (1, 0), (0, 1)):
                                mm = nc.tensor.matmul(out[:], wsw[:, pw, k, col:col + P], Y[:, px, k, :],
                                                      start=(k == 0 and pw == 0 and px == 0), stop=(k == DT - 1 and px == 1))
                        mm.then_inc(done, 1)
                    if s1 and j in (2, 5, 10):
                        reduce({2: MEAN, 5: VAR, 10: HSQ}[j], b + 2)
                    if not s1 and not s2 and j in (3, 7):
                        reduce({3: MEAN, 7: VAR}[j], NB)
                    if j:
                        output(b, j - 1)
                output(b, FT - 1)

            def iteration(b, s2, s1):
                if s2:
                    qkv(b + 1)
                swiglu(b, s2, s1)

            pe.wait_ge(const_ready, 1)
            for kind in (MEAN, VAR, HSQ):
                reduce_tiles(kind, 0)
            qkv(0)
            iteration(0, True, True)
            with pe.Fori(1, NB - 2) as b:
                iteration(b, True, True)
            iteration(NB - 2, True, False)
            iteration(NB - 1, False, False)

        @block.scalar
        def _(act):
            def square(kind, b, src, ready, per, c0=0):
                f, use = FAMILY[kind], nth_squares(kind, b)
                for c in range(DT):
                    act.wait_ge(ready, per * b + c0 + c + 1)
                    if c >= 2:
                        act.wait_ge(sq_sum[f], 3 * use + 1)
                    elif not (isinstance(use, int) and use == 0):
                        act.wait_ge(sq_sum[f], 3 * use - 1 + c)
                    nc.scalar.activation(SQ[f][:, c % 2, :], src[:, c, :], ACT.Square).then_inc(squared[f], 1)

            def sqrt(kind, b):
                f = FAMILY[kind]
                act.wait_ge(reduced[f], reductions(kind, b) + 1)
                if kind == HSQ:
                    act.wait_ge(scaled, DT * (b + 1))
                elif kind == QSQ and isinstance(b, int) and b == 0:
                    act.wait_ge(mod_summed, 6 * DT)
                elif not (isinstance(b, int) and b == 0):
                    act.wait_ge({VAR: hn_ready, KSQ: k_norm, QSQ: q_norm}[kind], DT * b)
                    if kind == QSQ and not (isinstance(b, int) and b == 1):
                        act.wait_ge(x1_ready, DT * (b - 1))
                nc.scalar.activation(DEV[kind], sum_bank(kind, b)[:], ACT.Sqrt,
                                     bias=eps[:, (0 if kind == VAR else 1):(1 if kind == VAR else 2)]).then_inc(root[f], 1)

            def s1_var(b):
                square(VAR, b, X, centred, DT)

            def s1_h(b):
                square(HSQ, b, X, h_ready, DT)

            def s1_split(b, ready=hn_ready):
                for c in range(DT):
                    act.wait_ge(ready, DT * b + c + 1)
                    if c == 0 and not (isinstance(b, int) and b == 0):
                        act.wait_ge(qkv_done, QKV * b)
                    nc.scalar.activation(H[:, 0, c, :], X[:, c, :], ACT.Copy).then_inc(H_high, 1)

            def copy_out(b, n, dst):
                act.wait_ge(qkv_done, QKV * b + n + 1)
                nc.scalar.activation(dst[:, n % DT, :], bank[n % 2][:], ACT.Copy).then_inc(qkv_out, 1)

            def s2_copies(b):
                pieces_after = {1: 9, 3: 10, 5: 11, 7: 12, 9: 13, 11: 14} if isinstance(b, int) and b == 1 else {}
                for n in range(QKV):
                    c = n % DT
                    if n < DT:
                        act.wait_ge(denominator, DT * (b - 1) + c + 1)
                    elif n < 2 * DT:
                        if isinstance(b, int) and b == 1:
                            s2_split_tile(0, c)
                        act.wait_ge(y_ready, DT * (b - 1) + c + 1)
                    if n == 2 * DT:
                        act.wait_ge(Y_low, DT * b)
                    copy_out(b, n, (Q, K, V)[n // DT])
                    if n == DT - 1:
                        square(QSQ, b, Q, qkv_out, QKV)
                    if n == 2 * DT:
                        square(KSQ, b, K, qkv_out, QKV, c0=DT)
                    if n in pieces_after:
                        split(pieces_after[n])

            def s2_exp(b):
                for c in range(DT):
                    act.wait_ge(k_norm, DT * b + c + 1)
                    nc.scalar.activation(K[:, c, :], K[:, c, :], ACT.Exp).then_inc(k_exp, 1)

            def s2_exp_q(b):
                for c in range(DT):
                    act.wait_ge(q_norm, DT * b + c + 1)
                    nc.scalar.activation(Q[:, c, :], Q[:, c, :], ACT.Exp, scale=-1.0).then_inc(q_exp, 1)

            def s2_split_tile(b, c):
                if not (isinstance(b, int) and b == 0):
                    act.wait_ge(u_done, FT * b)
                else:
                    wait_split(act, 6)
                act.wait_ge(y_ready, DT * b + c + 1)
                nc.scalar.activation(Y[:, 0, c, :], V[:, c, :], ACT.Copy).then_inc(Y_high, 1)

            def s2_split(b):
                for c in range(DT):
                    s2_split_tile(b, c)

            def silu(b, j):
                act.wait_ge(g_done, FT * b + j + 1)
                if j == 0 and isinstance(b, int) and b == 0:
                    wait_split(act, 13)
                if not (isinstance(b, int) and b == 0 and j == 0):
                    act.wait_ge(UG_low, FT * b + j)
                nc.scalar.activation(G, G_BANK[:], ACT.Silu).then_inc(g_silu, 1)

            def high(b, j):
                act.wait_ge(ug_ready, FT * b + j + 1)
                if j >= 2:
                    act.wait_ge(out_used, FT * b + j - 1)
                elif not (isinstance(b, int) and b == 0):
                    act.wait_ge(out_used, FT * b)
                nc.scalar.activation(UG[:, j % 2, 0, :], G, ACT.Copy).then_inc(UG_high, 1)

            def iteration(b, s2, s1):
                if s2:
                    s2_copies(b + 1)
                    sqrt(QSQ, b + 1)
                    sqrt(KSQ, b + 1)
                for j in range(FT):
                    silu(b, j)
                    if s2 and j == 1:
                        s2_exp(b + 1)
                    if s2 and j == 3:
                        s2_exp_q(b + 1)
                    if s1 and j == 4:
                        s1_var(b + 2)
                    if s1 and j == 6:
                        sqrt(VAR, b + 2)
                    if s1 and j == 9:
                        s1_h(b + 2)
                    if s1 and j == 11:
                        sqrt(HSQ, b + 2)
                    if not s1 and not s2:
                        if j == 5:
                            s1_var(NB)
                        if j == 8:
                            sqrt(VAR, NB)
                    high(b, j)
                    if s1 and j == 14:
                        s1_split(b + 2)
                    if not s1 and not s2 and j == 11:
                        s1_split(NB, h_ready)
                if s2:
                    s2_split(b + 1)

            def split(n):
                act.wait_ge(w_loaded[STAGE[n]], 16 * uses(n))
                if n == NQ:
                    act.wait_ge(mod_summed, first_cols)
                if n == n_wout:
                    act.wait_ge(mod_summed, 6 * DT)
                nc.scalar.activation(pieces[n][0][:, 0], STAGES[STAGE[n]], ACT.Copy).then_inc(w_high, 1)

            act.wait_ge(c_loaded, 16)
            nc.scalar.activation(c_silu_row, c_silu_row, ACT.Silu).then_inc(c_silu, 1)
            act.wait_ge(const_ready, 1)
            s1_var(0)
            split(0)
            sqrt(VAR, 0)
            split(1)
            split(2)
            act.wait_ge(gu_scales_loaded, 16)
            I_T = v["I_T"]
            nc.scalar.activation(gu_s[:, 0:I_T, :], gu_16[:, 0:I_T, :], ACT.Copy).then_inc(gu_scales_ready, 1)
            nc.scalar.activation(gu_s[:, I_T:, :], gu_16[:, I_T:, :], ACT.Copy,
                                 scale=v["HIDDEN_UNIT"]).then_inc(gu_scales_ready, 1)
            s1_h(0)
            split(3)
            sqrt(HSQ, 0)
            s1_split(0)
            split(4)
            split(5)
            act.wait_ge(w_low, NQ)
            for n in range(QKV):
                copy_out(0, n, (Q, K, V)[n // DT])
                if n == 2:
                    split(6)
                if n == DT - 1:
                    square(QSQ, 0, Q, qkv_out, QKV)
                if n == DT + 1:
                    s1_var(1)
                if n == DT + 2:
                    sqrt(QSQ, 0)
                if n == 2 * DT - 1:
                    square(KSQ, 0, K, qkv_out, QKV, c0=DT)
                if n == 2 * DT:
                    sqrt(VAR, 1)
                if n == 2 * DT + 1:
                    sqrt(KSQ, 0)
                    s2_exp_q(0)
            s1_h(1)
            s2_exp(0)
            sqrt(HSQ, 1)
            split(7)
            s1_split(1)
            split(8)
            iteration(0, True, True)
            with act.Fori(1, NB - 2) as b:
                iteration(b, True, True)
            iteration(NB - 2, True, False)
            iteration(NB - 1, False, False)

        @block.gpsimd
        def _(pool):
            def add_squares(kind, b):
                f, use = FAMILY[kind], nth_squares(kind, b)
                n = reductions(kind, b)
                if not (isinstance(n, int) and n == 0):
                    pool.wait_ge(reduced[f], n)
                pool.wait_ge(squared[f], DT * use + 2)
                nc.gpsimd.tensor_tensor(RS[f][:], SQ[f][:, 0, :], SQ[f][:, 1, :], ALU.add).then_inc(sq_sum[f], 1)
                for c in range(2, DT):
                    pool.wait_ge(squared[f], DT * use + c + 1)
                    pool.wait_ge(sq_sum[f], 3 * use + c - 1)
                    nc.gpsimd.tensor_tensor(RS[f][:], RS[f][:], SQ[f][:, c % 2, :], ALU.add).then_inc(sq_sum[f], 1)

            def add_x(b):
                pool.wait_ge(x_loaded, 16 * (b + 1))
                pool.wait_ge(reduced[0], reductions(MEAN, b))
                rs = RS[0][:]
                nc.gpsimd.tensor_tensor(rs, X[:, 0, :], X[:, 1, :], ALU.add).then_inc(tile_sum, 1)
                for c in range(2, DT):
                    pool.wait_ge(tile_sum, 3 * b + c - 1)
                    nc.gpsimd.tensor_tensor(rs, rs, X[:, c, :], ALU.add).then_inc(tile_sum, 1)

            def weigh(b):
                for c in range(DT):
                    pool.wait_ge(k_exp, DT * b + c + 1)
                    pool.wait_ge(qkv_out, QKV * (b + 1))
                    nc.gpsimd.tensor_tensor(V[:, c, :], K[:, c, :], V[:, c, :], ALU.mult).then_inc(wv_ready, 1)

            def low(b, j):
                pool.wait_ge(UG_high, FT * b + j + 1)
                nc.gpsimd.tensor_tensor(UG[:, j % 2, 1, :], G, UG[:, j % 2, 0, :], ALU.subtract).then_inc(UG_low, 1)

            def iteration(b, s2, s1):
                if s2:
                    add_squares(QSQ, b + 1)
                    if isinstance(b, int) and b == 0:
                        split_low(10)
                        split_low(12)
                    add_squares(KSQ, b + 1)
                for j in range(FT):
                    if s1 and j == 4:
                        add_squares(VAR, b + 2)
                    if s1 and j == 9:
                        add_squares(HSQ, b + 2)
                    if not s1 and not s2 and j == 5:
                        add_squares(VAR, NB)
                    low(b, j)
                    if not s1 and not s2 and j == 1:
                        add_x(NB)
                    if s1 and j == 0:
                        add_x(b + 2)
                    if s2 and j == 2:
                        weigh(b + 1)

            def split_low(n):
                pool.wait_ge(w_high, n + 1)
                nc.gpsimd.tensor_tensor(pieces[n][0][:, 1], STAGES[STAGE[n]], pieces[n][0][:, 0],
                                        ALU.subtract).then_inc(w_low_pool, 1)

            nc.gpsimd.iota(lane[:], pattern=[[0, 1]], base=0, channel_multiplier=1).then_inc(lane_ready, 1)
            split_low(4)
            add_x(1)
            split_low(5)
            add_squares(QSQ, 0)
            add_squares(VAR, 1)
            add_squares(KSQ, 0)
            add_squares(HSQ, 1)
            weigh(0)
            split_low(7)
            split_low(8)
            split_low(9)
            iteration(0, True, True)
            with pool.Fori(1, NB - 2) as b:
                iteration(b, True, True)
            iteration(NB - 2, True, False)
            iteration(NB - 1, False, False)

        @block.vector
        def _(dve):
            def inverse(kind, b):
                f, n = FAMILY[kind], nth_squares(kind, b) + 1
                dve.wait_ge(root[f], n)
                nc.vector.reciprocal(DEV[kind], DEV[kind]).then_inc(recip[kind], 1)
                dve.wait_ge(recip[kind], b + 1)

            def times(dst, a, b_, done):
                nc.vector.tensor_tensor(dst, a, b_, ALU.mult).then_inc(done, 1)

            def s1_centre(b):
                dve.wait_ge(reduced[0], reductions(MEAN, b) + 1)
                for c in range(DT):
                    nc.vector.tensor_tensor(X[:, c, :], X[:, c, :], R_BANK[MEAN][:], ALU.subtract).then_inc(centred, 1)

            def s1_modulate(b, CA=CA, SA=SA):
                dve.wait_ge(squared[0], DT * (nth_squares(VAR, b) + 1))
                for c in range(DT):
                    times(X[:, c, :], X[:, c, :], DEV[VAR], scaled)
                for c in range(DT):
                    dve.wait_ge(scaled, DT * b + c + 1)
                    nc.vector.tensor_scalar(X[:, c, :], X[:, c, :], mod[:, CA][:, c:c + 1], mod[:, SA][:, c:c + 1],
                                            ALU.mult, ALU.add).then_inc(h_ready, 1)

            def s1_norm(b, tiles=range(DT)):
                dve.wait_ge(h_stored, 16 * (b + 1))
                dve.wait_ge(squared[0], DT * (nth_squares(HSQ, b) + 1))
                for c in tiles:
                    times(X[:, c, :], X[:, c, :], DEV[HSQ], hn_ready)

            def s1_low(b, tiles=range(DT)):
                for c in tiles:
                    dve.wait_ge(H_high, DT * b + c + 1)
                    nc.vector.tensor_tensor(H[:, 1, c, :], X[:, c, :], H[:, 0, c, :], ALU.subtract).then_inc(H_low, 1)

            def s2_norm_k(b):
                for c in range(DT):
                    times(K[:, c, :], K[:, c, :], DEV[KSQ], k_norm)

            def s2_norm_q(b):
                for c in range(DT):
                    times(Q[:, c, :], Q[:, c, :], DEV[QSQ], q_norm)

            def scan(b, buf, which, ready, done, copied):
                for c in range(DT):
                    dve.wait_ge(ready, DT * b + c + 1)
                    dve.wait_ge(wv_ready, DT * b + c + 1)
                    if not (isinstance(b, int) and b == 0):
                        dve.wait_ge(copied, DT * b)
                    first = isinstance(b, int) and b == 0
                    nc.vector.tensor_tensor_scan(buf[:, c, :], run[:], buf[:, c, :],
                                                 0.0 if first else carry[:, which, c:c + 1],
                                                 ALU.mult, ALU.add).then_inc(done, 1)

            def keep_last(b, buf, which, done, copied):
                for c in range(DT):
                    dve.wait_ge(done, DT * b + c + 1)
                    nc.vector.tensor_copy(carry[:, which, c:c + 1], buf[:, c, T - 1:T]).then_inc(copied, 1)

            def s2_denominator(b):
                for c in range(DT):
                    dve.wait_ge(k_carry, DT * b + c + 1)
                    nc.vector.tensor_scalar(K[:, c, :], K[:, c, :], CUM_EPS, None, ALU.add).then_inc(k_eps, 1)
                for c in range(DT):
                    dve.wait_ge(k_eps, DT * b + c + 1)
                    dve.wait_ge(q_exp, DT * b + c + 1)
                    nc.vector.scalar_tensor_tensor(K[:, c, :], Q[:, c, :], 1.0, K[:, c, :],
                                                   ALU.add, ALU.mult).then_inc(denominator, 1)

            def s2_invert(b, c):
                dve.wait_ge(denominator, DT * b + c + 1)
                nc.vector.reciprocal(K[:, c, :], K[:, c, :]).then_inc(inverted, 1)

            def s2_y(b, c):
                dve.wait_ge(inverted, DT * b + c + 1)
                dve.wait_ge(v_carry, DT * b + c + 1)
                times(V[:, c, :], V[:, c, :], K[:, c, :], y_ready)

            def s2_low(b):
                for c in range(DT):
                    dve.wait_ge(Y_high, DT * b + c + 1)
                    nc.vector.tensor_tensor(Y[:, 1, c, :], V[:, c, :], Y[:, 0, c, :], ALU.subtract).then_inc(Y_low, 1)

            def hidden(b, j):
                dve.wait_ge(u_done, FT * b + j + 1)
                dve.wait_ge(g_silu, FT * b + j + 1)
                times(G, G, U_BANK[:], ug_ready)

            def residual(b):
                dve.wait_ge(out_used, FT * (b + 1))
                for c in range(DT):
                    n = DT * b + c
                    dve.wait_ge(res_loaded, 32 * (n + 1))
                    nc.vector.tensor_tensor(HR[:], HR[:], O_BANK[c][:], ALU.add).then_inc(res_sum, 1)
                    dve.wait_ge(res_sum, n + 1)
                    nc.vector.scalar_tensor_tensor(XR, HR[:], mod[:, GA][:, c:c + 1], XR,
                                                   ALU.mult, ALU.add).then_inc(x1_ready, 1)

            def wide_residual(b):
                dve.wait_ge(out_used, FT * (b + 1))
                dve.wait_ge(wide_loaded, 32 * (b - (NB - 2) + 1))
                for c in range(DT):
                    nc.vector.tensor_tensor(Q[:, c, :], Q[:, c, :], O_BANK[c][:], ALU.add).then_inc(res_sum, 1)
                for c in range(DT):
                    dve.wait_ge(res_sum, DT * b + c + 1)
                    nc.vector.scalar_tensor_tensor(K[:, c, :], Q[:, c, :], mod[:, GA][:, c:c + 1], K[:, c, :],
                                                   ALU.mult, ALU.add).then_inc(x1_ready, 1)

            def decode_chunk(b, k):
                n = CHUNKS * b + k + 1
                dve.wait_ge(words_loaded[k % 2], 16 * (CHUNKS // 2 * b + k // 2 + 1))
                w = word[:, k % 2, :]
                nc.vector.tensor_scalar(low3, w, shift[:, 0:1], 7, ALU.logical_shift_right, ALU.bitwise_and).then_inc(low_bits, 1)
                nc.vector.tensor_scalar(bit3, w, shift[:, 0:1], 8, ALU.logical_shift_right, ALU.bitwise_and).then_inc(words_used, 1)
                dve.wait_ge(low_bits, n)
                nc.vector.scalar_tensor_tensor(t1, low3, 4.0, low3, ALU.max, ALU.add).then_inc(decode[0], 1)
                nc.vector.tensor_scalar(t2, low3, 6.0, 2.0, ALU.max, ALU.mult).then_inc(decode[1], 1)
                dve.wait_ge(decode[0], n)
                dve.wait_ge(decode[1], n)
                nc.vector.scalar_tensor_tensor(t1, t1, -16.0, t2, ALU.add, ALU.add).then_inc(decode[2], 1)
                dve.wait_ge(decode[2], n)
                dve.wait_ge(words_used, n)
                half = 0.5 if k < GU_CHUNKS else 0.5 / v["HIDDEN_UNIT"]
                nc.vector.tensor_scalar(t2, bit3, -half / 4, half, ALU.mult, ALU.add).then_inc(decode[3], 1)
                dve.wait_ge(decode[3], n)
                stored = (CHUNKS + DOWN_CHUNKS) * b + k + max(k - GU_CHUNKS, 0)
                if not (isinstance(stored, int) and stored == 0):
                    dve.wait_ge(part_stored, 16 * stored)
                if k < GU_CHUNKS:
                    nc.vector.tensor_tensor(val, t1, t2, ALU.mult).then_inc(decoded, 1)
                else:
                    m = DOWN_CHUNKS * b + k - GU_CHUNKS + 1
                    nc.vector.tensor_tensor(t1, t1, t2, ALU.mult).then_inc(decode[4], 1)
                    dve.wait_ge(decode[4], 2 * m - 1)
                    dve.wait_ge(rows_loaded, 16 * m)
                    nc.vector.tensor_tensor(t1, t1, row[:, k - GU_CHUNKS, :], ALU.mult).then_inc(decode[4], 1)
                    dve.wait_ge(decode[4], 2 * m)
                    nc.vector.tensor_copy(val_hi, t1).then_inc(decode[5], 1)
                    dve.wait_ge(decode[5], m)
                    nc.vector.tensor_tensor(val, t1, val_hi, ALU.subtract).then_inc(decoded, 1)
                dve.wait_ge(decoded, n)

            def iteration(b, s2, s1):
                if isinstance(b, int) and b == 0:
                    split_low(13)
                if s2:
                    inverse(KSQ, b + 1)
                if isinstance(b, int) and b == 0:
                    split_low(14)
                for j in range(FT):
                    hidden(b, j)
                    if s2:
                        n = b + 1
                        if j == 0:
                            s2_norm_k(n)
                        if j == 1:
                            inverse(QSQ, n)
                        if j == 2:
                            s2_norm_q(n)
                        if j == 3:
                            scan(n, K, 0, k_exp, k_run, k_carry)
                        if j == 4:
                            scan(n, V, 1, wv_ready, v_run, v_carry)
                        if j == 5:
                            keep_last(n, K, 0, k_run, k_carry)
                            keep_last(n, V, 1, v_run, v_carry)
                            s2_denominator(n)
                        if j in (6, 9, 10, 11):
                            s2_invert(n, (6, 9, 10, 11).index(j))
                        if j == 13:
                            for c in range(DT):
                                s2_y(n, c)
                    if s1:
                        n = b + 2
                        if j == 2:
                            s1_centre(n)
                        if j == 7:
                            inverse(VAR, n)
                        if j == 8:
                            s1_modulate(n)
                        if j == 12:
                            inverse(HSQ, n)
                        if j == 13:
                            s1_norm(n)
                        if j == 15:
                            s1_low(n)
                    if not s1 and not s2:
                        if j == 4:
                            s1_centre(NB)
                        if j == 9:
                            inverse(VAR, NB)
                            s1_modulate(NB, CB, SB)
                        if j == 12:
                            s1_low(NB)
                    if j in (0, 6, 10, 11, 12, 14):
                        decode_chunk(b, (0, 6, 10, 11, 12, 14).index(j))
                if s2:
                    s2_low(b + 1)
                if s1:
                    residual(b)
                elif b == NB - 2:
                    wide_residual(b)

            def split_low(n):
                dve.wait_ge(w_high, n + 1)
                nc.vector.tensor_tensor(pieces[n][0][:, 1], STAGES[STAGE[n]], pieces[n][0][:, 0],
                                        ALU.subtract).then_inc(w_low, 1)

            def modulation(part, cols):
                dve.wait_ge(c_silu, 1)
                dve.wait_ge(wmod_loaded, 16 * (part + 1))
                for n in cols:
                    at = n - wmod_cols[part].start
                    row_ = wmod_sb[part][:, at * DT * P:(at + 1) * DT * P]
                    nc.vector.scalar_tensor_tensor(row_, row_, 1.0, c_silu_row, ALU.mult, ALU.mult,
                                                   accum_out=mod[:, n:n + 1]).then_inc(mod_summed, 1)

            dve.wait_ge(lane_ready, 1)
            nc.vector.tensor_scalar(lane[:], lane[:], 7, 2, ALU.bitwise_and, ALU.logical_shift_left).then_inc(shift_ready, 1)
            dve.wait_ge(shift_ready, 1)
            nc.vector.tensor_copy(shift[:], lane[:]).then_inc(shift_ready, 1)
            dve.wait_ge(shift_ready, 2)
            nc.vector.memset(ones[:], 1.0 / (DT * P)).then_inc(mod_step, 1)
            nc.vector.memset(eps[:, 0:1], v["LN_EPS"]).then_inc(mod_step, 1)
            nc.vector.memset(eps[:, 1:2], v["RMS_EPS"]).then_inc(mod_step, 1)
            nc.vector.memset(eps[:, 2:3], v["FFN_EPS"]).then_inc(mod_step, 1)
            nc.vector.memset(run[:], 1.0).then_inc(mod_step, 1)
            dve.wait_ge(mod_step, 5)
            nc.vector.memset(clamped[:], 0.0).then_inc(const_ready, 1)

            def add_one(cols):
                nc.vector.tensor_scalar(cols, cols, 1.0, None, ALU.add).then_inc(mod_step, 1)

            def clamp(gate, n):
                sign, size = clamped[:, 0, :], clamped[:, 1, :]
                nc.vector.tensor_scalar(sign, gate, 0.0, 2.0, ALU.is_ge, ALU.mult).then_inc(mod_step, 1)
                nc.vector.scalar_tensor_tensor(size, gate, -1.0, gate, ALU.mult, ALU.max).then_inc(mod_step, 1)
                dve.wait_ge(mod_step, n + 2)
                nc.vector.tensor_scalar(size, size, 0.25, None, ALU.max).then_inc(mod_step, 1)
                dve.wait_ge(mod_step, n + 3)
                nc.vector.scalar_tensor_tensor(gate, sign, -1.0, size, ALU.add, ALU.mult).then_inc(mod_step, 1)
                dve.wait_ge(mod_step, n + 4)

            s1_centre(0)
            modulation(0, wmod_cols[0])
            dve.wait_ge(mod_summed, first_cols)
            add_one(mod[:, CA])
            split_low(0)
            inverse(VAR, 0)
            dve.wait_ge(mod_step, 6)
            s1_modulate(0)
            split_low(1)
            split_low(2)
            inverse(HSQ, 0)
            s1_norm(0, (0,))
            for c in range(1, DT):
                s1_norm(0, (c,))
                s1_low(0, (c - 1,))
            s1_low(0, (DT - 1,))
            split_low(3)
            modulation(1, wmod_cols[1])
            dve.wait_ge(mod_summed, 6 * DT)
            add_one(mod[:, CB])
            clamp(mod[:, GA], 7)
            clamp(mod[:, GB], 11)
            split_low(6)
            s1_centre(1)
            inverse(QSQ, 0)
            s2_norm_q(0)
            inverse(VAR, 1)
            s1_modulate(1)
            inverse(KSQ, 0)
            s2_norm_k(0)
            inverse(HSQ, 1)
            s1_norm(1)
            scan(0, K, 0, k_exp, k_run, k_carry)
            scan(0, V, 1, wv_ready, v_run, v_carry)
            s1_low(1)
            keep_last(0, K, 0, k_run, k_carry)
            keep_last(0, V, 1, v_run, v_carry)
            s2_denominator(0)
            s2_invert(0, 0)
            s2_y(0, 0)
            for c in range(1, DT):
                s2_invert(0, c)
                s2_y(0, c)
            s2_low(0)
            split_low(11)
            iteration(0, True, True)
            with dve.Fori(1, NB - 2) as b:
                iteration(b, True, True)
            iteration(NB - 2, True, False)
            iteration(NB - 1, False, False)


def ffn(nc, v):
    T, NB, DT, I_T, GU, D = v["T"], v["NB"], v["DT"], v["I_T"], v["GU"], v["D"]
    mod, ones, eps, bank = v["mod"], v["ones"], v["eps"], v["bank"]
    SB, CB, GB = v["SB"], v["CB"], v["GB"]
    x1_t, outT_t = v["x1_t"], v["outT_t"]
    NSUM = DT - 1
    with ExitStack() as ctx:
        def sb(name, shape, dt):
            return ctx.enter_context(nc.sbuf_tensor("f_" + name, shape, dt))

        def sem(name):
            return v["sem"]("f_" + name)

        DOWN = v["DOWN"]
        gu_s, values = v["gu_s"], v["values"]
        down_hi = sb("down_hi", [P, DOWN], F16)
        down_lo = sb("down_lo", [P, DOWN], BF16)
        N = sb("N", [P, DT, T], F32)
        H = [v["H"], sb("H1", [P, 2, DT, T], F16)]
        SQ = sb("SQ", [P, DT, T], F32)
        SQY = sb("SQY", [P, DT, T], F32)
        RS = sb("RS", [P, T], F32)
        RSY = sb("RSY", [P, T], F32)
        RV = sb("RV", [P, T], F32)
        RY = sb("RY", [P, T], F32)
        A = sb("A", [P, 3, 4, T], F32)
        HH = sb("HH", [P, 3, 2, T], F16)
        Y = sb("Y", [P, DT, T], F32)
        X = sb("X", [P, DT, T], F32)
        EV = bank[0:4]
        R = bank[3]
        O = bank[4:8]

        def slot(j):
            return 2 if j == I_T - 1 else j % 2

        GROUPS = 2 * DT
        R_STEPS = range(2, 6)

        def ev_bank(j, m):
            return m % (3 if j in R_STEPS else 4)

        def before(j, m):
            for back, last in ((0, m), (1, GROUPS)):
                same = [k for k in range(last) if ev_bank((j - back) % I_T, k) == ev_bank(j, m)]
                if same:
                    return back, same[-1]
            assert ev_bank(j, m) == 3
            return None

        down_loaded = sem("down_loaded")
        n_loaded, x_sum, mean_red, centred = map(sem, ("n_loaded", "x_sum", "mean_red", "centred"))
        squared, sq_sum, var_red, var_root, var_recip = map(sem, ("squared", "sq_sum", "var_red", "var_root", "var_recip"))
        scaled, H_high, H_low = map(sem, ("scaled", "H_high", "H_low"))
        group_done, by_act, by_dve = map(sem, ("group_done", "by_act", "by_dve"))
        halves, gate_silu, hid_ready = map(sem, ("halves", "gate_silu", "hid_ready"))
        HH_high, HH_low, down_used, y_copied = map(sem, ("HH_high", "HH_low", "down_used", "y_copied"))
        y_squared, y_sum, y_red, y_kept, y_root, y_recip = map(sem, ("y_squared", "y_sum", "y_red", "y_kept", "y_root", "y_recip"))
        y_norm, res_loaded, out_ready, out_stored = map(sem, ("y_norm", "res_loaded", "out_ready", "out_stored"))

        K, Q, GA = v["K"], v["Q"], v["GA"]
        last_sum, last_ready, last_stored, tile_stored = map(sem, ("last_sum", "last_ready", "last_stored", "tile_stored"))

        block = ctx.enter_context(nc.Block())

        def tok(b):
            return bass.ds(b * T, T)

        def first(b):
            return isinstance(b, int) and b == 0

        def blocks(eng, iteration):
            iteration(0, 0, False, True)
            iteration(1, 1, True, True)
            iteration(2, 0, True, True)
            with eng.Fori(3, NB - 2, 2) as b:
                iteration(b, 1, True, True)
                iteration(b + 1, 0, True, True)
            iteration(NB - 1, 1, True, False)

        ADD_X, MEAN, CENTRE, SQUARE_N, ADD_N, VARIANCE = 1, 8, 9, 13, 15, 21
        COPY_Y, SQUARE_Y, ADD_Y, Y_MEAN = 2 * DT, 9, 10, 17
        ROOTS = 21
        INVERT_N, SCALE_N, HIGH_N, LOW_N = 22, 26, 28, 30
        INVERT_Y, NORM_Y, RESULT = 34, 38, 40

        POOL_STEPS = (1, 2, *range(5, I_T))

        def now(place, start, step=1):
            n = (place - start) // step
            return (place - start) % step == 0 and 0 <= n < DT, n

        def slot_free(eng, done, b, j):
            if j < 2:
                if not first(b):
                    eng.wait_ge(done, I_T * b - 2 + j)
            elif j == I_T - 1:
                if not first(b):
                    eng.wait_ge(done, I_T * b)
            else:
                eng.wait_ge(done, I_T * b + j - 1)

        @block.sync
        def _(sp):
            sp.dma_start(N[:], x1_t[:, :, tok(1)]).then_inc(n_loaded, 16)
            sp.dma_start(down_hi[:], v["down_hi_dram"]).then_inc(down_loaded, 16)
            sp.dma_start(down_lo[:], v["down_lo_dram"]).then_inc(down_loaded, 16)

            def load_n(b):
                sp.wait_ge(H_low, DT * (b - 1))
                sp.dma_start(N[:], x1_t[:, :, tok(b)]).then_inc(n_loaded, 16)

            def load_res(b):
                if not first(b):
                    sp.wait_ge(out_stored, 16 * b)
                sp.dma_start(X[:], x1_t[:, :, tok(b)]).then_inc(res_loaded, 16)

            def store(b):
                sp.wait_ge(out_ready, DT * (b + 1))
                sp.dma_start(outT_t[:, :, tok(b)], X[:]).then_inc(out_stored, 16)

            load_n(2)
            sp.wait_ge(last_ready, DT)
            sp.dma_start(x1_t[:, :, tok(NB - 1)], K[:]).then_inc(last_stored, 16)
            load_res(0)
            load_n(3)
            store(0)
            sp.wait_ge(last_stored, 16)
            with sp.Fori(1, NB - 3) as b:
                load_res(b)
                load_n(b + 3)
                store(b)
            for b in range(NB - 3, NB - 1):
                load_res(b)
                store(b)
            load_res(NB - 1)
            for c in range(DT):
                sp.wait_ge(out_ready, DT * (NB - 1) + c + 1)
                sp.dma_start(outT_t[:, c, tok(NB - 1)], X[:, c, :]).then_inc(tile_stored, 16)
            sp.wait_ge(tile_stored, 16 * DT)
            sp.wait_ge(out_stored, 16 * (NB - 1))
            sp.wait_ge(last_stored, 16)

        @block.tensor
        def _(pe):
            def bank_free(means, variances, ys):
                for s, n in ((centred, means * DT), (var_root, variances), (y_kept, ys)):
                    if not (isinstance(n, int) and n <= 0):
                        pe.wait_ge(s, n)

            def sums_left(b):
                pe.wait_ge(by_dve, DT * (I_T * b + R_STEPS.start))
                pe.wait_ge(by_act, DT * (I_T * b + R_STEPS.start))

            def mean(b):
                pe.wait_ge(x_sum, NSUM * b)
                nc.tensor.matmul(R[:], ones[:], RS[:], start=True, stop=True).then_inc(mean_red, 1)

            def variance(b):
                pe.wait_ge(sq_sum, NSUM * b)
                nc.tensor.matmul(R[:], ones[:], RS[:], start=True, stop=True).then_inc(var_red, 1)

            def y_square(b):
                pe.wait_ge(y_sum, NSUM * (b + 1))
                nc.tensor.matmul(R[:], ones[:], RSY[:], start=True, stop=True).then_inc(y_red, 1)

            def down(b, j, c):
                if c == 0:
                    if j == 0 and first(b):
                        pe.wait_ge(down_loaded, 32)
                    pe.wait_ge(HH_high, I_T * b + j + 1)
                    pe.wait_ge(HH_low, I_T * b + j + 1)
                if j == 0 and first(b):
                    pe.wait_ge(last_sum, c + 1)
                elif j == 0:
                    pe.wait_ge(y_copied, DT * (b - 1) + c + 1)
                col = j * D + c * P
                for w, part in ((down_hi, 0), (down_lo, 0), (down_hi, 1)):
                    mm = nc.tensor.matmul(O[c][:], w[:, col:col + P], HH[:, slot(j), part, :],
                                          start=(j == 0 and w is down_hi and part == 0),
                                          stop=(j == I_T - 1 and part == 1))
                if c == DT - 1:
                    mm.then_inc(down_used, 1)

            def iteration(b, s, prev, nxt):
                if not first(b):
                    pe.wait_ge(H_high, DT * b)
                    pe.wait_ge(H_low, DT * b)
                for j in range(I_T):
                    for m in range(GROUPS):
                        place = DT * j + m // 2
                        if m % 2 == 0 and nxt and place == MEAN:
                            sums_left(b)
                            bank_free(b, b, b - 1)
                            mean(b + 1)
                        if m % 2 == 0 and nxt and place == VARIANCE:
                            bank_free(b + 1, b, b if prev else 0)
                            variance(b + 1)
                        if m % 2 == 0 and prev and place == Y_MEAN:
                            sums_left(b)
                            bank_free(b + 1 if nxt else b, b, b - 1)
                            y_square(b - 1)
                        last = before(j, m)
                        if last is None:
                            n = b + 1 if nxt else b
                            bank_free(n, n, b if prev else 0)
                        elif not (j == 0 and last[0] and first(b)):
                            back, k = last
                            pe.wait_ge((by_act, by_dve)[k % 2], DT * (I_T * b + j - back) + k // 2 + 1)
                        which, g = m // DT, m % DT
                        col = (g * 2 * I_T + which * I_T + j) * P
                        for part in range(2):
                            mm = nc.tensor.matmul(EV[ev_bank(j, m)][:], values[:, col:col + P], H[s][:, part, g, :],
                                                  start=part == 0, stop=part == 1)
                        mm.then_inc(group_done, 1)
                        if m % 2:
                            if j >= 2:
                                down(b, j - 2, m // 2)
                            elif prev:
                                down(b - 1, I_T - 2 + j, m // 2)

            blocks(pe, iteration)
            for j in (I_T - 2, I_T - 1):
                for c in range(DT):
                    down(NB - 1, j, c)
            bank_free(NB - 1, NB - 1, NB - 1)
            pe.wait_ge(by_dve, DT * I_T * NB)
            pe.wait_ge(by_act, DT * I_T * NB)
            for c in range(DT):
                pe.wait_ge(y_squared, DT * (NB - 1) + c + 1)
                mm = nc.tensor.matmul(R[:], ones[:], SQY[:, c, :], start=c == 0, stop=c == DT - 1)
            mm.then_inc(y_red, 1)

        @block.scalar
        def _(act):
            def square(k, c, ring, src, ready, done, sums):
                act.wait_ge(ready, DT * k + c + 1)
                if c == 0 and not first(k):
                    act.wait_ge(sums, NSUM * k)
                nc.scalar.activation(ring[:, c, :], src[:, c, :], ACT.Square).then_inc(done, 1)

            def square_n(b, c):
                square(b - 1, c, SQ, N, centred, squared, sq_sum)

            def square_y(b, c):
                square(b, c, SQY, Y, y_copied, y_squared, y_sum)

            def copy_y(b, c):
                act.wait_ge(down_used, I_T * (b + 1))
                if not first(b):
                    act.wait_ge(out_ready, DT * b)
                nc.scalar.activation(Y[:, c, :], O[c][:], ACT.Copy).then_inc(y_copied, 1)

            def var_sqrt(b):
                act.wait_ge(var_red, b)
                if not first(b - 1):
                    act.wait_ge(scaled, DT * (b - 1))
                nc.scalar.activation(RV[:], R[:], ACT.Sqrt, bias=eps[:, 0:1]).then_inc(var_root, 1)

            def keep_y(b):
                act.wait_ge(y_red, b + 1)
                if not first(b):
                    act.wait_ge(y_norm, DT * b)
                nc.scalar.activation(RY[:], R[:], ACT.Copy).then_inc(y_kept, 1)

            def y_sqrt(b):
                act.wait_ge(y_kept, b + 1)
                nc.scalar.activation(RY[:], RY[:], ACT.Sqrt, bias=eps[:, 2:3]).then_inc(y_root, 1)

            def split(b, s, c):
                if not first(b - 1):
                    act.wait_ge(group_done, GROUPS * I_T * (b - 1))
                act.wait_ge(scaled, DT * (b - 1) + c + 1)
                nc.scalar.activation(H[s][:, 0, c, :], N[:, c, :], ACT.Identity,
                                     bias=mod[:, SB][:, c:c + 1]).then_inc(H_high, 1)

            def take(b, j, m):
                which, g = m // DT, m % DT
                act.wait_ge(group_done, GROUPS * (I_T * b + j) + m + 1)
                if m == 0:
                    slot_free(act, HH_low, b, j)
                t = which * I_T + j
                nc.scalar.activation(A[:, slot(j), 2 * which + g // 2, :], EV[ev_bank(j, m)][:], ACT.Copy,
                                     scale=gu_s[:, t, g:g + 1]).then_inc(by_act, 1)

            def high(b, j):
                act.wait_ge(hid_ready, I_T * b + j + 1)
                slot_free(act, down_used, b, j)
                nc.scalar.activation(HH[:, slot(j), 0, :], A[:, slot(j), 0, :], ACT.Copy).then_inc(HH_high, 1)

            def silu(b, j):
                act.wait_ge(halves, 2 * (I_T * b + j) + 1)
                nc.scalar.activation(A[:, slot(j), 0, :], A[:, slot(j), 0, :], ACT.Silu).then_inc(gate_silu, 1)

            def beside(b, s, place, prev, nxt):
                for there, n, start, work in ((prev, b - 1, COPY_Y, copy_y), (nxt, b + 1, SQUARE_N, square_n),
                                              (prev, b - 1, SQUARE_Y, square_y)):
                    due, c = now(place, start)
                    if there and due:
                        work(n, c)
                due, c = now(place, HIGH_N)
                if nxt and due:
                    split(b + 1, 1 - s, c)
                if prev and place == Y_MEAN:
                    keep_y(b - 1)
                if prev and place == ROOTS:
                    y_sqrt(b - 1)
                if nxt and place == ROOTS:
                    var_sqrt(b + 1)

            def iteration(b, s, prev, nxt):
                for j in range(I_T):
                    for m in range(0, GROUPS, 2):
                        beside(b, s, DT * j + m // 2, prev, nxt)
                        if m == GROUPS - 2:
                            if j:
                                high(b, j - 1)
                            elif prev:
                                high(b - 1, I_T - 1)
                        take(b, j, m)
                    silu(b, j)

            blocks(act, iteration)
            high(NB - 1, I_T - 1)
            act.wait_ge(down_used, I_T * NB)
            act.wait_ge(y_sum, NSUM * (NB - 1))
            for c in range(DT):
                nc.scalar.activation(SQY[:, c, :], O[c][:], ACT.Square).then_inc(y_squared, 1)
            act.wait_ge(y_red, NB)
            act.wait_ge(y_norm, DT * (NB - 1))
            nc.scalar.activation(RY[:], R[:], ACT.Sqrt, bias=eps[:, 2:3]).then_inc(y_root, 1)

        @block.gpsimd
        def _(pool):
            def add(k, n, tiles, rs, done, sums, reduced, reductions):
                pool.wait_ge(done, DT * k + n + 2)
                if n == 0 and not (isinstance(reductions, int) and reductions == 0):
                    pool.wait_ge(reduced, reductions)
                if n:
                    pool.wait_ge(sums, NSUM * k + n)
                nc.gpsimd.tensor_tensor(rs[:], rs[:] if n else tiles[:, 0, :], tiles[:, n + 1, :], ALU.add).then_inc(sums, 1)

            def add_x(b, n):
                if n == 0:
                    pool.wait_ge(n_loaded, 16 * b)
                    if not first(b - 1):
                        pool.wait_ge(var_red, b - 1)
                else:
                    pool.wait_ge(x_sum, NSUM * (b - 1) + n)
                nc.gpsimd.tensor_tensor(RS[:], RS[:] if n else N[:, 0, :], N[:, n + 1, :], ALU.add).then_inc(x_sum, 1)

            def add_n(b, n):
                add(b - 1, n, SQ, RS, squared, sq_sum, mean_red, b)

            def add_y(b, n):
                add(b, n, SQY, RSY, y_squared, y_sum, y_red, b)

            def half(b, j, which):
                pool.wait_ge(by_dve, DT * (I_T * b + j) + 2 * which + 2)
                a = A[:, slot(j), 2 * which, :]
                nc.gpsimd.tensor_tensor(a, a, A[:, slot(j), 2 * which + 1, :], ALU.add).then_inc(halves, 1)

            def hidden(b, j):
                pool.wait_ge(gate_silu, I_T * b + j + 1)
                pool.wait_ge(halves, 2 * (I_T * b + j) + 2)
                a = A[:, slot(j), 0, :]
                nc.gpsimd.tensor_tensor(a, a, A[:, slot(j), 2, :], ALU.mult).then_inc(hid_ready, 1)

            def low(b, j):
                pool.wait_ge(HH_high, I_T * b + j + 1)
                nc.gpsimd.tensor_tensor(HH[:, slot(j), 1, :], A[:, slot(j), 0, :], HH[:, slot(j), 0, :],
                                        ALU.subtract).then_inc(HH_low, 1)

            def beside(b, place, prev, nxt):
                for there, n, start, work in ((nxt, b + 1, ADD_X, add_x), (nxt, b + 1, ADD_N, add_n),
                                              (prev, b - 1, ADD_Y, add_y)):
                    due, c = now(place, start, 2)
                    if there and due and c < NSUM:
                        work(n, c)

            def iteration(b, s, prev, nxt):
                for j in range(I_T):
                    if j in POOL_STEPS:
                        hidden(b, j - 1)
                    for i in range(DT):
                        if i == DT - 2:
                            half(b, j, 0)
                        if i == DT - 1:
                            if j:
                                low(b, j - 1)
                            elif prev:
                                low(b - 1, I_T - 1)
                        beside(b, DT * j + i, prev, nxt)
                    half(b, j, 1)

            blocks(pool, iteration)
            low(NB - 1, I_T - 1)

        @block.vector
        def _(dve):
            def centre(b, c):
                dve.wait_ge(mean_red, b)
                nc.vector.tensor_tensor(N[:, c, :], N[:, c, :], R[:], ALU.subtract).then_inc(centred, 1)

            def inverse(k, c, buf, root, recip):
                dve.wait_ge(root, k + 1)
                part = buf[:, c * T // DT:(c + 1) * T // DT]
                nc.vector.reciprocal(part, part).then_inc(recip, 1)

            def invert_n(b, c):
                inverse(b - 1, c, RV, var_root, var_recip)

            def invert_y(b, c):
                inverse(b, c, RY, y_root, y_recip)

            def scale_n(b, c):
                dve.wait_ge(var_recip, DT * b)
                dve.wait_ge(squared, DT * b)
                nc.vector.scalar_tensor_tensor(N[:, c, :], N[:, c, :], mod[:, CB][:, c:c + 1], RV[:],
                                               ALU.mult, ALU.mult).then_inc(scaled, 1)

            def low_n(b, s, c):
                dve.wait_ge(H_high, DT * (b - 1) + c + 1)
                nc.vector.scalar_tensor_tensor(H[s][:, 1, c, :], N[:, c, :], mod[:, SB][:, c:c + 1], H[s][:, 0, c, :],
                                               ALU.add, ALU.subtract).then_inc(H_low, 1)

            def norm_y(b, c, y=None):
                dve.wait_ge(y_recip, DT * (b + 1))
                dve.wait_ge(y_squared, DT * (b + 1))
                nc.vector.scalar_tensor_tensor(Y[:, c, :], Y[:, c, :] if y is None else y, mod[:, GB][:, c:c + 1], RY[:],
                                               ALU.mult, ALU.mult).then_inc(y_norm, 1)

            def mixer_sum(c):
                nc.vector.tensor_tensor(Q[:, c, :], Q[:, c, :], O[c][:], ALU.add).then_inc(last_sum, 1)

            def mixer_result(c):
                dve.wait_ge(last_sum, c + 1)
                nc.vector.scalar_tensor_tensor(K[:, c, :], Q[:, c, :], mod[:, GA][:, c:c + 1], K[:, c, :],
                                               ALU.mult, ALU.add).then_inc(last_ready, 1)

            def result(b, c):
                dve.wait_ge(res_loaded, 16 * (b + 1))
                dve.wait_ge(y_norm, DT * b + c + 1)
                nc.vector.tensor_tensor(X[:, c, :], X[:, c, :], Y[:, c, :], ALU.add).then_inc(out_ready, 1)

            def take(b, j, m):
                which, g = m // DT, m % DT
                dve.wait_ge(group_done, GROUPS * (I_T * b + j) + m + 1)
                dve.wait_ge(by_act, DT * (I_T * b + j) + m // 2 + 1)
                a = A[:, slot(j), 2 * which + g // 2, :]
                nc.vector.scalar_tensor_tensor(a, EV[ev_bank(j, m)][:], gu_s[:, which * I_T + j, g:g + 1], a,
                                               ALU.mult, ALU.add).then_inc(by_dve, 1)

            def hidden(b, j):
                dve.wait_ge(gate_silu, I_T * b + j + 1)
                dve.wait_ge(halves, 2 * (I_T * b + j) + 2)
                a = A[:, slot(j), 0, :]
                nc.vector.tensor_tensor(a, a, A[:, slot(j), 2, :], ALU.mult).then_inc(hid_ready, 1)

            def beside(b, s, place, prev, nxt):
                for there, n, start, work in ((nxt, b + 1, CENTRE, centre), (nxt, b + 1, INVERT_N, invert_n),
                                              (nxt, b + 1, SCALE_N, scale_n), (prev, b - 1, INVERT_Y, invert_y),
                                              (prev, b - 1, NORM_Y, norm_y), (prev, b - 1, RESULT, result)):
                    due, c = now(place, start)
                    if there and due:
                        work(n, c)
                if first(b) and place < 2 * DT:
                    (mixer_sum if place < DT else mixer_result)(place % DT)
                due, c = now(place, LOW_N)
                if nxt and due:
                    low_n(b + 1, 1 - s, c)

            def iteration(b, s, prev, nxt):
                for j in range(I_T):
                    for m in range(1, GROUPS, 2):
                        beside(b, s, DT * j + m // 2, prev, nxt)
                        take(b, j, m)
                        if m == 3:
                            if j and j not in POOL_STEPS:
                                hidden(b, j - 1)
                            elif j == 0 and prev:
                                hidden(b - 1, I_T - 1)

            blocks(dve, iteration)
            hidden(NB - 1, I_T - 1)
            for c in range(DT):
                invert_y(NB - 1, c)
            dve.wait_ge(out_ready, DT * (NB - 1))
            norm_y(NB - 1, 0, O[0][:])
            for c in range(1, DT):
                norm_y(NB - 1, c, O[c][:])
                result(NB - 1, c - 1)
            result(NB - 1, DT - 1)


def kernel(L0_attn_x, L0_attn_w_qkv, L0_attn_w_swiglu, L0_attn_w_out, L0_ffn_gate_up_packed,
           L0_ffn_gate_up_scales, L0_ffn_down_packed, L0_ffn_down_scales, L0_c, L0_wmod):
    import numpy as np
    import concourse.bacc as bacc
    from concourse.bass_utils import run_bass_kernel_spmd

    def groups(words):
        out, n = words.shape
        return np.repeat(words.T.reshape(n // 16, 16, out).transpose(1, 0, 2).reshape(16, -1), 8, axis=0)

    gus, dns = np.asarray(L0_ffn_gate_up_scales), np.asarray(L0_ffn_down_scales)
    arrays = {
        "xT": np.asarray(L0_attn_x)[0].T,
        "wqkvT": np.asarray(L0_attn_w_qkv).T,
        "wswT": np.asarray(L0_attn_w_swiglu).T,
        "woutT": np.asarray(L0_attn_w_out).T,
        "packed": np.concatenate([groups(np.asarray(L0_ffn_gate_up_packed)), groups(np.asarray(L0_ffn_down_packed))], axis=1),
        "gu_scales": gus.reshape(gus.shape[0], -1, P).transpose(2, 1, 0),
        "down_scales": dns.reshape(1, -1),
        "c_row": np.asarray(L0_c),
        "wmodT": np.asarray(L0_wmod).T.reshape(-1, P, L0_wmod.shape[0]).transpose(1, 0, 2),
    }
    arrays = {name: np.ascontiguousarray(a) for name, a in arrays.items()}
    nc = bacc.Bacc("TRN2", target_bir_lowering=False, num_devices=1)
    args = [nc.dram_tensor(name, a.shape, mybir.dt.from_np(a.dtype), kind="ExternalInput").ap() for name, a in arrays.items()]
    D, S = arrays["xT"].shape
    outT = nc.dram_tensor("outT", (D, S), F32, kind="ExternalOutput").ap()
    program(nc, *args, outT)
    r = run_bass_kernel_spmd(nc, [arrays], core_ids=[0])
    return np.ascontiguousarray(r.results[0]["outT"].T)[None]
```
